# Optimizing a Trainium2 kernel written in Bass

```python
import numpy as np
import jax
import jax.numpy as jnp

def _softmax(x, axis=-1):
    return jax.nn.softmax(x, axis=axis)

def _gelu(x):
    return jax.nn.gelu(x, approximate=True)

def _silu(x):
    return jax.nn.silu(x)

def _sigmoid(x):
    return jax.nn.sigmoid(x)

def _layernorm(x, axis=-1, eps=1e-05):
    m = jnp.mean(x, axis=axis, keepdims=True)
    v = jnp.var(x, axis=axis, keepdims=True)
    return (x - m) / jnp.sqrt(v + eps)

def _scatter_add(tgt, idx, src, axis=0):
    return tgt.at[idx].add(src)

def _segment_sum(src, seg, n):
    return jax.ops.segment_sum(src, seg, n)
kernel_name = 'mk_flamingo_gated_d2_seqx_r4_ef8174'

def setup_inputs(seed: int=0):
    np.random.seed(seed)
    _w = jnp.asarray

    def _rec_inputs():
        import jax
        import jax.numpy as jnp
        _rk = jax.random.key(seed)
        x = -0.0002928 + 1 * jax.random.normal(jax.random.fold_in(_rk, 1), (16, 112, 256), jnp.float32)
        _lenS = 112 - jax.random.randint(jax.random.fold_in(_rk, 7), (16,), 0, max(1, 112 // 4) + 1, jnp.int32)
        _lenS2 = 375 - jax.random.randint(jax.random.fold_in(_rk, 8), (16,), 0, max(1, 375 // 4) + 1, jnp.int32)
        _ctx_1024P = jax.random.normal(jax.random.fold_in(_rk, 11), (16, 16, 256), jnp.float32)
        _ctx_1024c = jax.random.dirichlet(jax.random.fold_in(_rk, 511), 0.3 * jnp.ones((16,), jnp.float32), (16, 375))
        _ctx_1024t = jnp.einsum('bsk,bkd->bsd', _ctx_1024c, _ctx_1024P)
        _ctx_1024t = _ctx_1024t * jax.lax.rsqrt(jnp.mean(jnp.square(_ctx_1024t)) + 1e-12) * 0.953939
        ctx_1024 = 4.13588e-05 + 0.999923 * (_ctx_1024t + 0.3 * jax.random.normal(jax.random.fold_in(_rk, 611), (16, 375, 256), jnp.float32))
        _g = jax.random.normal(jax.random.fold_in(_rk, 9001), (2, 2), jnp.float32)
        _g = jnp.sign(_g) * jnp.maximum(jnp.abs(_g), 1.0) + (_g == 0) * 1.0
        g_xattn = _g[0]
        g_ffn = _g[1]
        return (x, ctx_1024, g_xattn, g_ffn)
    x, ctx_1024, g_xattn, g_ffn = _rec_inputs()

    def _L0_xattn_setup():
        import jax, jax.numpy as jnp
        import numpy as np
        DIM = 256
        NUM_HEADS = 16
        DIM_HEAD = 64
        INNER = NUM_HEADS * DIM_HEAD
        SCALE = DIM_HEAD ** (-0.5)

        def _layernorm(x, gamma, beta, eps=1e-05):
            mu = jnp.mean(x, axis=-1, keepdims=True)
            var = jnp.mean(jnp.square(x - mu), axis=-1, keepdims=True)
            return (x - mu) * jax.lax.rsqrt(var + eps) * gamma + beta
        key = jax.random.key(seed)
        ks = jax.random.split(key, 8)
        B, SQ, SK = (2, 512, 1024)
        x = jax.random.normal(ks[0], (B, SQ, DIM), dtype=jnp.float32)
        context = jax.random.normal(ks[1], (B, SK, DIM), dtype=jnp.float32)
        ln_gamma = jnp.ones((DIM,), jnp.float32)
        ln_beta = jnp.zeros((DIM,), jnp.float32)
        w_q = jax.random.normal(ks[2], (DIM, INNER), dtype=jnp.float32) / np.sqrt(DIM)
        w_kv = jax.random.normal(ks[3], (DIM, 2 * INNER), dtype=jnp.float32) / np.sqrt(DIM)
        w_out = jax.random.normal(ks[4], (INNER, DIM), dtype=jnp.float32) / np.sqrt(INNER)
        b_out = jnp.zeros((DIM,), jnp.float32)
        gate = jnp.array([0.5], jnp.float32)
        return {'x': x, 'context': context, 'ln_gamma': ln_gamma, 'ln_beta': ln_beta, 'w_q': w_q, 'w_kv': w_kv, 'w_out': w_out, 'b_out': b_out, 'gate': gate}
    _L0_xattn_all = _L0_xattn_setup()
    _L0_xattn_in = {k: v for k, v in _L0_xattn_all.items() if k in ('ln_gamma', 'ln_beta', 'w_q', 'w_kv', 'w_out', 'b_out', 'gate')}
    del _L0_xattn_all

    def _L0_ffn_setup():
        import jax, jax.numpy as jnp
        import numpy as np
        B, N, D = (4, 512, 256)
        SPARSITY = 0.01
        key = jax.random.key(seed)
        k1, k2, k3 = jax.random.split(key, 3)
        x = jax.random.normal(k1, (B, N, D), dtype=jnp.float32)
        spatial = jax.random.normal(k2, (D, D), dtype=jnp.float32) * 0.02
        freq = jnp.fft.fft(spatial, axis=-1)
        k = int(D * SPARSITY)
        mag = jnp.abs(freq)
        kth = jax.lax.top_k(mag, k)[0][:, -1:]
        w_sparse = jnp.where(mag >= kth, freq, 0.0 + 0j)
        bias = jax.random.normal(k3, (D,), dtype=jnp.float32) * 0.01
        return {'x': x, 'w_freq_real': jnp.real(w_sparse).astype(jnp.float32), 'w_freq_imag': jnp.imag(w_sparse).astype(jnp.float32), 'bias': bias}
    _L0_ffn_all = _L0_ffn_setup()
    _L0_ffn_in = {k: v for k, v in _L0_ffn_all.items() if k in ('w_freq_real', 'w_freq_imag', 'bias')}
    del _L0_ffn_all

    def _L1_xattn_setup():
        import jax, jax.numpy as jnp
        import numpy as np
        B, S, D_IN, D_MODEL = (4, 512, 256, 256)
        key = jax.random.key(seed)
        ks = jax.random.split(key, 9)
        return {'q': jax.random.normal(ks[0], (B, S, D_IN), jnp.float32), 'k': jax.random.normal(ks[1], (B, S, D_IN), jnp.float32), 'v': jax.random.normal(ks[2], (B, S, D_IN), jnp.float32), 'Wq': jax.random.normal(ks[3], (D_IN, D_MODEL), jnp.float32) * 0.02, 'bq': jax.random.normal(ks[4], (D_MODEL,), jnp.float32) * 0.02, 'Wk': jax.random.normal(ks[5], (D_IN, D_MODEL), jnp.float32) * 0.02, 'bk': jax.random.normal(ks[6], (D_MODEL,), jnp.float32) * 0.02, 'Wv': jax.random.normal(ks[7], (D_IN, D_MODEL), jnp.float32) * 0.02, 'bv': jax.random.normal(ks[8], (D_MODEL,), jnp.float32) * 0.02}
    _L1_xattn_all = _L1_xattn_setup()
    _L1_xattn_in = {k: v for k, v in _L1_xattn_all.items() if k in ('Wq', 'bq', 'Wk', 'bk', 'Wv', 'bv')}
    del _L1_xattn_all

    def _L1_ffn_setup():
        import jax, jax.numpy as jnp
        import numpy as np
        ALPHA = 1.702
        LIMIT = 7.0
        EPS = 1e-05
        E = 16
        K = 4

        def _swiglu(h):
            x_glu = jnp.minimum(h[..., ::2], LIMIT)
            x_lin = jnp.clip(h[..., 1::2], LIMIT, LIMIT)
            return x_glu * jax.nn.sigmoid(ALPHA * x_glu) * (x_lin + 1.0)
        key = jax.random.key(seed)
        ks = jax.random.split(key, 7)
        B, T, H, I = (1, 512, 256, 256)
        x = jax.random.normal(ks[0], (B, T, H), jnp.float32)
        scale = jnp.ones((H,), jnp.float32)
        gate_w = jax.random.normal(ks[1], (E, H), jnp.float32) * 0.02
        gate_b = jnp.zeros((E,), jnp.float32)
        mlp1_w = jax.random.normal(ks[2], (E, 2 * I, H), jnp.float32) * 0.02
        mlp1_b = jax.random.normal(ks[3], (E, 2 * I), jnp.float32) * 0.02
        mlp2_w = jax.random.normal(ks[4], (E, H, I), jnp.float32) * 0.02
        mlp2_b = jax.random.normal(ks[5], (E, H), jnp.float32) * 0.02
        return dict(x=x, scale=scale, gate_w=gate_w, gate_b=gate_b, mlp1_w=mlp1_w, mlp1_b=mlp1_b, mlp2_w=mlp2_w, mlp2_b=mlp2_b)
    _L1_ffn_all = _L1_ffn_setup()
    _L1_ffn_in = {k: v for k, v in _L1_ffn_all.items() if k in ('scale', 'gate_w', 'gate_b', 'mlp1_w', 'mlp1_b', 'mlp2_w', 'mlp2_b')}
    del _L1_ffn_all
    return {'x': x, 'ctx_1024': ctx_1024, 'g_xattn': g_xattn, 'g_ffn': g_ffn, 'L0_xattn_ln_gamma': _L0_xattn_in['ln_gamma'], 'L0_xattn_ln_beta': _L0_xattn_in['ln_beta'], 'L0_xattn_w_q': _L0_xattn_in['w_q'], 'L0_xattn_w_kv': _L0_xattn_in['w_kv'], 'L0_xattn_w_out': _L0_xattn_in['w_out'], 'L0_xattn_b_out': _L0_xattn_in['b_out'], 'L0_xattn_gate': _L0_xattn_in['gate'], 'L0_ffn_w_freq_real': _L0_ffn_in['w_freq_real'], 'L0_ffn_w_freq_imag': _L0_ffn_in['w_freq_imag'], 'L0_ffn_bias': _L0_ffn_in['bias'], 'L1_xattn_Wq': _L1_xattn_in['Wq'], 'L1_xattn_bq': _L1_xattn_in['bq'], 'L1_xattn_Wk': _L1_xattn_in['Wk'], 'L1_xattn_bk': _L1_xattn_in['bk'], 'L1_xattn_Wv': _L1_xattn_in['Wv'], 'L1_xattn_bv': _L1_xattn_in['bv'], 'L1_ffn_scale': _L1_ffn_in['scale'], 'L1_ffn_gate_w': _L1_ffn_in['gate_w'], 'L1_ffn_gate_b': _L1_ffn_in['gate_b'], 'L1_ffn_mlp1_w': _L1_ffn_in['mlp1_w'], 'L1_ffn_mlp1_b': _L1_ffn_in['mlp1_b'], 'L1_ffn_mlp2_w': _L1_ffn_in['mlp2_w'], 'L1_ffn_mlp2_b': _L1_ffn_in['mlp2_b']}

def reference(x, ctx_1024, g_xattn, g_ffn, L0_xattn_ln_gamma, L0_xattn_ln_beta, L0_xattn_w_q, L0_xattn_w_kv, L0_xattn_w_out, L0_xattn_b_out, L0_xattn_gate, L0_ffn_w_freq_real, L0_ffn_w_freq_imag, L0_ffn_bias, L1_xattn_Wq, L1_xattn_bq, L1_xattn_Wk, L1_xattn_bk, L1_xattn_Wv, L1_xattn_bv, L1_ffn_scale, L1_ffn_gate_w, L1_ffn_gate_b, L1_ffn_mlp1_w, L1_ffn_mlp1_b, L1_ffn_mlp2_w, L1_ffn_mlp2_b):
    import jax
    import jax.numpy as jnp

    def _L0_xattn_ref(x, context, ln_gamma, ln_beta, w_q, w_kv, w_out, b_out, gate):
        import jax, jax.numpy as jnp
        import numpy as np
        DIM = 256
        NUM_HEADS = 16
        DIM_HEAD = 64
        INNER = NUM_HEADS * DIM_HEAD
        SCALE = DIM_HEAD ** (-0.5)

        def _layernorm(x, gamma, beta, eps=1e-05):
            mu = jnp.mean(x, axis=-1, keepdims=True)
            var = jnp.mean(jnp.square(x - mu), axis=-1, keepdims=True)
            return (x - mu) * jax.lax.rsqrt(var + eps) * gamma + beta
        B, SQ, _ = x.shape
        SK = context.shape[1]
        xn = _layernorm(x, ln_gamma, ln_beta)
        q = (xn @ w_q).reshape(B, SQ, NUM_HEADS, DIM_HEAD)
        kv = context @ w_kv
        k, v = jnp.split(kv, 2, axis=-1)
        k = k.reshape(B, SK, NUM_HEADS, DIM_HEAD)
        v = v.reshape(B, SK, NUM_HEADS, DIM_HEAD)
        scores = jnp.einsum('bqhd,bkhd->bhqk', q * SCALE, k)
        attn = jax.nn.softmax(scores, axis=-1)
        out = jnp.einsum('bhqk,bkhd->bqhd', attn, v).reshape(B, SQ, INNER)
        out = out @ w_out + b_out
        return out * jnp.tanh(gate[0])

    def _L0_ffn_ref(x, w_freq_real, w_freq_imag, bias):
        import jax, jax.numpy as jnp
        import numpy as np
        B, N, D = (4, 512, 256)
        SPARSITY = 0.01
        w = jax.lax.complex(w_freq_real, w_freq_imag)
        x_freq = jnp.fft.fft(x, axis=-1)
        y_freq = jnp.einsum('bnd,do->bno', x_freq, w)
        y = jnp.real(jnp.fft.ifft(y_freq, axis=-1))
        return y + bias

    def _L1_xattn_ref(q, k, v, Wq, bq, Wk, bk, Wv, bv):
        import jax, jax.numpy as jnp
        import numpy as np
        B, S, D_IN, D_MODEL = (4, 512, 256, 256)
        qp = jnp.einsum('bsd,de->bse', q, Wq) + bq
        kp = jnp.einsum('bsd,de->bse', k, Wk) + bk
        vp = jnp.einsum('bsd,de->bse', v, Wv) + bv
        scale = 1.0 / jnp.sqrt(jnp.asarray(kp.shape[-1], jnp.float32))
        logits = jnp.einsum('bqe,bke->bqk', qp, kp) * scale
        attn = jax.nn.softmax(logits, axis=-1)
        return jnp.einsum('bqk,bke->bqe', attn, vp)

    def _L1_ffn_ref(x, scale, gate_w, gate_b, mlp1_w, mlp1_b, mlp2_w, mlp2_b):
        import jax, jax.numpy as jnp
        import numpy as np
        ALPHA = 1.702
        LIMIT = 7.0
        EPS = 1e-05
        E = 16
        K = 4

        def _swiglu(h):
            x_glu = jnp.minimum(h[..., ::2], LIMIT)
            x_lin = jnp.clip(h[..., 1::2], LIMIT, LIMIT)
            return x_glu * jax.nn.sigmoid(ALPHA * x_glu) * (x_lin + 1.0)
        t = x * jax.lax.rsqrt(jnp.mean(x * x, axis=-1, keepdims=True) + EPS) * scale
        g = jnp.einsum('bth,eh->bte', t, gate_w) + gate_b
        vals, idx = jax.lax.top_k(g, K)
        w = jax.nn.softmax(vals, axis=-1)
        route = jnp.sum(jax.nn.one_hot(idx, E, dtype=t.dtype) * w[..., None], axis=-2)
        route_e = jnp.moveaxis(route, -1, 0)

        def step(acc, p):
            w1, b1, w2, b2, r = p
            h = jnp.einsum('bth,ih->bti', t, w1) + b1
            s = _swiglu(h)
            y = jnp.einsum('bti,hi->bth', s, w2) + b2
            return (acc + r[..., None] * y, None)
        acc, _ = jax.lax.scan(step, jnp.zeros_like(x), (mlp1_w, mlp1_b, mlp2_w, mlp2_b, route_e))
        return x + acc
    x = x + jnp.tanh(g_xattn[0]) * _L0_xattn_ref(_layernorm(x, axis=-1), ctx_1024, L0_xattn_ln_gamma, L0_xattn_ln_beta, L0_xattn_w_q, L0_xattn_w_kv, L0_xattn_w_out, L0_xattn_b_out, L0_xattn_gate)
    x = x + jnp.tanh(g_ffn[0]) * _L0_ffn_ref(_layernorm(x, axis=-1), L0_ffn_w_freq_real, L0_ffn_w_freq_imag, L0_ffn_bias)
    x = x + jnp.tanh(g_xattn[1]) * _L1_xattn_ref(_layernorm(x, axis=-1), ctx_1024, ctx_1024, L1_xattn_Wq, L1_xattn_bq, L1_xattn_Wk, L1_xattn_bk, L1_xattn_Wv, L1_xattn_bv)
    x = x + jnp.tanh(g_ffn[1]) * _L1_ffn_ref(_layernorm(x, axis=-1), L1_ffn_scale, L1_ffn_gate_w, L1_ffn_gate_b, L1_ffn_mlp1_w, L1_ffn_mlp1_b, L1_ffn_mlp2_w, L1_ffn_mlp2_b)
    return x

_drawn_inputs = setup_inputs


def setup_inputs(seed=0):
    import zlib

    import numpy as np

    out = dict(_drawn_inputs(seed))
    spreads = {'g_ffn': (-1.0, 0.2),
     'L0_xattn_ln_gamma': (1.0, 0.2),
     'L0_xattn_ln_beta': (0.0, 0.1),
     'L0_xattn_b_out': (0.0, 0.1),
     'L1_ffn_scale': (1.0, 0.2),
     'L1_ffn_gate_b': (0.0, 0.1)}
    factors = {'L1_xattn_bq': 25.011, 'L1_xattn_bk': 64.0, 'L1_ffn_mlp2_b': 2.745}
    for name, (base, spread) in spreads.items():
        noise = np.random.default_rng([zlib.crc32(name.encode()), seed]).standard_normal(out[name].shape)
        drawn = base * np.exp(spread * noise) if base else spread * noise
        out[name] = jnp.asarray(drawn.astype(out[name].dtype))
    for name, factor in factors.items():
        out[name] = (out[name] * factor).astype(out[name].dtype)
    return out
```

```python
from contextlib import ExitStack

import numpy as np
import concourse.bass as bass
from concourse import mybir

F32 = mybir.dt.float32
F32R = mybir.dt.float32r
ALU = mybir.AluOpType
ACT = mybir.ActivationFunctionType
AX = mybir.AxisListType

B, TQ, D = 16, 112, 256
SK = 375
KT = D // 128
NH, DH = 16, 64
NP = NH // 2
INNER = NH * DH
KEYT, NKEY = 125, 3
SKE = SK + 1
NE, TOPK = 16, 4
HID = 256
CB = 4
NC = B // CB
CT = CB * TQ
EPS = 1e-5
ALPHA, LIMIT = 1.702, 7.0


class Event:

    def __init__(self, handle, per, unit=1):
        self.handle, self.per, self.unit = handle, per, unit

    def wait(self, eng, step, k, shift=0):
        n = step.off + shift
        fixed = (self.per * n + k) * self.unit
        if step.reg is None:
            if fixed > 0:
                eng.wait_ge(self.handle, fixed)
        else:
            eng.wait_ge(self.handle, step.reg * (self.per * self.unit) + fixed)

    def done(self, ins):
        ins.then_inc(self.handle, self.unit)


class Step:

    def __init__(self, reg, off, par, heads=True, tail=True, load=True):
        self.reg, self.off, self.par = reg, off, par
        self.heads, self.tail, self.load = heads, tail, load

    def before(self):
        return Step(self.reg, self.off - 1, 1 - self.par)

    def after(self):
        return Step(self.reg, self.off + 1, 1 - self.par)

    def index(self):
        return self.off if self.reg is None else self.reg + self.off


def pipeline(eng, body, n):
    body(Step(None, 0, 0, tail=False))
    body(Step(None, 1, 1))
    with eng.Fori(2, n - 3, 2) as i:
        body(Step(i, 0, 0))
        body(Step(i, 1, 1))
    body(Step(None, n - 2, 0))
    body(Step(None, n - 1, 1, load=False))
    body(Step(None, n, 0, heads=False, load=False))


class Chain:

    def __init__(self, eng, event):
        self.eng, self.event, self.n = eng, event, 0

    def __call__(self, ins):
        self.event.done(ins)
        self.n += 1

    def wait(self, step):
        self.event.wait(self.eng, step, self.n)


def build(nc, x, ctx, g_xattn, g_ffn, ln_gamma, ln_beta, w_q, w_kv, w_out, b_out, gate, w_re, w_im,
          ffn_bias, Wq1, bq1, Wk1, bk1, Wv1, bv1, rms_scale, gate_w, gate_b, mlp1_w, mlp1_b, mlp2_w,
          mlp2_b, dft, out):
    top = ExitStack()
    with top:
        def sb(name, shape, dt=F32, scope=top):
            return scope.enter_context(nc.sbuf_tensor(name, shape, dt))

        def sem(name):
            return top.enter_context(nc.semaphore(name))

        def event(name, per, unit=1):
            return Event(sem(name), per, unit)

        ident = sb("ident", [128, 128])
        acc = sb("acc", [128, B, D])
        tT_hi = sb("tT_hi", [128, KT, B * TQ], F32R)
        tT_lo = sb("tT_lo", [128, KT, B * TQ], F32R)
        route = sb("route", [TQ, NE, B])

        psum = [top.enter_context(nc.psum_tensor(f"bank{i}", [128, 512], F32)) for i in range(8)]

        phase1(nc, sb, event, sem, psum, ident, acc, tT_hi, tT_lo, route, x, ctx, g_xattn, g_ffn,
               ln_gamma, ln_beta, w_q, w_kv, w_out, b_out, gate, w_re, w_im, ffn_bias, Wq1, bq1, Wk1,
               bk1, Wv1, bv1, rms_scale, gate_w, gate_b, mlp2_b, dft)
        phase2(nc, sb, event, sem, psum, ident, acc, tT_hi, tT_lo, route, mlp1_w, mlp1_b, mlp2_w, out)


def phase1(nc, sb, event, sem, psum, ident, acc, tT_hi, tT_lo, route, x, ctx, g_xattn, g_ffn,
           ln_gamma, ln_beta, w_q, w_kv, w_out, b_out, gate, w_re, w_im, ffn_bias, Wq1, bq1, Wk1,
           bk1, Wv1, bv1, rms_scale, gate_w, gate_b, mlp2_b, dft):
    scope = ExitStack()
    with scope:
        def t(name, shape, dt=F32):
            return sb(name, shape, dt, scope)

        wq = t("wq", [128, KT, INNER])
        wkv_hi = t("wkv_hi", [128, KT, 2 * INNER], F32R)
        wkv_lo = t("wkv_lo", [128, KT, 2 * INNER], F32R)
        wo = t("wo", [128, NP, D])
        wq1 = t("wq1", [128, KT, D])
        wk1T = t("wk1T", [128, KT, D])
        wv1 = t("wv1", [128, KT, D])
        fmix = t("fmix", [128, KT, D])
        gwT = t("gwT", [128, KT, NE])
        b2 = t("b2", [NE, D])
        cols = t("cols", [128, 5, KT])
        GAMMA, BETA, BQ, BK, RMS = range(5)
        rows = t("rows", [128, 3, D])
        gbrow = t("gbrow", [128, NE])
        gates = t("gates", [128, 5])
        gt = t("gt", [128, 6])
        consts = t("consts", [128, 3])
        carrier = t("carrier", [1, 1])
        earlier = t("earlier", [TQ, NE, NE])

        x_in = t("x_in", [TQ, 2, D])
        ctx_in = t("ctx_in", [128, 2, NKEY, D])
        ctxT_hi = t("ctxT_hi", [128, 2, KT, SKE], F32R)
        ctxT_lo = t("ctxT_lo", [128, 2, KT, SKE], F32R)
        n0 = t("n0", [TQ, D])
        xn = t("xn", [TQ, D])
        xnT = t("xnT", [128, KT, TQ])
        q_hi = t("q_hi", [128, NP, 2, TQ], F32R)
        q_lo = t("q_lo", [128, NP, 2, TQ], F32R)
        k_hi = t("k_hi", [128, NP, SKE], F32R)
        k_lo = t("k_lo", [128, NP, SKE], F32R)
        v = t("v", [128, NKEY, INNER])
        prob = t("prob", [128, 2, SK])
        probT = t("probT", [KEYT, 2, NKEY, TQ])
        negmax = t("negmax", [TQ, NH])
        rowsum = t("rowsum", [TQ, NH])
        rinv = t("rinv", [TQ, NH])
        oT = t("oT", [128, NP, TQ])
        ln_h = t("ln_h", [TQ, 24])
        ln_t = t("ln_t", [TQ, 24])
        xb0 = t("xb0", [TQ, 2, D])
        x1 = x2 = x3 = t("x123", [TQ, D])
        xb1 = xb2 = t("xb12", [TQ, D])
        n1 = n2 = tn = t("n12t", [TQ, D])
        n3 = t("n3", [TQ, D])
        xm = t("xm", [TQ, D])
        nT = t("nT", [128, KT, TQ])
        q1T = t("q1T", [128, KT, TQ])
        qk_hi = t("qk_hi", [128, KT, TQ], F32R)
        qk_lo = t("qk_lo", [128, KT, TQ], F32R)
        prob1 = t("prob1", [TQ, SK])
        prob1T = t("prob1T", [KEYT, NKEY, TQ])
        sm1 = t("sm1", [TQ, 8])
        cT = t("cT", [128, KT, TQ])
        tf = t("tf", [128, KT, TQ])
        gl = t("gl", [TQ, NE])
        cmp_a = t("cmp_a", [TQ, NE, NE])
        cmp_b = t("cmp_b", [TQ, NE, NE])
        rk = t("rk", [TQ, 4, NE])
        rs = t("rs", [TQ, 4])
        rT = t("rT", [NE, TQ])

        KV = [psum[0], psum[1]]
        S = [psum[2], psum[3]]
        PT = [psum[4], psum[5]]
        OT = psum[6]
        TL = psum[7]

        ld_wkv, ld_w, ld_stage, ld_vec = sem("ld_wkv"), sem("ld_w"), sem("ld_stage"), sem("ld_vec")
        s_ident = sem("s_ident")
        s_zero = sem("s_zero")
        s_zero_q = sem("s_zero_q")
        s_gates = sem("s_gates")
        s_rows = sem("s_rows")
        s_wkv = sem("s_wkv")
        s_wkv_lo = sem("s_wkv_lo")
        s_su_pe = sem("s_su_pe")
        s_su = sem("s_su")

        e_x = event("e_x", 1, 16)
        e_ctx = event("e_ctx", 1, 16)
        e_kv_pe = event("e_kv_pe", 18)
        e_kv_act = event("e_kv_act", 15)
        e_kv_dve = event("e_kv_dve", 15)
        e_mv_h = event("e_mv_h", 2)
        e_rs_h = event("e_rs_h", 2)
        e_xn = event("e_xn", 1)
        e_xnT_pe = event("e_xnT_pe", 1)
        e_xnT = event("e_xnT", 1)
        e_s = event("e_s", NH)
        e_max = event("e_max", NH)
        e_exp = event("e_exp", NH)
        e_rinv = event("e_rinv", NH)
        e_prob = event("e_prob", NH)
        e_pt_pe = event("e_pt_pe", NH)
        e_pt = event("e_pt", NH)
        e_o = event("e_o", NH)
        e_oT = event("e_oT", NP)
        e_xb0 = event("e_xb0", 1)
        e_ch = event("e_ch", 3)
        e_tl = event("e_tl", 14)
        e_tl_act = event("e_tl_act", 7)
        e_tl_dve = event("e_tl_dve", 9)
        e_mv_t = event("e_mv_t", 4)
        e_rs_t = event("e_rs_t", 4)
        e_n = event("e_n", 3)
        e_n3 = event("e_n3", 1)
        e_xb = event("e_xb", 3)
        e_ct = event("e_ct", 14)
        e_bias1 = event("e_bias1", 1)
        e_r1 = event("e_r1", 1)
        e_gmax = event("e_gmax", 1)
        e_gexp = event("e_gexp", 1)
        e_tT = event("e_tT", 1)
        e_route = event("e_route", 1)
        e_route_c = event("e_route_c", 1)
        e_ph = event("e_ph", 12)
        e_pt_ch = event("e_pt_ch", 28)

        scale_h = float(DH) ** -0.5
        scale_1 = float(D) ** -0.5
        PASSES = ((0, 0), (0, 1), (1, 0))
        ctxT = (ctxT_hi, ctxT_lo)
        wkv = (wkv_hi, wkv_lo)
        kk = (k_hi, k_lo)
        qq = (q_hi, q_lo)
        qk = (qk_hi, qk_lo)

        USES = ["c"] * KT + ["v0", "v1"] * NKEY + ["q"] * 2 + ["k"] * NP
        ACT_READS = [int(u != "v1") for u in USES]
        DVE_READS = [int(u != "v0") for u in USES]
        USE_V, USE_Q, USE_K = KT, KT + 2 * NKEY, KT + 2 * NKEY + 2

        def wait_kv_free(eng, step, n):
            last, shift = (n - 2, 0) if n >= 2 else (n - 2 + len(USES), -1)
            if ACT_READS[last]:
                e_kv_act.wait(eng, step, sum(ACT_READS[:last + 1]), shift)
            if DVE_READS[last]:
                e_kv_dve.wait(eng, step, sum(DVE_READS[:last + 1]), shift)

        TL_READ = {0: (0, 1), 1: (1, 1), 2: (1, 2), 3: (2, 2), 4: (3, 2), 5: (4, 3), 6: (5, 4),
                   7: (6, 4), 8: (6, 5), 9: (6, 6), 10: (7, 6), 11: (7, 7), 12: (7, 8), 13: (7, 9)}
        SLOT = {1: 1, 2: 2, 3: 4, 4: 5, 5: 6, 6: 7, 7: 9, 8: 10, 9: 11, 10: 14, 11: 15, 12: 17, 13: 18}
        STAGE = {s: n for n, s in SLOT.items()}
        SLOTS = NH + 3

        stage = v[:, :, :].rearrange("p a n -> p (a n)").rearrange("p (s n) -> p s n", n=D)
        gw_in = cmp_a[0:NE, :, :].rearrange("p a b -> p (a b)")
        dft_ab = [ctx_in[:, 1, 0:KT, :],
                  prob[:, :, :].rearrange("p a n -> p (a n)")[:, 0:KT * D].rearrange("p (k n) -> p k n", k=KT)]
        ST_WK, ST_RE, ST_IM, ST_COS, ST_SIN, ST_NSIN = 0, 2, 4, 6, 8, 10

        block = scope.enter_context(nc.Block())

        @block.sync
        def _(eng):
            def load(dst, src, s):
                eng.dma_start(dst, src).then_inc(s, 16)

            def wide(a):
                return a.rearrange("(k p) n -> p k n", p=128)

            load(acc[:, :, :].rearrange("p b d -> p (b d)").rearrange("p (k n) -> p k n", k=KT),
                 wide(w_kv), ld_wkv)
            load(stage[:, ST_WK:ST_WK + KT, :], wide(Wk1), ld_stage)
            load(stage[:, ST_RE:ST_RE + KT, :], wide(w_re), ld_stage)
            load(stage[:, ST_IM:ST_IM + KT, :], wide(w_im), ld_stage)
            for n, at in enumerate((ST_COS, ST_SIN, ST_NSIN)):
                load(stage[:, at:at + KT, :], wide(dft[n]), ld_stage)
            load(gw_in, gate_w, ld_stage)
            load(wq[:, :, :], wide(w_q), ld_w)
            load(wo[:, :, :], wide(w_out), ld_w)
            load(wq1[:, :, :], wide(Wq1), ld_w)
            load(wv1[:, :, :], wide(Wv1), ld_w)
            load(b2[:, :], mlp2_b, ld_w)

        N_STAGE, N_W, N_VEC = 7, 5, 12

        @block.gpsimd
        def _(eng):
            def load(dst, src, s):
                eng.dma_start(dst, src).then_inc(s, 16)

            def load_batch(b, par):
                eng.dma_start(x_in[:, par, :], x[bass.ds(b, 1), :, :].rearrange("b t d -> t (b d)")
                              ).then_inc(e_x.handle, 16)
                eng.dma_start(ctx_in[0:KEYT, par, :, :],
                              ctx[bass.ds(b, 1), :, :].rearrange("b (k t) d -> t (b k) d", t=KEYT)
                              ).then_inc(e_ctx.handle, 16)

            for n, value in enumerate((-0.5, EPS, 1.5)):
                eng.memset(consts[:, n:n + 1], value)
            eng.memset(ident[:, :], 0.0).then_inc(s_ident, 1)
            eng.memset(earlier[:, :, :], 1.0).then_inc(s_zero, 1)
            eng.wait_ge(s_ident, 1)
            eng.affine_select(out=ident[:, :], in_=ident[:, :], compare_op=ALU.not_equal, fill=1.0,
                              base=0, pattern=[[-1, 128]], channel_multiplier=1).then_inc(s_ident, 1)
            eng.wait_ge(s_zero, 1)
            eng.affine_select(out=earlier[:, :, :], in_=earlier[:, :, :], compare_op=ALU.is_gt, fill=0.0,
                              base=0, pattern=[[1, NE], [-1, NE]], channel_multiplier=0)
            for par in range(2):
                for k in range(KT):
                    for c in ctxT:
                        last = eng.memset(c[:, par, k, SK:SKE].bitcast(F32), 0.0)
            last.then_inc(s_zero, 1)
            load_batch(0, 0)
            for n, g in enumerate((g_xattn, g_ffn)):
                load(gates[:, 2 * n:2 * n + 2], g.partition_broadcast(128), ld_vec)
            load(gates[:, 4:5], gate.partition_broadcast(128), ld_vec)
            for n, r in enumerate((b_out, ffn_bias, bv1)):
                load(rows[:, n, :], r.partition_broadcast(128), ld_vec)
            load(gbrow[:, :], gate_b.partition_broadcast(128), ld_vec)
            for n, c in enumerate((ln_gamma, ln_beta, bq1, bk1, rms_scale)):
                eng.dma_start(cols[:, n, :], c.rearrange("(k p) -> p k", p=128),
                              allow_slow_non_contiguous=True).then_inc(ld_vec, 16)
            eng.wait_ge(s_gates, 2)
            for n, g in enumerate((5, 2, 1)):
                eng.tensor_scalar(rows[:, n, :], rows[:, n, :], gt[:, g:g + 1], None, ALU.mult)
            eng.tensor_scalar(cols[:, BQ, :], cols[:, BQ, :], scale_1, None, ALU.mult
                              ).then_inc(s_rows, 1)
            eng.wait_ge(s_rows, 1)

            def rsqrt(chain, step, src, a, w, y, e_done, square=None):
                if square is not None:
                    chain(eng.tensor_tensor(a, square, square, ALU.mult))
                    chain.wait(step)
                    chain(eng.tensor_tensor(a, a, src, ALU.add))
                    chain.wait(step)
                    src = a
                chain(eng.tensor_tensor(a, src, consts[0:TQ, 1:2], ALU.add))
                chain.wait(step)
                chain(eng.tensor_tensor(y, a, consts[0:TQ, 0:1], ALU.pow))
                chain.wait(step)
                chain(eng.tensor_tensor(w, y, y, ALU.mult))
                chain.wait(step)
                chain(eng.tensor_tensor(w, w, a, ALU.mult))
                chain.wait(step)
                chain(eng.tensor_tensor(w, w, consts[0:TQ, 0:1], ALU.mult))
                chain.wait(step)
                chain(eng.tensor_tensor(w, w, consts[0:TQ, 2:3], ALU.add))
                chain.wait(step)
                e_done.done(eng.tensor_tensor(y, y, w, ALU.mult))

            def body(st):
                tb = st.before()
                ph, pt = Chain(eng, e_ph), Chain(eng, e_pt_ch)
                if st.heads:
                    for n in range(2):
                        e_mv_h.wait(eng, st, n + 1)
                        rsqrt(ph, st, ln_h[:, 12 * n + 7:12 * n + 8], ln_h[:, 12 * n + 8:12 * n + 9],
                              ln_h[:, 12 * n + 9:12 * n + 10], ln_h[:, 12 * n + 10:12 * n + 11], e_rs_h)
                    e_tl_dve.wait(eng, st, TL_READ[13][1], -2)
                    e_xb0.done(eng.tensor_tensor(xb0[:, st.par, :], x_in[:, st.par, :], rows[0:TQ, 0, :],
                                                 ALU.add))
                for s in range(SLOTS):
                    if st.heads and 1 <= s <= NH:
                        h = s - 1
                        e_rinv.wait(eng, st, h + 1)
                        e_prob.done(eng.tensor_tensor(prob[0:TQ, h % 2, :], prob[0:TQ, h % 2, :],
                                                      rinv[:, h:h + 1].broadcast_to([TQ, SK]), ALU.mult))
                    if st.tail:
                        lt = [ln_t[:, n:n + 1] for n in range(24)]
                        if s == 0:
                            e_mv_t.wait(eng, tb, 1)
                            rsqrt(pt, tb, lt[7], lt[8], lt[9], lt[10], e_rs_t)
                            e_xb.done(eng.tensor_tensor(xb1[:, :], x1[:, :], rows[0:TQ, 1, :], ALU.add))
                        if s == SLOT[2]:
                            e_mv_t.wait(eng, tb, 2)
                            rsqrt(pt, tb, lt[7], lt[8], lt[9], lt[10], e_rs_t)
                            e_xb.done(eng.tensor_tensor(xb2[:, :], x2[:, :], rows[0:TQ, 2, :], ALU.add))
                        if s == SLOT[9]:
                            e_mv_t.wait(eng, tb, 3)
                            rsqrt(pt, tb, lt[7], lt[8], lt[9], lt[10], e_rs_t)
                        if s == SLOT[9] + 1:
                            e_mv_t.wait(eng, tb, 4)
                            rsqrt(pt, tb, lt[19], lt[20], lt[21], lt[22], e_rs_t, square=lt[18])
                            e_n3.wait(eng, tb, 1)
                            e_tl_dve.wait(eng, tb, TL_READ[13][1], -1)
                            pt(eng.tensor_tensor(xm[:, :], n3[:, :],
                                                 gt[0:TQ, 3:4].broadcast_to([TQ, D]), ALU.mult))
                            pt.wait(tb)
                            e_xb.done(eng.tensor_tensor(xm[:, :], xm[:, :], x3[:, :], ALU.add))
                        if s == SLOT[10]:
                            at = bass.ds(tb.index() * TQ, TQ)
                            e_tl_act.wait(eng, tb, TL_READ[10][0])
                            pt(eng.tensor_copy(tT_hi[:, :, at], tf[:, :, :]))
                            pt.wait(tb)
                            e_tT.done(eng.tensor_tensor(tT_lo[:, :, at], tf[:, :, :],
                                                        tT_hi[:, :, at].bitcast(F32), ALU.subtract))
                        if s == SLOT[12]:
                            e_route.wait(eng, tb, 1)
                            e_route_c.done(eng.tensor_copy(
                                route[:, :, bass.ds(tb.index(), 1)].rearrange("t e b -> t (e b)"),
                                rk[:, 2, :]))
                    if s == SLOT[8] + 1 and st.heads and st.load:
                        if st.tail:
                            e_tl.wait(eng, tb, 9)
                        load_batch(st.after().index(), 1 - st.par)
                assert ph.n in (0, e_ph.per) and pt.n in (0, e_pt_ch.per), (ph.n, pt.n)

            pipeline(eng, body, B)

        @block.scalar
        def _(eng):
            eng.wait_ge(ld_vec, 16 * N_VEC)
            eng.activation(gt[:, 0:5], gates[:, :], ACT.Tanh).then_inc(s_gates, 1)
            eng.wait_ge(ld_wkv, 16)
            eng.activation(wkv_hi[:, :, :].rearrange("p k n -> p (k n)"),
                           acc[:, :, :].rearrange("p b d -> p (b d)"), ACT.Copy).then_inc(s_wkv, 1)
            eng.wait_ge(s_rows, 1)
            eng.wait_ge(s_zero, 2)

            def body(st):
                tb = st.before()
                uses = [0]

                def read_kv(n):
                    assert ACT_READS[n] and sum(ACT_READS[:n]) == uses[0]
                    uses[0] += 1
                    e_kv_pe.wait(eng, st, n + 1)
                    return KV[n % 2]

                def key_hi(p):
                    bank = read_kv(USE_K + p)
                    e_kv_act.done(eng.activation(k_hi[:, p, :], bank[:, 0:SKE], ACT.Copy))

                if st.heads:
                    for k in range(KT):
                        bank = read_kv(k)
                        e_kv_act.done(eng.activation(ctxT_hi[:, st.par, k, 0:SK], bank[:, 0:SK],
                                                     ACT.Copy))
                    for n in range(2 * NKEY):
                        if n % 2 == 0:
                            bank = read_kv(USE_V + n)
                            e_kv_act.done(eng.activation(v[0:KEYT, n // 2, 0:512], bank[0:KEYT, :],
                                                         ACT.Copy))
                    e_xnT_pe.wait(eng, st, 1)
                    for k in range(KT):
                        last = eng.activation(xnT[:, k, :], PT[0][:, k * TQ:(k + 1) * TQ], ACT.Identity,
                                              bias=cols[:, BETA, k:k + 1], scale=cols[:, GAMMA, k:k + 1])
                    e_xnT.done(last)
                    for n in range(2):
                        bank = read_kv(USE_Q + n)
                        pairs = slice(n * NP // 2, (n + 1) * NP // 2)
                        for half in range(2):
                            rows_ = slice(64 * half, 64 * half + 64)
                            last = eng.activation(
                                q_hi[rows_, pairs, half, :],
                                bank[rows_, 0:NP // 2 * TQ].rearrange("p (a t) -> p a t", t=TQ),
                                ACT.Copy, scale=scale_h)
                        e_kv_act.done(last)
                    key_hi(0)
                    key_hi(1)
                for s in range(SLOTS):
                    if st.heads and s < NH:
                        e_max.wait(eng, st, s + 1)
                        e_pt_pe.wait(eng, st, s - 1)
                        e_exp.done(eng.activation(prob[0:TQ, s % 2, :], S[s % 2][0:TQ, 0:SK], ACT.Exp,
                                                  bias=negmax[:, s:s + 1], accum_out=rowsum[:, s:s + 1]))
                    if st.heads and s % 2 == 0 and s // 2 + 2 < NP:
                        key_hi(s // 2 + 2)
                    if st.tail:
                        if s in (SLOT[1], SLOT[3]):
                            e_tl.wait(eng, tb, STAGE[s] + 1)
                            e_tl_act.done(eng.activation(nT[:, :, :].rearrange("p k t -> p (k t)"),
                                                         TL[:, 0:KT * TQ], ACT.Copy))
                        if s == SLOT[4]:
                            e_tl.wait(eng, tb, 5)
                            for k in range(KT):
                                last = eng.activation(q1T[:, k, :], TL[:, k * TQ:(k + 1) * TQ],
                                                      ACT.Identity, bias=cols[:, BQ, k:k + 1],
                                                      scale=scale_1)
                            e_tl_act.done(last)
                        if s == SLOT[5]:
                            e_tl.wait(eng, tb, 6)
                            e_tl_act.done(eng.activation(qk_hi[:, :, :].rearrange("p k t -> p (k t)"),
                                                         TL[:, 0:KT * TQ], ACT.Copy))
                        if s == SLOT[6]:
                            e_bias1.wait(eng, tb, 1)
                            e_tl_act.done(eng.activation(prob1[:, :], TL[0:TQ, 0:SK], ACT.Exp,
                                                         bias=sm1[:, 3:4], accum_out=sm1[:, 4:5]))
                        if s == SLOT[7]:
                            e_tl.wait(eng, tb, 8)
                            e_tl_act.done(eng.activation(prob1T[:, :, :].rearrange("p k t -> p (k t)"),
                                                         TL[0:KEYT, 0:NKEY * TQ], ACT.Copy))
                        if s == SLOT[10]:
                            e_tl.wait(eng, tb, 11)
                            e_tT.wait(eng, tb, 1, -1)
                            for k in range(KT):
                                last = eng.activation(tf[:, k, :], TL[:, k * TQ:(k + 1) * TQ],
                                                      ACT.Copy, scale=cols[:, RMS, k:k + 1])
                            e_tl_act.done(last)
                        if s == SLOT[11]:
                            e_gmax.wait(eng, tb, 1)
                            e_gexp.done(eng.activation(rk[:, 1, :], gl[:, :], ACT.Exp, bias=rs[:, 0:1]))
                    if st.heads and 1 <= s <= NH:
                        h = s - 1
                        e_pt_pe.wait(eng, st, h + 1)
                        e_o.wait(eng, st, h - 1)
                        e_pt.done(eng.activation(probT[:, h % 2, :, :].rearrange("p k t -> p (k t)"),
                                                 PT[h % 2][0:KEYT, 0:NKEY * TQ], ACT.Copy))

            pipeline(eng, body, B)

        @block.vector
        def _(eng):
            for q in qq:
                eng.memset(q[0:64, :, 1, :].bitcast(F32), 0.0)
                last = eng.memset(q[64:128, :, 0, :].bitcast(F32), 0.0)
            last.then_inc(s_zero_q, 1)
            eng.wait_ge(s_gates, 1)
            eng.tensor_tensor(gt[:, 5:6], gt[:, 0:1], gt[:, 4:5], ALU.mult).then_inc(s_gates, 1)
            eng.wait_ge(s_wkv, 1)
            eng.tensor_tensor(wkv_lo[:, :, :].rearrange("p k n -> p (k n)"),
                              acc[:, :, :].rearrange("p b d -> p (b d)"),
                              wkv_hi[:, :, :].bitcast(F32).rearrange("p k n -> p (k n)"),
                              ALU.subtract).then_inc(s_wkv_lo, 1)
            eng.wait_ge(s_su_pe, 1)
            eng.tensor_copy(wk1T[:, :, :].rearrange("p k n -> p (k n)"), KV[0][:, :])
            eng.tensor_copy(gwT[:, :, :].rearrange("p k n -> p (k n)"), KV[1][:, 0:KT * NE]
                            ).then_inc(s_su, 1)
            for n in range(2):
                eng.wait_ge(s_su_pe, 2 + n)
                eng.tensor_scalar(dft_ab[n].rearrange("p k n -> p (k n)"), S[n][:, :],
                                  1.0 / D, None, ALU.mult).then_inc(s_su, 1)
            eng.wait_ge(s_su_pe, 4)
            eng.tensor_copy(fmix[:, :, :].rearrange("p k n -> p (k n)"), PT[0][:, :]).then_inc(s_su, 1)

            eng.wait_ge(ld_vec, 16 * N_VEC)
            eng.wait_ge(s_zero, 2)

            def norm(dst, src, mv, r):
                return eng.tensor_scalar(dst, src, mv[:, 0:1], r, ALU.subtract, ALU.mult)

            def body(st):
                tb = st.before()
                ch, ct = Chain(eng, e_ch), Chain(eng, e_ct)
                uses = [0]

                def read_kv(n):
                    assert DVE_READS[n] and sum(DVE_READS[:n]) == uses[0]
                    uses[0] += 1
                    e_kv_pe.wait(eng, st, n + 1)
                    if ACT_READS[n]:
                        e_kv_act.wait(eng, st, sum(ACT_READS[:n + 1]))
                    return KV[n % 2]

                def key_lo(p):
                    bank = read_kv(USE_K + p)
                    e_kv_dve.done(eng.tensor_tensor(k_lo[:, p, :], bank[:, 0:SKE],
                                                    k_hi[:, p, :].bitcast(F32), ALU.subtract))

                def value(t_):
                    bank = read_kv(USE_V + 2 * t_ + 1)
                    e_kv_dve.done(eng.tensor_copy(v[0:KEYT, t_, 512:1024], bank[0:KEYT, :]))

                def stats(chain, step, src, at, e_done):
                    chain(eng.bn_stats(at[:, 0:6], src))
                    chain.wait(step)
                    eng.memset(carrier[:, :], 0.0)
                    e_done.done(eng.bn_aggr(at[:, 6:8], at[:, 0:6]))

                lh = [ln_h[:, 0:12], ln_h[:, 12:24]]
                lt = [ln_t[:, 0:12], ln_t[:, 12:24]]
                if st.heads:
                    e_x.wait(eng, st, 1)
                    stats(ch, st, x_in[:, st.par, :], lh[0], e_mv_h)
                    for k in range(KT):
                        bank = read_kv(k)
                        e_kv_dve.done(eng.tensor_tensor(ctxT_lo[:, st.par, k, 0:SK], bank[:, 0:SK],
                                                        ctxT_hi[:, st.par, k, 0:SK].bitcast(F32),
                                                        ALU.subtract))
                    e_rs_h.wait(eng, st, 1)
                    ch(norm(n0[:, :], x_in[:, st.par, :], lh[0][:, 6:8], lh[0][:, 10:11]))
                    ch.wait(st)
                    stats(ch, st, n0[:, :], lh[1], e_mv_h)
                if st.tail:
                    e_tl.wait(eng, tb, 1)
                    e_xb0.wait(eng, tb, 1)
                    e_xb.wait(eng, tb, 3, -1)
                    e_tl_dve.done(eng.scalar_tensor_tensor(x1[:, :], TL[0:TQ, 0:D], gt[0:TQ, 5:6],
                                                           xb0[:, tb.par, :], ALU.mult, ALU.add))
                    e_tl_dve.wait(eng, tb, 1)
                    stats(ct, tb, x1[:, :], lt[0], e_mv_t)
                if st.heads:
                    value(0)
                    e_rs_h.wait(eng, st, 2)
                    e_xn.done(norm(xn[:, :], n0[:, :], lh[1][:, 6:8], lh[1][:, 10:11]))
                    value(1)
                    value(2)
                    for n in range(2):
                        bank = read_kv(USE_Q + n)
                        pairs = slice(n * NP // 2, (n + 1) * NP // 2)
                        for half in range(2):
                            rows_ = slice(64 * half, 64 * half + 64)
                            last = eng.scalar_tensor_tensor(
                                q_lo[rows_, pairs, half, :],
                                bank[rows_, 0:NP // 2 * TQ].rearrange("p (a t) -> p a t", t=TQ),
                                scale_h, q_hi[rows_, pairs, half, :].bitcast(F32),
                                ALU.mult, ALU.subtract)
                        e_kv_dve.done(last)
                    key_lo(0)
                    key_lo(1)
                for s in range(SLOTS):
                    if st.heads:
                        if 1 <= s <= NH:
                            e_exp.wait(eng, st, s)
                            e_rinv.done(eng.reciprocal(rinv[:, s - 1:s], rowsum[:, s - 1:s]))
                        if s < NH:
                            e_s.wait(eng, st, s + 1)
                            e_max.done(eng.tensor_reduce(negmax[:, s:s + 1], S[s % 2][0:TQ, 0:SK], AX.X,
                                                         ALU.max, negate=True))
                        if s % 2 == 0 and s // 2 + 2 < NP:
                            key_lo(s // 2 + 2)
                        if s >= 4 and s % 2 == 0:
                            p = (s - 4) // 2
                            e_o.wait(eng, st, 2 * p + 2)
                            e_oT.done(eng.tensor_copy(oT[:, p, :], OT[:, 0:TQ]))
                    if not st.tail:
                        continue
                    if s == 0:
                        e_rs_t.wait(eng, tb, 1)
                        e_n.done(norm(n1[:, :], x1[:, :], lt[0][:, 6:8], lt[0][:, 10:11]))
                    if s == SLOT[2]:
                        e_tl.wait(eng, tb, 3)
                        e_xb.wait(eng, tb, 1)
                        e_tl_dve.done(eng.scalar_tensor_tensor(x2[:, :], TL[0:TQ, 0:D], gt[0:TQ, 2:3],
                                                               xb1[:, :], ALU.mult, ALU.add))
                        e_tl_dve.wait(eng, tb, TL_READ[2][1])
                        stats(ct, tb, x2[:, :], lt[0], e_mv_t)
                    if s == SLOT[2] + 1:
                        e_rs_t.wait(eng, tb, 2)
                        e_n.done(norm(n2[:, :], x2[:, :], lt[0][:, 6:8], lt[0][:, 10:11]))
                    if s == SLOT[5]:
                        e_tl.wait(eng, tb, 6)
                        e_tl_act.wait(eng, tb, TL_READ[5][0])
                        eng.tensor_copy(sm1[:, 0:1], TL[0:TQ, 256:257])
                        e_tl_dve.done(eng.tensor_tensor(
                            qk_lo[:, :, :].rearrange("p k t -> p (k t)"), TL[:, 0:KT * TQ],
                            qk_hi[:, :, :].bitcast(F32).rearrange("p k t -> p (k t)"), ALU.subtract))
                    if s == SLOT[6]:
                        e_tl.wait(eng, tb, 7)
                        e_tl_dve.done(eng.tensor_reduce(sm1[:, 1:2], TL[0:TQ, 0:SK], AX.X, ALU.max))
                        e_tl_dve.wait(eng, tb, TL_READ[6][1])
                        ct(eng.tensor_tensor(sm1[:, 2:3], sm1[:, 1:2], sm1[:, 0:1], ALU.add))
                        ct.wait(tb)
                        e_bias1.done(eng.tensor_tensor(sm1[:, 3:4], sm1[:, 0:1], sm1[:, 2:3],
                                                       ALU.subtract))
                    if s == SLOT[6] + 1:
                        e_tl_act.wait(eng, tb, TL_READ[6][0])
                        ct(eng.reciprocal(sm1[:, 5:6], sm1[:, 4:5]))
                        ct.wait(tb)
                        ct(eng.tensor_tensor(sm1[:, 6:7], sm1[:, 5:6], gt[0:TQ, 1:2], ALU.mult))
                    if s == SLOT[8]:
                        e_tl.wait(eng, tb, 9)
                        e_tl_dve.done(eng.tensor_copy(cT[:, :, :].rearrange("p k t -> p (k t)"),
                                                      TL[:, 0:KT * TQ]))
                    if s == SLOT[9]:
                        e_tl.wait(eng, tb, 10)
                        e_xb.wait(eng, tb, 2)
                        ct.wait(tb)
                        e_tl_dve.done(eng.scalar_tensor_tensor(x3[:, :], TL[0:TQ, 0:D], sm1[:, 6:7],
                                                               xb2[:, :], ALU.mult, ALU.add))
                        e_tl_dve.wait(eng, tb, TL_READ[9][1])
                        stats(ct, tb, x3[:, :], lt[0], e_mv_t)
                    if s == SLOT[9] + 1:
                        e_rs_t.wait(eng, tb, 3)
                        e_n3.done(norm(n3[:, :], x3[:, :], lt[0][:, 6:8], lt[0][:, 10:11]))
                        e_n3.wait(eng, tb, 1)
                        stats(ct, tb, n3[:, :], lt[1], e_mv_t)
                    if s == SLOT[9] + 2:
                        e_rs_t.wait(eng, tb, 4)
                        e_n.done(eng.tensor_scalar(tn[:, :], n3[:, :], lt[1][:, 10:11], None, ALU.mult))
                    if s == SLOT[11]:
                        e_tl.wait(eng, tb, 12)
                        e_tl_dve.done(eng.tensor_tensor(gl[:, :], TL[0:TQ, 0:NE], gbrow[0:TQ, :],
                                                        ALU.add))
                        e_tl_dve.wait(eng, tb, TL_READ[11][1])
                        e_gmax.done(eng.tensor_reduce(rs[:, 0:1], gl[:, :], AX.X, ALU.max, negate=True))
                        g_j = gl[:, :].unsqueeze(1).broadcast_to([TQ, NE, NE])
                        g_e = gl[:, :].unsqueeze(2).broadcast_to([TQ, NE, NE])
                        ct(eng.tensor_tensor(cmp_b[:, :, :], g_j, g_e, ALU.is_equal))
                        ct(eng.tensor_tensor(cmp_a[:, :, :], g_j, g_e, ALU.is_gt))
                        ct.wait(tb)
                        ct(eng.tensor_tensor(cmp_b[:, :, :], cmp_b[:, :, :], earlier[:, :, :], ALU.mult))
                        ct.wait(tb)
                        ct(eng.tensor_tensor(cmp_a[:, :, :], cmp_a[:, :, :], cmp_b[:, :, :], ALU.add))
                        ct.wait(tb)
                        ct(eng.tensor_reduce(rk[:, 0, :], cmp_a[:, :, :], AX.X, ALU.add))
                        ct.wait(tb)
                    if s == SLOT[11] + 1:
                        e_gexp.wait(eng, tb, 1)
                        ct(eng.scalar_tensor_tensor(rk[:, 3, :], rk[:, 0, :], TOPK - 0.5, rk[:, 1, :],
                                                    ALU.is_lt, ALU.mult, accum_out=rs[:, 1:2]))
                        ct.wait(tb)
                        ct(eng.reciprocal(rs[:, 2:3], rs[:, 1:2]))
                        ct.wait(tb)
                        e_route_c.wait(eng, tb, 1, -1)
                        e_route.done(eng.tensor_scalar(rk[:, 2, :], rk[:, 3, :], rs[:, 2:3],
                                                       gt[0:TQ, 3:4], ALU.mult, ALU.mult))
                    if s == SLOT[12]:
                        e_tl.wait(eng, tb, 13)
                        e_tl_dve.done(eng.tensor_copy(rT[:, :], TL[0:NE, 0:TQ]))
                    if s == SLOT[13]:
                        e_tl.wait(eng, tb, 14)
                        e_xb.wait(eng, tb, 3)
                        e_tl_dve.done(eng.tensor_tensor(
                            acc[0:TQ, bass.ds(tb.index(), 1), :].rearrange("t b d -> t (b d)"),
                            TL[0:TQ, 0:D], xm[:, :], ALU.add))
                assert ch.n in (0, e_ch.per) and ct.n in (0, e_ct.per), (ch.n, ct.n)

            pipeline(eng, body, B)

        @block.tensor
        def _(eng):
            eng.wait_ge(s_ident, 2)
            eng.wait_ge(ld_stage, 16 * N_STAGE)
            for e in range(KT):
                for d in range(KT):
                    eng.transpose(KV[0][:, e * D + d * 128:e * D + (d + 1) * 128],
                                  stage[:, ST_WK + d, e * 128:(e + 1) * 128], ident[:, :])
            for k in range(KT):
                last = eng.transpose(KV[1][:, k * NE:(k + 1) * NE], gw_in[:, k * 128:(k + 1) * 128],
                                     ident[0:NE, 0:NE])
            last.then_inc(s_su_pe, 1)

            def square(bank, terms):
                for m in range(KT):
                    n = 0
                    for a, b in terms:
                        for k in range(KT):
                            n += 1
                            last = eng.matmul(bank[:, m * D:(m + 1) * D], a(k, m), b(k), start=(n == 1),
                                              stop=(n == KT * len(terms)))
                last.then_inc(s_su_pe, 1)

            def left(at):
                return lambda k, m: stage[:, at + k, m * 128:(m + 1) * 128]

            def right(at):
                return lambda k: stage[:, at + k, :]

            square(S[0], [(left(ST_RE), right(ST_COS)), (left(ST_IM), right(ST_SIN))])
            square(S[1], [(left(ST_IM), right(ST_COS)), (left(ST_RE), right(ST_NSIN))])
            eng.wait_ge(s_su, 3)
            square(PT[0], [(lambda k, m: dft_ab[0][:, k, m * 128:(m + 1) * 128], right(ST_COS)),
                           (lambda k, m: dft_ab[1][:, k, m * 128:(m + 1) * 128], right(ST_NSIN))])
            eng.wait_ge(s_su, 4)
            eng.wait_ge(s_wkv_lo, 1)
            eng.wait_ge(ld_w, 16 * N_W)
            eng.wait_ge(s_zero, 2)
            eng.wait_ge(s_zero_q, 1)
            eng.wait_ge(s_rows, 1)

            def body(st):
                tb = st.before()

                def split_product(out_, lhs, rhs):
                    n = 0
                    for i, j in PASSES:
                        for k in range(KT):
                            n += 1
                            last = eng.matmul(out_, lhs(i, k), rhs(j, k), start=(n == 1),
                                              stop=(n == KT * len(PASSES)))
                    return last

                def key(p):
                    n = USE_K + p
                    wait_kv_free(eng, st, n)
                    e_kv_pe.done(split_product(
                        KV[n % 2][:, 0:SKE], lambda i, k: wkv[i][:, k, p * 128:(p + 1) * 128],
                        lambda j, k: ctxT[j][:, st.par, k, :]))

                def tail(n):
                    if n == 0:
                        e_oT.wait(eng, tb, NP)
                        e_tl_dve.wait(eng, tb, TL_READ[13][1], -1)
                    else:
                        a, d = TL_READ[n - 1]
                        if n == 1 or TL_READ[n - 2][0] != a:
                            if a:
                                e_tl_act.wait(eng, tb, a)
                        if n == 1 or TL_READ[n - 2][1] != d:
                            e_tl_dve.wait(eng, tb, d)
                    if n == 0:
                        for p in range(NP):
                            last = eng.matmul(TL[0:TQ, 0:D], oT[:, p, :], wo[:, p, :], start=(p == 0),
                                              stop=(p == NP - 1))
                    if n in (1, 3, 10):
                        e_n.wait(eng, tb, {1: 1, 3: 2, 10: 3}[n])
                        src = {1: n1, 3: n2, 10: tn}[n]
                        for k in range(KT):
                            last = eng.transpose(TL[:, k * TQ:(k + 1) * TQ],
                                                 src[:, k * 128:(k + 1) * 128], ident[0:TQ, 0:TQ])
                    if n == 2:
                        for k in range(KT):
                            last = eng.matmul(TL[0:TQ, 0:D], nT[:, k, :], fmix[:, k, :], start=(k == 0),
                                              stop=(k == KT - 1))
                    if n == 4:
                        for m in range(KT):
                            for k in range(KT):
                                last = eng.matmul(TL[:, m * TQ:(m + 1) * TQ],
                                                  wq1[:, k, m * 128:(m + 1) * 128], nT[:, k, :],
                                                  start=(k == 0), stop=(k == KT - 1))
                    if n == 5:
                        for k in range(KT):
                            eng.matmul(TL[0:TQ, 256:257], q1T[:, k, :], cols[:, BK, k:k + 1],
                                       start=(k == 0), stop=(k == KT - 1))
                        for m in range(KT):
                            for k in range(KT):
                                last = eng.matmul(TL[:, m * TQ:(m + 1) * TQ],
                                                  wk1T[:, k, m * 128:(m + 1) * 128], q1T[:, k, :],
                                                  start=(k == 0), stop=(k == KT - 1))
                    if n == 6:
                        last = split_product(TL[0:TQ, 0:SKE], lambda i, k: qk[i][:, k, :],
                                             lambda j, k: ctxT[j][:, tb.par, k, :])
                    if n == 7:
                        for k in range(NKEY):
                            last = eng.transpose(TL[0:KEYT, k * TQ:(k + 1) * TQ],
                                                 prob1[:, k * KEYT:(k + 1) * KEYT], ident[0:TQ, 0:TQ])
                    if n == 8:
                        for m in range(KT):
                            for k in range(NKEY):
                                last = eng.matmul(TL[:, m * TQ:(m + 1) * TQ],
                                                  ctx_in[0:KEYT, tb.par, k, m * 128:(m + 1) * 128],
                                                  prob1T[:, k, :], start=(k == 0), stop=(k == NKEY - 1))
                    if n == 9:
                        for k in range(KT):
                            last = eng.matmul(TL[0:TQ, 0:D], cT[:, k, :], wv1[:, k, :], start=(k == 0),
                                              stop=(k == KT - 1))
                    if n == 11:
                        for k in range(KT):
                            last = eng.matmul(TL[0:TQ, 0:NE], tf[:, k, :], gwT[:, k, :], start=(k == 0),
                                              stop=(k == KT - 1))
                    if n == 12:
                        e_route.wait(eng, tb, 1)
                        last = eng.transpose(TL[0:NE, 0:TQ], rk[:, 2, :], ident[0:TQ, 0:TQ])
                    if n == 13:
                        last = eng.matmul(TL[0:TQ, 0:D], rT[:, :], b2[:, :], start=True, stop=True)
                    e_tl.done(last)

                if st.heads:
                    e_ctx.wait(eng, st, 1)
                    for k in range(KT):
                        wait_kv_free(eng, st, k)
                        for j in range(NKEY):
                            last = eng.transpose(KV[k % 2][:, j * KEYT:(j + 1) * KEYT],
                                                 ctx_in[0:KEYT, st.par, j, k * 128:(k + 1) * 128],
                                                 ident[0:KEYT, 0:KEYT])
                        e_kv_pe.done(last)
                if st.tail:
                    tail(0)
                if st.heads:
                    for n in range(2 * NKEY):
                        j, half = n // 2, n % 2
                        wait_kv_free(eng, st, USE_V + n)
                        if n == 0:
                            e_kv_dve.wait(eng, st, KT)
                        e_kv_pe.done(split_product(
                            KV[n % 2][0:KEYT, :],
                            lambda i, k: ctxT[i][:, st.par, k, j * KEYT:(j + 1) * KEYT],
                            lambda jj, k: wkv[jj][:, k, INNER + half * 512:INNER + (half + 1) * 512]))
                    e_xn.wait(eng, st, 1)
                    for k in range(KT):
                        last = eng.transpose(PT[0][:, k * TQ:(k + 1) * TQ], xn[:, k * 128:(k + 1) * 128],
                                             ident[0:TQ, 0:TQ])
                    e_xnT_pe.done(last)
                    e_xnT.wait(eng, st, 1)
                    for n in range(2):
                        wait_kv_free(eng, st, USE_Q + n)
                        for a in range(NP // 2):
                            p = n * NP // 2 + a
                            for k in range(KT):
                                last = eng.matmul(KV[n % 2][:, a * TQ:(a + 1) * TQ],
                                                  wq[:, k, p * 128:(p + 1) * 128], xnT[:, k, :],
                                                  start=(k == 0), stop=(k == KT - 1))
                        e_kv_pe.done(last)
                    key(0)
                    key(1)
                for s in range(SLOTS):
                    if st.heads and s < NH:
                        p, half = s // 2, s % 2
                        if half == 0:
                            e_kv_dve.wait(eng, st, sum(DVE_READS[:USE_K + p + 1]))
                        e_exp.wait(eng, st, *((s - 1, 0) if s >= 2 else (NH + s - 1, -1)))
                        for n, (i, j) in enumerate(PASSES):
                            last = eng.matmul(S[s % 2][0:TQ, 0:SKE], qq[i][:, p, half, :], kk[j][:, p, :],
                                              start=(n == 0), stop=(n == len(PASSES) - 1))
                        e_s.done(last)
                    if st.heads and s % 2 == 0 and s // 2 + 2 < NP:
                        key(s // 2 + 2)
                    if st.tail and s in STAGE:
                        tail(STAGE[s])
                    if st.heads and 1 <= s <= NH:
                        h = s - 1
                        e_prob.wait(eng, st, h + 1)
                        e_pt.wait(eng, st, *((h - 1, 0) if h >= 2 else (NH + h - 1, -1)))
                        for k in range(NKEY):
                            last = eng.transpose(PT[h % 2][0:KEYT, k * TQ:(k + 1) * TQ],
                                                 prob[0:TQ, h % 2, k * KEYT:(k + 1) * KEYT],
                                                 ident[0:TQ, 0:TQ])
                        e_pt_pe.done(last)
                    if st.heads and 2 <= s <= NH + 1:
                        h = s - 2
                        p, half = h // 2, h % 2
                        e_pt.wait(eng, st, h + 1)
                        if half == 0:
                            e_oT.wait(eng, st, p)
                        for k in range(NKEY):
                            last = eng.matmul(
                                OT[64 * half:64 * half + 64, 0:TQ],
                                v[0:KEYT, k, h * DH:(h + 1) * DH], probT[:, h % 2, k, :],
                                start=(k == 0), stop=(k == NKEY - 1))
                        e_o.done(last)

            pipeline(eng, body, B)


def phase2(nc, sb, event, sem, psum, ident, acc, tT_hi, tT_lo, route, mlp1_w, mlp1_b, mlp2_w, out):
    scope = ExitStack()
    with scope:
        def t(name, shape, dt=F32):
            return sb(name, shape, dt, scope)

        HT = HID // 128
        w1_in = t("w1_in", [128, HT, D])
        w2_in = t("w2_in", [128, KT, HID])
        w1_hi = t("w1_hi", [128, 2, KT, HID], F32R)
        w1_lo = t("w1_lo", [128, 2, KT, HID], F32R)
        w2_hi = t("w2_hi", [128, 2, HT, D], F32R)
        w2_lo = t("w2_lo", [128, 2, HT, D], F32R)
        b1_in = t("b1_in", [NE, 2 * HID])
        b1T = t("b1T", [128, NE, HT])
        b1c = t("b1c", [128, 2, HT])
        rc = t("rc", [TQ, 2, B])
        u = t("u", [128, 2, HT, CT])
        sg = t("sg", [128, 2, HT, CT])
        s_f = t("s_f", [128, 2, HT, CT])
        s_hi = t("s_hi", [128, 2, HT, CT], F32R)
        s_lo = t("s_lo", [128, 2, HT, CT], F32R)
        w1, w2, tt, ss = (w1_hi, w1_lo), (w2_hi, w2_lo), (tT_hi, tT_lo), (s_hi, s_lo)
        H = [[psum[0], psum[1]], [psum[2], psum[3]]]
        Y = [psum[4], psum[5]]
        WB = [psum[6], psum[7]]
        PASSES = ((0, 0), (0, 1), (1, 0))

        NCH = NC * HT
        f_w = event("f_w", 1, 32)
        f_b = sem("f_b")
        f_bT = sem("f_bT")
        f_wt = event("f_wt", 2)
        f_whi = event("f_whi", 2)
        f_wlo = event("f_wlo", 2)
        f_col = event("f_col", 1)
        f_h = event("f_h", NCH)
        f_u = event("f_u", NCH)
        f_sg = event("f_sg", NCH)
        f_s = event("f_s", NCH)
        f_shi = event("f_shi", NCH)
        f_slo = event("f_slo", NCH)
        f_y = event("f_y", B)
        f_acc = event("f_acc", B)
        f_out = sem("f_out")

        block = scope.enter_context(nc.Block())

        @block.sync
        def _(eng):
            eng.dma_start(b1_in[:, :], mlp1_b).then_inc(f_b, 16)
            for c in range(NC):
                eng.wait_ge(f_acc.handle, B * (NE - 1) + CB * (c + 1))
                eng.dma_start(out[c * CB:(c + 1) * CB, :, :].rearrange("b t d -> t b d"),
                              acc[0:TQ, c * CB:(c + 1) * CB, :]).then_inc(f_out, 16)
            eng.wait_ge(f_out, 16 * NC)

        @block.gpsimd
        def _(eng):
            def columns(st):
                f_acc.wait(eng, st, B, -2)
                b1_e = b1T[:, bass.ds(st.index(), 1), :].rearrange("p e m -> p (e m)")
                rc_e = route[:, bass.ds(st.index(), 1), :].rearrange("t e b -> t (e b)")
                eng.tensor_copy(b1c[:, st.par, :], b1_e)
                f_col.done(eng.tensor_copy(rc[:, st.par, :], rc_e))

            eng.wait_ge(f_bT, 2)
            columns(Step(None, 0, 0))

            def body(st):
                for c in range(NC):
                    if st.heads:
                        for m in range(HT):
                            n = c * HT + m
                            f_shi.wait(eng, st, n + 1)
                            f_y.wait(eng, st, CB * (c - 1))
                            f_slo.done(eng.tensor_tensor(s_lo[:, c % 2, m, :], s_f[:, c % 2, m, :],
                                                         s_hi[:, c % 2, m, :].bitcast(F32),
                                                         ALU.subtract))
                    if c == 1 and st.load:
                        columns(st.after())

            pipeline(eng, body, NE)

        @block.scalar
        def _(eng):
            def load(st):
                at = st.index()
                eng.dma_start(w1_in[:, :, :],
                              mlp1_w[bass.ds(at, 1), :, :].rearrange(
                                  "e (k p two) h -> two p (e k) h", two=2, p=128)[0]
                              ).then_inc(f_w.handle, 16)
                eng.dma_start(w2_in[:, :, :],
                              mlp2_w[bass.ds(at, 1), :, :].rearrange("e (k p) i -> p (e k) i", p=128)
                              ).then_inc(f_w.handle, 16)

            def high(st):
                for n, w in enumerate((w1_hi, w2_hi)):
                    f_wt.wait(eng, st, n + 1)
                    f_whi.done(eng.activation(w[:, st.par, :, :].rearrange("p k n -> p (k n)"),
                                              WB[n][:, :], ACT.Copy))

            load(Step(None, 0, 0))
            high(Step(None, 0, 0))

            def body(st):
                if st.load:
                    f_wt.wait(eng, st, 2)
                    load(st.after())
                for c in range(NC):
                    if not st.heads:
                        continue
                    for m in range(HT):
                        n = c * HT + m
                        f_u.wait(eng, st, n + 1)
                        f_sg.done(eng.activation(sg[:, c % 2, m, :], u[:, c % 2, m, :], ACT.Sigmoid,
                                                 scale=ALPHA))
                    for m in range(HT):
                        n = c * HT + m
                        f_s.wait(eng, st, n + 1)
                        f_y.wait(eng, st, CB * (c - 1))
                        f_shi.done(eng.activation(s_hi[:, c % 2, m, :], s_f[:, c % 2, m, :], ACT.Copy))
                    if c == 2 and st.load:
                        high(st.after())

            pipeline(eng, body, NE)

        @block.vector
        def _(eng):
            def low(st):
                for n, (w, hi) in enumerate(((w1_lo, w1_hi), (w2_lo, w2_hi))):
                    f_whi.wait(eng, st, n + 1)
                    f_wlo.done(eng.tensor_tensor(
                        w[:, st.par, :, :].rearrange("p k n -> p (k n)"), WB[n][:, :],
                        hi[:, st.par, :, :].bitcast(F32).rearrange("p k n -> p (k n)"), ALU.subtract))

            eng.wait_ge(f_bT, 1)
            for m in range(HT):
                last = eng.tensor_copy(b1T[:, :, m], Y[0][:, m * NE:(m + 1) * NE])
            last.then_inc(f_bT, 1)
            low(Step(None, 0, 0))

            def body(st):
                for c in range(NC):
                    if st.heads:
                        for m in range(HT):
                            n = c * HT + m
                            if n == 0:
                                f_col.wait(eng, st, 1)
                            f_h.wait(eng, st, n + 1)
                            f_sg.wait(eng, st, n + 1 - 2 * HT)
                            f_u.done(eng.tensor_scalar(u[:, c % 2, m, :], H[c % 2][m][:, 0:CT],
                                                       b1c[:, st.par, m:m + 1], LIMIT, ALU.add,
                                                       ALU.min))
                        for m in range(HT):
                            n = c * HT + m
                            f_sg.wait(eng, st, n + 1)
                            f_slo.wait(eng, st, n + 1 - 2 * HT)
                            f_s.done(eng.scalar_tensor_tensor(s_f[:, c % 2, m, :], u[:, c % 2, m, :],
                                                              LIMIT + 1.0, sg[:, c % 2, m, :],
                                                              ALU.mult, ALU.mult))
                    if c == 2 and st.load:
                        low(st.after())
                    add(st, c)

            def add(st, c):
                if c == 0:
                    if not st.tail:
                        return
                    own, cc = st.before(), NC - 1
                else:
                    if not st.heads:
                        return
                    own, cc = st, c - 1
                for b in range(CB):
                    batch = cc * CB + b
                    if b % 2 == 0:
                        f_y.wait(eng, own, batch + 2)
                    f_acc.wait(eng, own, batch + 1 - CB)
                    f_acc.done(eng.scalar_tensor_tensor(
                        acc[0:TQ, batch, :], Y[b // 2][0:TQ, (b % 2) * D:(b % 2 + 1) * D],
                        rc[:, own.par, batch:batch + 1], acc[0:TQ, batch, :], ALU.mult, ALU.add))

            pipeline(eng, body, NE)

        @block.tensor
        def _(eng):
            def weights(st):
                f_w.wait(eng, st, 1)
                f_wlo.wait(eng, st, 2, -1)
                for k in range(KT):
                    for m in range(HT):
                        last = eng.transpose(WB[0][:, k * HID + m * 128:k * HID + (m + 1) * 128],
                                             w1_in[:, m, k * 128:(k + 1) * 128], ident[:, :])
                f_wt.done(last)
                for m in range(HT):
                    for k in range(KT):
                        last = eng.transpose(WB[1][:, m * D + k * 128:m * D + (k + 1) * 128],
                                             w2_in[:, k, m * 128:(m + 1) * 128], ident[:, :])
                f_wt.done(last)

            eng.wait_ge(f_b, 16)
            for m in range(HT):
                last = eng.transpose(Y[0][:, m * NE:(m + 1) * NE],
                                     b1_in[:, m * D:(m + 1) * D].rearrange("e (i two) -> e two i",
                                                                          two=2)[:, 0, :],
                                     ident[0:NE, 0:NE])
            last.then_inc(f_bT, 1)
            weights(Step(None, 0, 0))
            eng.wait_ge(f_bT, 2)

            def output(st, c):
                if c == 0:
                    if not st.tail:
                        return
                    own, cc = st.before(), NC - 1
                else:
                    if not st.heads:
                        return
                    own, cc = st, c - 1
                f_slo.wait(eng, own, (cc + 1) * HT)
                for b in range(CB):
                    batch = cc * CB + b
                    if b % 2 == 0:
                        f_acc.wait(eng, own, batch - 2)
                    n = 0
                    for i, j in PASSES:
                        for m in range(HT):
                            n += 1
                            last = eng.matmul(Y[b // 2][0:TQ, (b % 2) * D:(b % 2 + 1) * D],
                                              ss[i][:, cc % 2, m, b * TQ:(b + 1) * TQ],
                                              w2[j][:, own.par, m, :], start=(n == 1),
                                              stop=(n == HT * len(PASSES)))
                    f_y.done(last)

            def body(st):
                for c in range(NC):
                    if st.heads:
                        for m in range(HT):
                            if c == 0 and m == 0:
                                f_wlo.wait(eng, st, 2)
                            f_u.wait(eng, st, c * HT + m + 1 - 2 * HT)
                            n = 0
                            for i, j in PASSES:
                                for k in range(KT):
                                    n += 1
                                    last = eng.matmul(H[c % 2][m][:, 0:CT],
                                                      w1[i][:, st.par, k, m * 128:(m + 1) * 128],
                                                      tt[j][:, k, c * CT:(c + 1) * CT],
                                                      start=(n == 1), stop=(n == KT * len(PASSES)))
                            f_h.done(last)
                    output(st, c)
                    if c == 1 and st.load:
                        weights(st.after())

            pipeline(eng, body, NE)


_INS = ["x", "ctx_1024", "g_xattn", "g_ffn", "L0_xattn_ln_gamma", "L0_xattn_ln_beta", "L0_xattn_w_q",
        "L0_xattn_w_kv", "L0_xattn_w_out", "L0_xattn_b_out", "L0_xattn_gate", "L0_ffn_w_freq_real",
        "L0_ffn_w_freq_imag", "L0_ffn_bias", "L1_xattn_Wq", "L1_xattn_bq", "L1_xattn_Wk",
        "L1_xattn_bk", "L1_xattn_Wv", "L1_xattn_bv", "L1_ffn_scale", "L1_ffn_gate_w",
        "L1_ffn_gate_b", "L1_ffn_mlp1_w", "L1_ffn_mlp1_b", "L1_ffn_mlp2_w", "L1_ffn_mlp2_b"]


def kernel(**inputs):
    import concourse.bacc as bacc
    from concourse.bass_utils import run_bass_kernel_spmd

    nc = bacc.Bacc("TRN2", target_bir_lowering=False, num_devices=1)
    arrays, args = {}, []

    def give(name, a):
        a = np.ascontiguousarray(a)
        arrays[name] = a
        args.append(nc.dram_tensor(name, a.shape, mybir.dt.from_np(a.dtype), kind="ExternalInput").ap())

    for name in _INS:
        give(f"in_{name}", inputs[name])
    jk = (np.arange(D)[:, None] * np.arange(D)[None, :]) % D
    angle = 2.0 * np.pi * jk / D
    give("dft", np.stack([np.cos(angle), np.sin(angle), -np.sin(angle)]).astype(np.float32))
    out = nc.dram_tensor("out_0", (B, TQ, D), F32, kind="ExternalOutput").ap()
    build(nc, *args, out)
    r = run_bass_kernel_spmd(nc, [arrays], core_ids=[0])
    return r.results[0]["out_0"]
```

```python
from contextlib import ExitStack

import numpy as np
import concourse.bass as bass
from concourse import mybir

F32 = mybir.dt.float32
F32R = mybir.dt.float32r
ALU = mybir.AluOpType
ACT = mybir.ActivationFunctionType
AX = mybir.AxisListType

B, TQ, D = 16, 112, 256
SK = 375
KT = D // 128
NH, DH = 16, 64
NP = NH // 2
INNER = NH * DH
KEYT, NKEY = 125, 3
SKE = SK + 1
NE, TOPK = 16, 4
HID = 256
CB = 4
NC = B // CB
CT = CB * TQ
EPS = 1e-5
ALPHA, LIMIT = 1.702, 7.0


class Event:

    def __init__(self, handle, per, unit=1):
        self.handle, self.per, self.unit = handle, per, unit

    def wait(self, eng, step, k, shift=0):
        n = step.off + shift
        fixed = (self.per * n + k) * self.unit
        if step.reg is None:
            if fixed > 0:
                eng.wait_ge(self.handle, fixed)
        else:
            eng.wait_ge(self.handle, step.reg * (self.per * self.unit) + fixed)

    def done(self, ins):
        ins.then_inc(self.handle, self.unit)


class Step:

    def __init__(self, reg, off, par, heads=True, tail=True, load=True):
        self.reg, self.off, self.par = reg, off, par
        self.heads, self.tail, self.load = heads, tail, load

    def before(self):
        return Step(self.reg, self.off - 1, 1 - self.par)

    def after(self):
        return Step(self.reg, self.off + 1, 1 - self.par)

    def index(self):
        return self.off if self.reg is None else self.reg + self.off


def pipeline(eng, body, n):
    body(Step(None, 0, 0, tail=False))
    body(Step(None, 1, 1))
    with eng.Fori(2, n - 3, 2) as i:
        body(Step(i, 0, 0))
        body(Step(i, 1, 1))
    body(Step(None, n - 2, 0))
    body(Step(None, n - 1, 1, load=False))
    body(Step(None, n, 0, heads=False, load=False))


class Chain:

    def __init__(self, eng, event):
        self.eng, self.event, self.n = eng, event, 0

    def __call__(self, ins):
        self.event.done(ins)
        self.n += 1

    def wait(self, step):
        self.event.wait(self.eng, step, self.n)


def build(nc, x, ctx, g_xattn, g_ffn, ln_gamma, ln_beta, w_q, w_kv, w_out, b_out, gate, w_re, w_im,
          ffn_bias, Wq1, bq1, Wk1, bk1, Wv1, bv1, rms_scale, gate_w, gate_b, mlp1_w, mlp1_b, mlp2_w,
          mlp2_b, dft, out):
    top = ExitStack()
    with top:
        def sb(name, shape, dt=F32, scope=top):
            return scope.enter_context(nc.sbuf_tensor(name, shape, dt))

        def sem(name):
            return top.enter_context(nc.semaphore(name))

        def event(name, per, unit=1):
            return Event(sem(name), per, unit)

        ident = sb("ident", [128, 128])
        acc = sb("acc", [128, B, D])
        tT_hi = sb("tT_hi", [128, KT, B * TQ], F32R)
        tT_lo = sb("tT_lo", [128, KT, B * TQ], F32R)
        route = sb("route", [TQ, NE, B])

        psum = [top.enter_context(nc.psum_tensor(f"bank{i}", [128, 512], F32)) for i in range(8)]

        phase1(nc, sb, event, sem, psum, ident, acc, tT_hi, tT_lo, route, x, ctx, g_xattn, g_ffn,
               ln_gamma, ln_beta, w_q, w_kv, w_out, b_out, gate, w_re, w_im, ffn_bias, Wq1, bq1, Wk1,
               bk1, Wv1, bv1, rms_scale, gate_w, gate_b, mlp2_b, dft)
        phase2(nc, sb, event, sem, psum, ident, acc, tT_hi, tT_lo, route, mlp1_w, mlp1_b, mlp2_w, out)


def phase1(nc, sb, event, sem, psum, ident, acc, tT_hi, tT_lo, route, x, ctx, g_xattn, g_ffn,
           ln_gamma, ln_beta, w_q, w_kv, w_out, b_out, gate, w_re, w_im, ffn_bias, Wq1, bq1, Wk1,
           bk1, Wv1, bv1, rms_scale, gate_w, gate_b, mlp2_b, dft):
    scope = ExitStack()
    with scope:
        def t(name, shape, dt=F32):
            return sb(name, shape, dt, scope)

        wq = t("wq", [128, KT, INNER])
        wkv_hi = t("wkv_hi", [128, KT, 2 * INNER], F32R)
        wkv_lo = t("wkv_lo", [128, KT, 2 * INNER], F32R)
        wo = t("wo", [128, NP, D])
        wq1 = t("wq1", [128, KT, D])
        wk1T = t("wk1T", [128, KT, D])
        wv1 = t("wv1", [128, KT, D])
        fmix = t("fmix", [128, KT, D])
        gwT = t("gwT", [128, KT, NE])
        b2 = t("b2", [NE, D])
        cols = t("cols", [128, 5, KT])
        GAMMA, BETA, BQ, BK, RMS = range(5)
        rows = t("rows", [128, 3, D])
        gbrow = t("gbrow", [128, NE])
        gates = t("gates", [128, 5])
        gt = t("gt", [128, 6])
        consts = t("consts", [128, 3])
        carrier = t("carrier", [1, 1])
        earlier = t("earlier", [TQ, NE, NE])

        x_in = t("x_in", [TQ, 2, D])
        ctx_in = t("ctx_in", [128, 2, NKEY, D])
        ctxT_hi = t("ctxT_hi", [128, 2, KT, SKE], F32R)
        ctxT_lo = t("ctxT_lo", [128, 2, KT, SKE], F32R)
        n0 = t("n0", [TQ, D])
        xn = t("xn", [TQ, D])
        xnT = t("xnT", [128, KT, TQ])
        q_hi = t("q_hi", [128, NP, 2, TQ], F32R)
        q_lo = t("q_lo", [128, NP, 2, TQ], F32R)
        k_hi = t("k_hi", [128, NP, SKE], F32R)
        k_lo = t("k_lo", [128, NP, SKE], F32R)
        v = t("v", [128, NKEY, INNER])
        prob = t("prob", [128, 2, SK])
        probT = t("probT", [KEYT, 2, NKEY, TQ])
        negmax = t("negmax", [TQ, NH])
        rowsum = t("rowsum", [TQ, NH])
        rinv = t("rinv", [TQ, NH])
        oT = t("oT", [128, NP, TQ])
        ln_h = t("ln_h", [TQ, 24])
        ln_t = t("ln_t", [TQ, 24])
        xb0 = t("xb0", [TQ, 2, D])
        x1 = x2 = x3 = t("x123", [TQ, D])
        xb1 = xb2 = t("xb12", [TQ, D])
        n1 = n2 = tn = t("n12t", [TQ, D])
        n3 = t("n3", [TQ, D])
        xm = t("xm", [TQ, D])
        nT = t("nT", [128, KT, TQ])
        q1T = t("q1T", [128, KT, TQ])
        qk_hi = t("qk_hi", [128, KT, TQ], F32R)
        qk_lo = t("qk_lo", [128, KT, TQ], F32R)
        prob1 = t("prob1", [TQ, SK])
        prob1T = t("prob1T", [KEYT, NKEY, TQ])
        sm1 = t("sm1", [TQ, 8])
        cT = t("cT", [128, KT, TQ])
        tf = t("tf", [128, KT, TQ])
        gl = t("gl", [TQ, NE])
        cmp_a = t("cmp_a", [TQ, NE, NE])
        cmp_b = t("cmp_b", [TQ, NE, NE])
        rk = t("rk", [TQ, 4, NE])
        rs = t("rs", [TQ, 4])
        rT = t("rT", [NE, TQ])

        KV = [psum[0], psum[1]]
        S = [psum[2], psum[3]]
        PT = [psum[4], psum[5]]
        OT = psum[6]
        TL = psum[7]

        ld_wkv, ld_w, ld_stage, ld_vec = sem("ld_wkv"), sem("ld_w"), sem("ld_stage"), sem("ld_vec")
        s_ident = sem("s_ident")
        s_zero = sem("s_zero")
        s_zero_q = sem("s_zero_q")
        s_gates = sem("s_gates")
        s_rows = sem("s_rows")
        s_wkv = sem("s_wkv")
        s_wkv_lo = sem("s_wkv_lo")
        s_su_pe = sem("s_su_pe")
        s_su = sem("s_su")

        e_x = event("e_x", 1, 16)
        e_ctx = event("e_ctx", 1, 16)
        e_kv_pe = event("e_kv_pe", 20)
        e_kv_act = event("e_kv_act", 17)
        e_kv_dve = event("e_kv_dve", 15)
        e_mv_h = event("e_mv_h", 2)
        e_rs_h = event("e_rs_h", 2)
        e_xn = event("e_xn", 1)
        e_s = event("e_s", NH)
        e_max = event("e_max", NH)
        e_exp = event("e_exp", NH)
        e_rinv = event("e_rinv", NH)
        e_prob = event("e_prob", NH)
        e_pt_pe = event("e_pt_pe", NH)
        e_pt = event("e_pt", NH)
        e_o = event("e_o", NH)
        e_oT = event("e_oT", NP)
        e_xb0 = event("e_xb0", 1)
        e_ch = event("e_ch", 11)
        e_tl = event("e_tl", 14)
        e_tl_act = event("e_tl_act", 7)
        e_tl_dve = event("e_tl_dve", 9)
        e_mv_t = event("e_mv_t", 4)
        e_rs_t = event("e_rs_t", 4)
        e_n = event("e_n", 3)
        e_n3 = event("e_n3", 1)
        e_xb = event("e_xb", 3)
        e_ct = event("e_ct", 31)
        e_bias1 = event("e_bias1", 1)
        e_r1 = event("e_r1", 1)
        e_gmax = event("e_gmax", 1)
        e_gexp = event("e_gexp", 1)
        e_tT = event("e_tT", 1)
        e_route = event("e_route", 1)
        e_route_c = event("e_route_c", 1)
        e_pt_ch = event("e_pt_ch", 2)

        scale_h = float(DH) ** -0.5
        scale_1 = float(D) ** -0.5
        PASSES = ((0, 0), (0, 1), (1, 0))
        ctxT = (ctxT_hi, ctxT_lo)
        wkv = (wkv_hi, wkv_lo)
        kk = (k_hi, k_lo)
        qq = (q_hi, q_lo)
        qk = (qk_hi, qk_lo)

        USES = ["x"] * KT + ["q"] + ["c"] * KT + ["k"] * 2 + ["q"] + ["v0", "v1"] * NKEY + ["k"] * (NP - 2)
        ACT_READS = [int(u != "v1") for u in USES]
        DVE_READS = [int(u not in ("v0", "x")) for u in USES]
        USE_X, USE_C, USE_V = USES.index("x"), USES.index("c"), USES.index("v0")
        USE_Q = [n for n, u in enumerate(USES) if u == "q"]
        USE_K = [n for n, u in enumerate(USES) if u == "k"]

        def wait_kv_free(eng, step, n):
            last, shift = (n - 2, 0) if n >= 2 else (n - 2 + len(USES), -1)
            if ACT_READS[last]:
                e_kv_act.wait(eng, step, sum(ACT_READS[:last + 1]), shift)
            if DVE_READS[last]:
                e_kv_dve.wait(eng, step, sum(DVE_READS[:last + 1]), shift)

        TL_READ = {0: (0, 1), 1: (1, 1), 2: (1, 2), 3: (2, 2), 4: (3, 2), 5: (4, 3), 6: (5, 4),
                   7: (6, 4), 8: (6, 5), 9: (6, 6), 10: (7, 6), 11: (7, 7), 12: (7, 8), 13: (7, 9)}
        SLOT = {1: -1, 2: 0, 3: 3, 4: 4, 5: 5, 6: 6, 7: 8, 8: 9, 9: 10, 10: 13, 11: 14, 12: 17, 13: 18}
        STAGE = {s: n for n, s in SLOT.items()}
        SLOTS = NH + 3
        AT_STATS, AT_XN, AT_X, AT_CTX, AT_K, AT_Q = (7, 8), 9, 11, (13, 14), (15, 16), (12, 17)
        LAG_T, LAG_O = 2, 3

        stage = v[:, :, :].rearrange("p a n -> p (a n)").rearrange("p (s n) -> p s n", n=D)
        gw_in = cmp_a[0:NE, :, :].rearrange("p a b -> p (a b)")
        dft_ab = [ctx_in[:, 1, 0:KT, :],
                  prob[:, :, :].rearrange("p a n -> p (a n)")[:, 0:KT * D].rearrange("p (k n) -> p k n", k=KT)]
        ST_WK, ST_RE, ST_IM, ST_COS, ST_SIN, ST_NSIN = 0, 2, 4, 6, 8, 10

        block = scope.enter_context(nc.Block())

        @block.sync
        def _(eng):
            def load(dst, src, s):
                eng.dma_start(dst, src).then_inc(s, 16)

            def wide(a):
                return a.rearrange("(k p) n -> p k n", p=128)

            load(acc[:, :, :].rearrange("p b d -> p (b d)").rearrange("p (k n) -> p k n", k=KT),
                 wide(w_kv), ld_wkv)
            load(stage[:, ST_WK:ST_WK + KT, :], wide(Wk1), ld_stage)
            load(stage[:, ST_RE:ST_RE + KT, :], wide(w_re), ld_stage)
            load(stage[:, ST_IM:ST_IM + KT, :], wide(w_im), ld_stage)
            for n, at in enumerate((ST_COS, ST_SIN, ST_NSIN)):
                load(stage[:, at:at + KT, :], wide(dft[n]), ld_stage)
            load(gw_in, gate_w, ld_stage)
            load(wq[:, :, :], wide(w_q), ld_w)
            load(wo[:, :, :], wide(w_out), ld_w)
            load(wq1[:, :, :], wide(Wq1), ld_w)
            load(wv1[:, :, :], wide(Wv1), ld_w)
            load(b2[:, :], mlp2_b, ld_w)

        N_STAGE, N_W, N_VEC = 7, 5, 12

        @block.gpsimd
        def _(eng):
            def load(dst, src, s):
                eng.dma_start(dst, src).then_inc(s, 16)

            def load_x(b, par):
                eng.dma_start(x_in[:, par, :], x[bass.ds(b, 1), :, :].rearrange("b t d -> t (b d)")
                              ).then_inc(e_x.handle, 16)

            def load_ctx(b, par):
                eng.dma_start(ctx_in[0:KEYT, par, :, :],
                              ctx[bass.ds(b, 1), :, :].rearrange("b (k t) d -> t (b k) d", t=KEYT)
                              ).then_inc(e_ctx.handle, 16)

            for n, value in enumerate((-0.5, EPS, 1.5)):
                eng.memset(consts[:, n:n + 1], value)
            eng.memset(ident[:, :], 0.0).then_inc(s_ident, 1)
            eng.memset(earlier[:, :, :], 1.0).then_inc(s_zero, 1)
            eng.wait_ge(s_ident, 1)
            eng.affine_select(out=ident[:, :], in_=ident[:, :], compare_op=ALU.not_equal, fill=1.0,
                              base=0, pattern=[[-1, 128]], channel_multiplier=1).then_inc(s_ident, 1)
            eng.wait_ge(s_zero, 1)
            eng.affine_select(out=earlier[:, :, :], in_=earlier[:, :, :], compare_op=ALU.is_gt, fill=0.0,
                              base=0, pattern=[[1, NE], [-1, NE]], channel_multiplier=0)
            for par in range(2):
                for k in range(KT):
                    for c in ctxT:
                        last = eng.memset(c[:, par, k, SK:SKE].bitcast(F32), 0.0)
            last.then_inc(s_zero, 1)
            load_x(0, 0)
            load_ctx(0, 0)
            for n, g in enumerate((g_xattn, g_ffn)):
                load(gates[:, 2 * n:2 * n + 2], g.partition_broadcast(128), ld_vec)
            load(gates[:, 4:5], gate.partition_broadcast(128), ld_vec)
            for n, r in enumerate((b_out, ffn_bias, bv1)):
                load(rows[:, n, :], r.partition_broadcast(128), ld_vec)
            load(gbrow[:, :], gate_b.partition_broadcast(128), ld_vec)
            for n, c in enumerate((ln_gamma, ln_beta, bq1, bk1, rms_scale)):
                eng.dma_start(cols[:, n, :], c.rearrange("(k p) -> p k", p=128),
                              allow_slow_non_contiguous=True).then_inc(ld_vec, 16)
            eng.wait_ge(s_gates, 2)
            for n, g in enumerate((5, 2, 1)):
                eng.tensor_scalar(rows[:, n, :], rows[:, n, :], gt[:, g:g + 1], None, ALU.mult)
            eng.tensor_scalar(cols[:, BQ, :], cols[:, BQ, :], scale_1, None, ALU.mult
                              ).then_inc(s_rows, 1)
            eng.wait_ge(s_rows, 1)

            def power(a, y, e_done):
                e_done.done(eng.tensor_tensor(y, a, consts[0:TQ, 0:1], ALU.pow))

            lh = [ln_h[:, n:n + 1] for n in range(24)]
            lt = [ln_t[:, n:n + 1] for n in range(24)]

            def ahead(nx, s):
                if s in AT_STATS:
                    n = AT_STATS.index(s)
                    e_mv_h.wait(eng, nx, n + 1)
                    power(lh[12 * n + 8], lh[12 * n + 9], e_rs_h)
                if s == AT_XN:
                    e_tl_dve.wait(eng, nx, 1, -2)
                    e_xb0.done(eng.tensor_tensor(xb0[:, nx.par, :], x_in[:, nx.par, :], rows[0:TQ, 0, :],
                                                 ALU.add))

            def body(st):
                tb = st.before()
                pt = Chain(eng, e_pt_ch)
                if st.load:
                    e_xn.wait(eng, st, 1, -1)
                    e_xb0.wait(eng, st, 1, -1)
                    load_x(st.after().index(), 1 - st.par)
                if st.tail:
                    e_mv_t.wait(eng, tb, 1)
                    power(lt[8], lt[9], e_rs_t)
                    e_xb.done(eng.tensor_tensor(xb1[:, :], x1[:, :], rows[0:TQ, 1, :], ALU.add))
                for s in range(SLOTS):
                    if s == SLOT[8] + 1 and st.load:
                        if st.tail:
                            e_tl.wait(eng, tb, 9)
                        else:
                            e_s.wait(eng, st, s)
                        load_ctx(st.after().index(), 1 - st.par)
                    if st.tail:
                        if s == SLOT[2]:
                            e_mv_t.wait(eng, tb, 2)
                            power(lt[8], lt[9], e_rs_t)
                            e_xb.done(eng.tensor_tensor(xb2[:, :], x2[:, :], rows[0:TQ, 2, :], ALU.add))
                        if s == SLOT[9]:
                            e_mv_t.wait(eng, tb, 3)
                            power(lt[8], lt[9], e_rs_t)
                        if s == SLOT[9] + 1:
                            e_mv_t.wait(eng, tb, 4)
                            power(lt[20], lt[21], e_rs_t)
                            e_n3.wait(eng, tb, 1)
                            e_tl_dve.wait(eng, tb, TL_READ[13][1], -1)
                            pt(eng.tensor_tensor(xm[:, :], n3[:, :],
                                                 gt[0:TQ, 3:4].broadcast_to([TQ, D]), ALU.mult))
                            pt.wait(tb)
                            e_xb.done(eng.tensor_tensor(xm[:, :], xm[:, :], x3[:, :], ALU.add))
                        if s == SLOT[10]:
                            at = bass.ds(tb.index() * TQ, TQ)
                            e_tl_act.wait(eng, tb, TL_READ[10][0])
                            pt(eng.tensor_copy(tT_hi[:, :, at], tf[:, :, :]))
                            pt.wait(tb)
                            e_tT.done(eng.tensor_tensor(tT_lo[:, :, at], tf[:, :, :],
                                                        tT_hi[:, :, at].bitcast(F32), ALU.subtract))
                        if s == SLOT[12]:
                            e_route.wait(eng, tb, 1)
                            e_route_c.done(eng.tensor_copy(
                                route[:, :, bass.ds(tb.index(), 1)].rearrange("t e b -> t (e b)"),
                                rk[:, 2, :]))
                    if st.load:
                        ahead(st.after(), s)
                assert pt.n in (0, e_pt_ch.per), pt.n

            for s in range(SLOTS):
                ahead(Step(None, 0, 0), s)
            pipeline(eng, body, B)

        @block.scalar
        def _(eng):
            eng.wait_ge(ld_vec, 16 * N_VEC)
            eng.activation(gt[:, 0:5], gates[:, :], ACT.Tanh).then_inc(s_gates, 1)
            eng.wait_ge(ld_wkv, 16)
            eng.activation(wkv_hi[:, :, :].rearrange("p k n -> p (k n)"),
                           acc[:, :, :].rearrange("p b d -> p (b d)"), ACT.Copy).then_inc(s_wkv, 1)
            eng.wait_ge(s_rows, 1)
            eng.wait_ge(s_zero, 2)

            def read_kv(step, n):
                assert ACT_READS[n]
                e_kv_pe.wait(eng, step, n + 1)
                return KV[n % 2]

            def key_hi(step, p):
                bank = read_kv(step, USE_K[p])
                e_kv_act.done(eng.activation(k_hi[:, p, :], bank[:, 0:SKE], ACT.Copy))

            def ahead(nx, s):
                if s in AT_CTX:
                    k = AT_CTX.index(s)
                    bank = read_kv(nx, USE_C + k)
                    e_kv_act.done(eng.activation(ctxT_hi[:, nx.par, k, 0:SK], bank[:, 0:SK],
                                                 ACT.Copy))
                if s == AT_X:
                    for k in range(KT):
                        bank = read_kv(nx, USE_X + k)
                        e_kv_act.done(eng.activation(xnT[:, k, :], bank[:, 0:TQ], ACT.Identity,
                                                     bias=cols[:, BETA, k:k + 1],
                                                     scale=cols[:, GAMMA, k:k + 1]))
                if s in AT_K:
                    key_hi(nx, AT_K.index(s))
                if s in AT_Q:
                    n = AT_Q.index(s)
                    bank = read_kv(nx, USE_Q[n])
                    pairs = slice(n * NP // 2, (n + 1) * NP // 2)
                    for half in range(2):
                        rows_ = slice(64 * half, 64 * half + 64)
                        last = eng.activation(
                            q_hi[rows_, pairs, half, :],
                            bank[rows_, 0:NP // 2 * TQ].rearrange("p (a t) -> p a t", t=TQ),
                            ACT.Copy, scale=scale_h)
                    e_kv_act.done(last)

            def body(st):
                tb = st.before()
                if st.heads:
                    for j in range(NKEY):
                        bank = read_kv(st, USE_V + 2 * j)
                        e_kv_act.done(eng.activation(v[0:KEYT, j, 0:512], bank[0:KEYT, :], ACT.Copy))
                if st.tail:
                    normed(tb, 1)
                for s in range(SLOTS + 1):
                    if s >= 1:
                        read(st, s - 1)
                    if st.heads and LAG_T <= s < NH + LAG_T:
                        h = s - LAG_T
                        e_pt_pe.wait(eng, st, h + 1)
                        e_o.wait(eng, st, h - 1)
                        e_pt.done(eng.activation(probT[:, h % 2, :, :].rearrange("p k t -> p (k t)"),
                                                 PT[h % 2][0:KEYT, 0:NKEY * TQ], ACT.Copy))
                    if st.heads and s < NH:
                        e_max.wait(eng, st, s + 1)
                        e_pt_pe.wait(eng, st, s - 1)
                        e_exp.done(eng.activation(prob[0:TQ, s % 2, :], S[s % 2][0:TQ, 0:SK], ACT.Exp,
                                                  bias=negmax[:, s:s + 1], accum_out=rowsum[:, s:s + 1]))
                    if st.tail:
                        if s == SLOT[6] + 1:
                            e_bias1.wait(eng, tb, 1)
                            e_tl_act.done(eng.activation(prob1[:, :], TL[0:TQ, 0:SK], ACT.Exp,
                                                         bias=sm1[:, 3:4], accum_out=sm1[:, 4:5]))
                        if s == SLOT[11] + 1:
                            e_gmax.wait(eng, tb, 1)
                            e_gexp.done(eng.activation(rk[:, 1, :], gl[:, :], ACT.Exp, bias=rs[:, 0:1]))

            def normed(tb, n):
                e_tl.wait(eng, tb, n + 1)
                e_tl_act.done(eng.activation(nT[:, :, :].rearrange("p k t -> p (k t)"),
                                             TL[:, 0:KT * TQ], ACT.Copy))

            def read(st, s):
                tb = st.before()
                if st.heads and s % 2 == 0 and s // 2 + 2 < NP:
                    key_hi(st, s // 2 + 2)
                if st.tail:
                    if s == SLOT[3]:
                        normed(tb, 3)
                    if s == SLOT[4]:
                        e_tl.wait(eng, tb, 5)
                        for k in range(KT):
                            last = eng.activation(q1T[:, k, :], TL[:, k * TQ:(k + 1) * TQ],
                                                  ACT.Identity, bias=cols[:, BQ, k:k + 1],
                                                  scale=scale_1)
                        e_tl_act.done(last)
                    if s == SLOT[5]:
                        e_tl.wait(eng, tb, 6)
                        e_tl_act.done(eng.activation(qk_hi[:, :, :].rearrange("p k t -> p (k t)"),
                                                     TL[:, 0:KT * TQ], ACT.Copy))
                    if s == SLOT[7]:
                        e_tl.wait(eng, tb, 8)
                        e_tl_act.done(eng.activation(prob1T[:, :, :].rearrange("p k t -> p (k t)"),
                                                     TL[0:KEYT, 0:NKEY * TQ], ACT.Copy))
                    if s == SLOT[10]:
                        e_tl.wait(eng, tb, 11)
                        e_tT.wait(eng, tb, 1, -1)
                        for k in range(KT):
                            last = eng.activation(tf[:, k, :], TL[:, k * TQ:(k + 1) * TQ],
                                                  ACT.Copy, scale=cols[:, RMS, k:k + 1])
                        e_tl_act.done(last)
                if st.load:
                    ahead(st.after(), s)

            for s in range(SLOTS):
                ahead(Step(None, 0, 0), s)
            pipeline(eng, body, B)

        @block.vector
        def _(eng):
            for q in qq:
                eng.memset(q[0:64, :, 1, :].bitcast(F32), 0.0)
                last = eng.memset(q[64:128, :, 0, :].bitcast(F32), 0.0)
            last.then_inc(s_zero_q, 1)
            eng.wait_ge(s_gates, 1)
            eng.tensor_tensor(gt[:, 5:6], gt[:, 0:1], gt[:, 4:5], ALU.mult).then_inc(s_gates, 1)
            eng.wait_ge(s_wkv, 1)
            eng.tensor_tensor(wkv_lo[:, :, :].rearrange("p k n -> p (k n)"),
                              acc[:, :, :].rearrange("p b d -> p (b d)"),
                              wkv_hi[:, :, :].bitcast(F32).rearrange("p k n -> p (k n)"),
                              ALU.subtract).then_inc(s_wkv_lo, 1)
            eng.wait_ge(s_su_pe, 1)
            eng.tensor_copy(wk1T[:, :, :].rearrange("p k n -> p (k n)"), KV[0][:, :])
            eng.tensor_copy(gwT[:, :, :].rearrange("p k n -> p (k n)"), KV[1][:, 0:KT * NE]
                            ).then_inc(s_su, 1)
            for n in range(2):
                eng.wait_ge(s_su_pe, 2 + n)
                eng.tensor_scalar(dft_ab[n].rearrange("p k n -> p (k n)"), S[n][:, :],
                                  1.0 / D, None, ALU.mult).then_inc(s_su, 1)
            eng.wait_ge(s_su_pe, 4)
            eng.tensor_copy(fmix[:, :, :].rearrange("p k n -> p (k n)"), PT[0][:, :]).then_inc(s_su, 1)

            eng.wait_ge(ld_vec, 16 * N_VEC)
            eng.wait_ge(s_zero, 2)

            def read_kv(step, n):
                assert DVE_READS[n]
                e_kv_pe.wait(eng, step, n + 1)
                if ACT_READS[n]:
                    e_kv_act.wait(eng, step, sum(ACT_READS[:n + 1]))
                return KV[n % 2]

            def key_lo(step, p):
                bank = read_kv(step, USE_K[p])
                e_kv_dve.done(eng.tensor_tensor(k_lo[:, p, :], bank[:, 0:SKE],
                                                k_hi[:, p, :].bitcast(F32), ALU.subtract))

            def value(step, j):
                bank = read_kv(step, USE_V + 2 * j + 1)
                e_kv_dve.done(eng.tensor_copy(v[0:KEYT, j, 512:1024], bank[0:KEYT, :]))

            def stats(chain, step, src, at, e_done, squares=False):
                chain(eng.bn_stats(at[:, 0:6], src))
                chain.wait(step)
                eng.memset(carrier[:, :], 0.0)
                chain(eng.bn_aggr(at[:, 6:8], at[:, 0:6]))
                chain.wait(step)
                var = at[:, 7:8]
                if squares:
                    var = at[:, 11:12]
                    chain(eng.scalar_tensor_tensor(var, at[:, 6:7], at[:, 6:7], at[:, 7:8], ALU.mult,
                                                   ALU.add))
                    chain.wait(step)
                e_done.done(eng.tensor_scalar(at[:, 8:9], var, EPS, None, ALU.add))

            def refine(chain, step, at):
                a, y, w = at[:, 8:9], at[:, 9:10], at[:, 10:11]
                chain(eng.scalar_tensor_tensor(w, y, y, a, ALU.mult, ALU.mult))
                chain.wait(step)
                chain(eng.tensor_scalar(w, w, -0.5, 1.5, ALU.mult, ALU.add))
                chain.wait(step)
                chain(eng.tensor_tensor(y, y, w, ALU.mult))
                chain.wait(step)

            def norm(dst, src, at):
                return eng.tensor_scalar(dst, src, at[:, 6:7], at[:, 9:10], ALU.subtract, ALU.mult)

            lh = [ln_h[:, 0:12], ln_h[:, 12:24]]
            lt = [ln_t[:, 0:12], ln_t[:, 12:24]]

            def ahead(nx, s, ch):
                if s == AT_STATS[0]:
                    e_x.wait(eng, nx, 1)
                    stats(ch, nx, x_in[:, nx.par, :], lh[0], e_mv_h)
                if s == AT_STATS[1]:
                    e_rs_h.wait(eng, nx, 1)
                    refine(ch, nx, lh[0])
                    ch(norm(n0[:, :], x_in[:, nx.par, :], lh[0]))
                    ch.wait(nx)
                    stats(ch, nx, n0[:, :], lh[1], e_mv_h)
                if s == AT_XN:
                    e_rs_h.wait(eng, nx, 2)
                    refine(ch, nx, lh[1])
                    e_xn.done(norm(xn[:, :], n0[:, :], lh[1]))
                if s in AT_CTX:
                    k = AT_CTX.index(s)
                    bank = read_kv(nx, USE_C + k)
                    e_kv_dve.done(eng.tensor_tensor(ctxT_lo[:, nx.par, k, 0:SK], bank[:, 0:SK],
                                                    ctxT_hi[:, nx.par, k, 0:SK].bitcast(F32),
                                                    ALU.subtract))
                if s in AT_K:
                    key_lo(nx, AT_K.index(s))
                if s in AT_Q:
                    n = AT_Q.index(s)
                    bank = read_kv(nx, USE_Q[n])
                    pairs = slice(n * NP // 2, (n + 1) * NP // 2)
                    for half in range(2):
                        rows_ = slice(64 * half, 64 * half + 64)
                        last = eng.scalar_tensor_tensor(
                            q_lo[rows_, pairs, half, :],
                            bank[rows_, 0:NP // 2 * TQ].rearrange("p (a t) -> p a t", t=TQ),
                            scale_h, q_hi[rows_, pairs, half, :].bitcast(F32),
                            ALU.mult, ALU.subtract)
                    e_kv_dve.done(last)

            def body(st):
                tb = st.before()
                ch, ct = Chain(eng, e_ch), Chain(eng, e_ct)
                if st.heads:
                    value(st, 0)
                if st.tail:
                    e_tl.wait(eng, tb, 1)
                    e_xb0.wait(eng, tb, 1)
                    e_xb.wait(eng, tb, 3, -1)
                    e_tl_dve.done(eng.scalar_tensor_tensor(x1[:, :], TL[0:TQ, 0:D], gt[0:TQ, 5:6],
                                                           xb0[:, tb.par, :], ALU.mult, ALU.add))
                    e_tl_dve.wait(eng, tb, 1)
                    stats(ct, tb, x1[:, :], lt[0], e_mv_t)
                if st.heads:
                    value(st, 1)
                if st.tail:
                    e_rs_t.wait(eng, tb, 1)
                    refine(ct, tb, lt[0])
                    e_n.done(norm(n1[:, :], x1[:, :], lt[0]))
                if st.heads:
                    value(st, 2)
                for s in range(SLOTS + 1):
                    if st.heads:
                        if s > LAG_O + 1 and (s - LAG_O) % 2 == 0:
                            p = (s - LAG_O) // 2 - 1
                            e_o.wait(eng, st, 2 * p + 2)
                            e_oT.done(eng.tensor_copy(oT[:, p, :], OT[:, 0:TQ]))
                        if 1 <= s <= NH:
                            e_exp.wait(eng, st, s)
                            e_rinv.done(eng.reciprocal(rinv[:, s - 1:s], rowsum[:, s - 1:s]))
                        if s < NH:
                            e_s.wait(eng, st, s + 1)
                            e_max.done(eng.tensor_reduce(negmax[:, s:s + 1], S[s % 2][0:TQ, 0:SK], AX.X,
                                                         ALU.max, negate=True))
                        if 1 <= s <= NH:
                            e_rinv.wait(eng, st, s)
                            e_prob.done(eng.tensor_scalar(prob[0:TQ, (s - 1) % 2, :],
                                                          prob[0:TQ, (s - 1) % 2, :],
                                                          rinv[:, s - 1:s], None, ALU.mult))
                    if s >= 1:
                        if st.heads and (s - 1) % 2 == 0 and (s - 1) // 2 + 2 < NP:
                            key_lo(st, (s - 1) // 2 + 2)
                        if st.tail:
                            tail(tb, s - 1, ct)
                        if st.load:
                            ahead(st.after(), s - 1, ch)
                        if st.tail:
                            router(tb, s - 1, ct)
                assert ch.n in (0, e_ch.per) and ct.n in (0, e_ct.per), (ch.n, ct.n)

            def router(tb, s, ct):
                if s == SLOT[11]:
                    e_tl.wait(eng, tb, 12)
                    e_tl_dve.done(eng.tensor_tensor(gl[:, :], TL[0:TQ, 0:NE], gbrow[0:TQ, :],
                                                    ALU.add))
                    e_tl_dve.wait(eng, tb, TL_READ[11][1])
                    e_gmax.done(eng.tensor_reduce(rs[:, 0:1], gl[:, :], AX.X, ALU.max, negate=True))
                    g_j = gl[:, :].unsqueeze(1).broadcast_to([TQ, NE, NE])
                    g_e = gl[:, :].unsqueeze(2).broadcast_to([TQ, NE, NE])
                    ct(eng.tensor_tensor(cmp_b[:, :, :], g_j, g_e, ALU.is_equal))
                    ct(eng.tensor_tensor(cmp_a[:, :, :], g_j, g_e, ALU.is_gt))
                if s == SLOT[11] + 1:
                    ct.wait(tb)
                    ct(eng.tensor_tensor(cmp_b[:, :, :], cmp_b[:, :, :], earlier[:, :, :], ALU.mult))
                    ct.wait(tb)
                    ct(eng.tensor_tensor(cmp_a[:, :, :], cmp_a[:, :, :], cmp_b[:, :, :], ALU.add))
                    ct.wait(tb)
                    ct(eng.tensor_reduce(rk[:, 0, :], cmp_a[:, :, :], AX.X, ALU.add))
                    ct.wait(tb)
                    e_gexp.wait(eng, tb, 1)
                    ct(eng.scalar_tensor_tensor(rk[:, 3, :], rk[:, 0, :], TOPK - 0.5, rk[:, 1, :],
                                                ALU.is_lt, ALU.mult, accum_out=rs[:, 1:2]))
                    ct.wait(tb)
                    ct(eng.reciprocal(rs[:, 2:3], rs[:, 1:2]))
                    ct.wait(tb)
                    e_route_c.wait(eng, tb, 1, -1)
                    e_route.done(eng.tensor_scalar(rk[:, 2, :], rk[:, 3, :], rs[:, 2:3],
                                                   gt[0:TQ, 3:4], ALU.mult, ALU.mult))

            def tail(tb, s, ct):
                if s == SLOT[2]:
                    e_tl.wait(eng, tb, 3)
                    e_xb.wait(eng, tb, 1)
                    e_tl_dve.done(eng.scalar_tensor_tensor(x2[:, :], TL[0:TQ, 0:D], gt[0:TQ, 2:3],
                                                           xb1[:, :], ALU.mult, ALU.add))
                    e_tl_dve.wait(eng, tb, TL_READ[2][1])
                    stats(ct, tb, x2[:, :], lt[0], e_mv_t)
                if s == SLOT[2] + 1:
                    e_rs_t.wait(eng, tb, 2)
                    refine(ct, tb, lt[0])
                    e_n.done(norm(n2[:, :], x2[:, :], lt[0]))
                if s == SLOT[5]:
                    e_tl.wait(eng, tb, 6)
                    e_tl_act.wait(eng, tb, TL_READ[5][0])
                    eng.tensor_copy(sm1[:, 0:1], TL[0:TQ, 256:257])
                    e_tl_dve.done(eng.tensor_tensor(
                        qk_lo[:, :, :].rearrange("p k t -> p (k t)"), TL[:, 0:KT * TQ],
                        qk_hi[:, :, :].bitcast(F32).rearrange("p k t -> p (k t)"), ALU.subtract))
                if s == SLOT[6]:
                    e_tl.wait(eng, tb, 7)
                    e_tl_dve.done(eng.tensor_reduce(sm1[:, 1:2], TL[0:TQ, 0:SK], AX.X, ALU.max))
                    e_tl_dve.wait(eng, tb, TL_READ[6][1])
                    ct(eng.tensor_tensor(sm1[:, 2:3], sm1[:, 1:2], sm1[:, 0:1], ALU.add))
                    ct.wait(tb)
                    e_bias1.done(eng.tensor_tensor(sm1[:, 3:4], sm1[:, 0:1], sm1[:, 2:3],
                                                   ALU.subtract))
                if s == SLOT[6] + 1:
                    e_tl_act.wait(eng, tb, TL_READ[6][0])
                    ct(eng.reciprocal(sm1[:, 5:6], sm1[:, 4:5]))
                    ct.wait(tb)
                    ct(eng.tensor_tensor(sm1[:, 6:7], sm1[:, 5:6], gt[0:TQ, 1:2], ALU.mult))
                if s == SLOT[8]:
                    e_tl.wait(eng, tb, 9)
                    e_tl_dve.done(eng.tensor_copy(cT[:, :, :].rearrange("p k t -> p (k t)"),
                                                  TL[:, 0:KT * TQ]))
                if s == SLOT[9]:
                    e_tl.wait(eng, tb, 10)
                    e_xb.wait(eng, tb, 2)
                    ct.wait(tb)
                    e_tl_dve.done(eng.scalar_tensor_tensor(x3[:, :], TL[0:TQ, 0:D], sm1[:, 6:7],
                                                           xb2[:, :], ALU.mult, ALU.add))
                    e_tl_dve.wait(eng, tb, TL_READ[9][1])
                    stats(ct, tb, x3[:, :], lt[0], e_mv_t)
                if s == SLOT[9] + 1:
                    e_rs_t.wait(eng, tb, 3)
                    refine(ct, tb, lt[0])
                    e_n3.done(norm(n3[:, :], x3[:, :], lt[0]))
                    e_n3.wait(eng, tb, 1)
                    stats(ct, tb, n3[:, :], lt[1], e_mv_t, squares=True)
                if s == SLOT[9] + 2:
                    e_rs_t.wait(eng, tb, 4)
                    refine(ct, tb, lt[1])
                    e_n.done(eng.tensor_scalar(tn[:, :], n3[:, :], lt[1][:, 9:10], None, ALU.mult))
                if s == SLOT[12]:
                    e_tl.wait(eng, tb, 13)
                    e_tl_dve.done(eng.tensor_copy(rT[:, :], TL[0:NE, 0:TQ]))
                if s == SLOT[13]:
                    e_tl.wait(eng, tb, 14)
                    e_xb.wait(eng, tb, 3)
                    e_tl_dve.done(eng.tensor_tensor(
                        acc[0:TQ, bass.ds(tb.index(), 1), :].rearrange("t b d -> t (b d)"),
                        TL[0:TQ, 0:D], xm[:, :], ALU.add))

            ch = Chain(eng, e_ch)
            for s in range(SLOTS):
                ahead(Step(None, 0, 0), s, ch)
            pipeline(eng, body, B)

        @block.tensor
        def _(eng):
            eng.wait_ge(s_ident, 2)
            eng.wait_ge(ld_stage, 16 * N_STAGE)
            for e in range(KT):
                for d in range(KT):
                    eng.transpose(KV[0][:, e * D + d * 128:e * D + (d + 1) * 128],
                                  stage[:, ST_WK + d, e * 128:(e + 1) * 128], ident[:, :])
            for k in range(KT):
                last = eng.transpose(KV[1][:, k * NE:(k + 1) * NE], gw_in[:, k * 128:(k + 1) * 128],
                                     ident[0:NE, 0:NE])
            last.then_inc(s_su_pe, 1)

            def square(bank, terms):
                for m in range(KT):
                    n = 0
                    for a, b in terms:
                        for k in range(KT):
                            n += 1
                            last = eng.matmul(bank[:, m * D:(m + 1) * D], a(k, m), b(k), start=(n == 1),
                                              stop=(n == KT * len(terms)))
                last.then_inc(s_su_pe, 1)

            def left(at):
                return lambda k, m: stage[:, at + k, m * 128:(m + 1) * 128]

            def right(at):
                return lambda k: stage[:, at + k, :]

            square(S[0], [(left(ST_RE), right(ST_COS)), (left(ST_IM), right(ST_SIN))])
            square(S[1], [(left(ST_IM), right(ST_COS)), (left(ST_RE), right(ST_NSIN))])
            eng.wait_ge(s_su, 3)
            square(PT[0], [(lambda k, m: dft_ab[0][:, k, m * 128:(m + 1) * 128], right(ST_COS)),
                           (lambda k, m: dft_ab[1][:, k, m * 128:(m + 1) * 128], right(ST_NSIN))])
            eng.wait_ge(s_su, 4)
            eng.wait_ge(s_wkv_lo, 1)
            eng.wait_ge(ld_w, 16 * N_W)
            eng.wait_ge(s_zero, 2)
            eng.wait_ge(s_zero_q, 1)
            eng.wait_ge(s_rows, 1)

            def split_product(out_, lhs, rhs):
                n = 0
                for i, j in PASSES:
                    for k in range(KT):
                        n += 1
                        last = eng.matmul(out_, lhs(i, k), rhs(j, k), start=(n == 1),
                                          stop=(n == KT * len(PASSES)))
                return last

            def key(step, p):
                n = USE_K[p]
                wait_kv_free(eng, step, n)
                e_kv_pe.done(split_product(
                    KV[n % 2][:, 0:SKE], lambda i, k: wkv[i][:, k, p * 128:(p + 1) * 128],
                    lambda j, k: ctxT[j][:, step.par, k, :]))

            def tail(tb, n):
                if n == 0:
                    e_oT.wait(eng, tb, NP)
                    e_tl_dve.wait(eng, tb, TL_READ[13][1], -1)
                else:
                    a, d = TL_READ[n - 1]
                    if n == 1 or TL_READ[n - 2][0] != a:
                        if a:
                            e_tl_act.wait(eng, tb, a)
                    if n == 1 or TL_READ[n - 2][1] != d:
                        e_tl_dve.wait(eng, tb, d)
                if n == 0:
                    for p in range(NP):
                        last = eng.matmul(TL[0:TQ, 0:D], oT[:, p, :], wo[:, p, :], start=(p == 0),
                                          stop=(p == NP - 1))
                if n in (1, 3, 10):
                    e_n.wait(eng, tb, {1: 1, 3: 2, 10: 3}[n])
                    src = {1: n1, 3: n2, 10: tn}[n]
                    for k in range(KT):
                        last = eng.transpose(TL[:, k * TQ:(k + 1) * TQ],
                                             src[:, k * 128:(k + 1) * 128], ident[0:TQ, 0:TQ])
                if n == 2:
                    for k in range(KT):
                        last = eng.matmul(TL[0:TQ, 0:D], nT[:, k, :], fmix[:, k, :], start=(k == 0),
                                          stop=(k == KT - 1))
                if n == 4:
                    for m in range(KT):
                        for k in range(KT):
                            last = eng.matmul(TL[:, m * TQ:(m + 1) * TQ],
                                              wq1[:, k, m * 128:(m + 1) * 128], nT[:, k, :],
                                              start=(k == 0), stop=(k == KT - 1))
                if n == 5:
                    for k in range(KT):
                        eng.matmul(TL[0:TQ, 256:257], q1T[:, k, :], cols[:, BK, k:k + 1],
                                   start=(k == 0), stop=(k == KT - 1))
                    for m in range(KT):
                        for k in range(KT):
                            last = eng.matmul(TL[:, m * TQ:(m + 1) * TQ],
                                              wk1T[:, k, m * 128:(m + 1) * 128], q1T[:, k, :],
                                              start=(k == 0), stop=(k == KT - 1))
                if n == 6:
                    last = split_product(TL[0:TQ, 0:SKE], lambda i, k: qk[i][:, k, :],
                                         lambda j, k: ctxT[j][:, tb.par, k, :])
                if n == 7:
                    for k in range(NKEY):
                        last = eng.transpose(TL[0:KEYT, k * TQ:(k + 1) * TQ],
                                             prob1[:, k * KEYT:(k + 1) * KEYT], ident[0:TQ, 0:TQ])
                if n == 8:
                    for m in range(KT):
                        for k in range(NKEY):
                            last = eng.matmul(TL[:, m * TQ:(m + 1) * TQ],
                                              ctx_in[0:KEYT, tb.par, k, m * 128:(m + 1) * 128],
                                              prob1T[:, k, :], start=(k == 0), stop=(k == NKEY - 1))
                if n == 9:
                    for k in range(KT):
                        last = eng.matmul(TL[0:TQ, 0:D], cT[:, k, :], wv1[:, k, :], start=(k == 0),
                                          stop=(k == KT - 1))
                if n == 11:
                    for k in range(KT):
                        last = eng.matmul(TL[0:TQ, 0:NE], tf[:, k, :], gwT[:, k, :], start=(k == 0),
                                          stop=(k == KT - 1))
                if n == 12:
                    e_route.wait(eng, tb, 1)
                    last = eng.transpose(TL[0:NE, 0:TQ], rk[:, 2, :], ident[0:TQ, 0:TQ])
                if n == 13:
                    last = eng.matmul(TL[0:TQ, 0:D], rT[:, :], b2[:, :], start=True, stop=True)
                e_tl.done(last)

            def ahead(nx, s):
                if s in AT_CTX:
                    k = AT_CTX.index(s)
                    if k == 0:
                        e_ctx.wait(eng, nx, 1)
                    wait_kv_free(eng, nx, USE_C + k)
                    for j in range(NKEY):
                        last = eng.transpose(KV[(USE_C + k) % 2][:, j * KEYT:(j + 1) * KEYT],
                                             ctx_in[0:KEYT, nx.par, j, k * 128:(k + 1) * 128],
                                             ident[0:KEYT, 0:KEYT])
                    e_kv_pe.done(last)
                if s == AT_X:
                    e_xn.wait(eng, nx, 1)
                    for k in range(KT):
                        wait_kv_free(eng, nx, USE_X + k)
                        e_kv_pe.done(eng.transpose(KV[(USE_X + k) % 2][:, 0:TQ], xn[:, k * 128:(k + 1) * 128],
                                                   ident[0:TQ, 0:TQ]))
                if s in AT_K:
                    if s == AT_K[0]:
                        e_kv_dve.wait(eng, nx, sum(DVE_READS[:USE_C + KT]))
                    key(nx, AT_K.index(s))
                if s in AT_Q:
                    n = AT_Q.index(s)
                    if n == 0:
                        e_kv_act.wait(eng, nx, sum(ACT_READS[:USE_X + KT]))
                    wait_kv_free(eng, nx, USE_Q[n])
                    for a in range(NP // 2):
                        p = n * NP // 2 + a
                        for k in range(KT):
                            last = eng.matmul(KV[USE_Q[n] % 2][:, a * TQ:(a + 1) * TQ],
                                              wq[:, k, p * 128:(p + 1) * 128], xnT[:, k, :],
                                              start=(k == 0), stop=(k == KT - 1))
                    e_kv_pe.done(last)

            def body(st):
                tb = st.before()
                for n in range(2 * NKEY):
                    j, half = n // 2, n % 2
                    if n == 2 and st.tail:
                        tail(tb, 0)
                    if not st.heads:
                        continue
                    wait_kv_free(eng, st, USE_V + n)
                    e_kv_pe.done(split_product(
                        KV[(USE_V + n) % 2][0:KEYT, :],
                        lambda i, k: ctxT[i][:, st.par, k, j * KEYT:(j + 1) * KEYT],
                        lambda jj, k: wkv[jj][:, k, INNER + half * 512:INNER + (half + 1) * 512]))
                if st.tail:
                    tail(tb, 1)
                for s in range(SLOTS):
                    if st.heads and s < NH:
                        p, half = s // 2, s % 2
                        if half == 0:
                            n = max(USE_Q[1], USE_K[p])
                            e_kv_dve.wait(eng, st, sum(DVE_READS[:n + 1]))
                        e_exp.wait(eng, st, *((s - 1, 0) if s >= 2 else (NH + s - 1, -1)))
                        for n, (i, j) in enumerate(PASSES):
                            last = eng.matmul(S[s % 2][0:TQ, 0:SKE], qq[i][:, p, half, :], kk[j][:, p, :],
                                              start=(n == 0), stop=(n == len(PASSES) - 1))
                        e_s.done(last)
                    if st.heads and LAG_T <= s < NH + LAG_T:
                        h = s - LAG_T
                        e_prob.wait(eng, st, h + 1)
                        e_pt.wait(eng, st, *((h - 1, 0) if h >= 2 else (NH + h - 1, -1)))
                        for k in range(NKEY):
                            last = eng.transpose(PT[h % 2][0:KEYT, k * TQ:(k + 1) * TQ],
                                                 prob[0:TQ, h % 2, k * KEYT:(k + 1) * KEYT],
                                                 ident[0:TQ, 0:TQ])
                        e_pt_pe.done(last)
                    if st.heads and LAG_O <= s < NH + LAG_O:
                        h = s - LAG_O
                        p, half = h // 2, h % 2
                        e_pt.wait(eng, st, h + 1)
                        if half == 0:
                            e_oT.wait(eng, st, p)
                        for k in range(NKEY):
                            last = eng.matmul(
                                OT[64 * half:64 * half + 64, 0:TQ],
                                v[0:KEYT, k, h * DH:(h + 1) * DH], probT[:, h % 2, k, :],
                                start=(k == 0), stop=(k == NKEY - 1))
                        e_o.done(last)
                    if st.heads and s % 2 == 0 and s // 2 + 2 < NP:
                        key(st, s // 2 + 2)
                    if st.load:
                        ahead(st.after(), s)
                    if st.tail and s in STAGE:
                        tail(tb, STAGE[s])

            for s in range(SLOTS):
                ahead(Step(None, 0, 0), s)
            pipeline(eng, body, B)


def phase2(nc, sb, event, sem, psum, ident, acc, tT_hi, tT_lo, route, mlp1_w, mlp1_b, mlp2_w, out):
    scope = ExitStack()
    with scope:
        def t(name, shape, dt=F32):
            return sb(name, shape, dt, scope)

        HT = HID // 128
        w1_in = t("w1_in", [128, HT, D])
        w2_in = t("w2_in", [128, KT, HID])
        w1_hi = t("w1_hi", [128, 2, KT, HID], F32R)
        w1_lo = t("w1_lo", [128, 2, KT, HID], F32R)
        w2_hi = t("w2_hi", [128, 2, HT, D], F32R)
        w2_lo = t("w2_lo", [128, 2, HT, D], F32R)
        b1_in = t("b1_in", [NE, 2 * HID])
        b1T = t("b1T", [128, NE, HT])
        b1c = t("b1c", [128, 2, HT])
        rc = t("rc", [TQ, 2, B])
        u = t("u", [128, 2, HT, CT])
        sg = t("sg", [128, 2, HT, CT])
        s_f = t("s_f", [128, 2, HT, CT])
        s_hi = t("s_hi", [128, 2, HT, CT], F32R)
        s_lo = t("s_lo", [128, 2, HT, CT], F32R)
        w1, w2, tt, ss = (w1_hi, w1_lo), (w2_hi, w2_lo), (tT_hi, tT_lo), (s_hi, s_lo)
        H = [[psum[0], psum[1]], [psum[2], psum[3]]]
        Y = [psum[4], psum[5]]
        WB = [psum[6], psum[7]]
        PASSES = ((0, 0), (0, 1), (1, 0))

        NCH = NC * HT
        f_w = event("f_w", 1, 32)
        f_b = sem("f_b")
        f_bT = sem("f_bT")
        f_wt = event("f_wt", 2)
        f_whi = event("f_whi", 2)
        f_wlo = event("f_wlo", 2)
        f_col = event("f_col", 1)
        f_h = event("f_h", NCH)
        f_u = event("f_u", NCH)
        f_sg = event("f_sg", NCH)
        f_s = event("f_s", NCH)
        f_shi = event("f_shi", NCH)
        f_slo = event("f_slo", NCH)
        f_y = event("f_y", B)
        f_acc = event("f_acc", B)
        f_out = sem("f_out")

        block = scope.enter_context(nc.Block())

        @block.sync
        def _(eng):
            eng.dma_start(b1_in[:, :], mlp1_b).then_inc(f_b, 16)
            for c in range(NC):
                eng.wait_ge(f_acc.handle, B * (NE - 1) + CB * (c + 1))
                eng.dma_start(out[c * CB:(c + 1) * CB, :, :].rearrange("b t d -> t b d"),
                              acc[0:TQ, c * CB:(c + 1) * CB, :]).then_inc(f_out, 16)
            eng.wait_ge(f_out, 16 * NC)

        @block.gpsimd
        def _(eng):
            def columns(st):
                f_acc.wait(eng, st, B, -2)
                b1_e = b1T[:, bass.ds(st.index(), 1), :].rearrange("p e m -> p (e m)")
                rc_e = route[:, bass.ds(st.index(), 1), :].rearrange("t e b -> t (e b)")
                eng.tensor_copy(b1c[:, st.par, :], b1_e)
                f_col.done(eng.tensor_copy(rc[:, st.par, :], rc_e))

            eng.wait_ge(f_bT, 2)
            columns(Step(None, 0, 0))

            def body(st):
                for c in range(NC):
                    if st.heads:
                        for m in range(HT):
                            n = c * HT + m
                            f_shi.wait(eng, st, n + 1)
                            f_y.wait(eng, st, CB * (c - 1))
                            f_slo.done(eng.tensor_tensor(s_lo[:, c % 2, m, :], s_f[:, c % 2, m, :],
                                                         s_hi[:, c % 2, m, :].bitcast(F32),
                                                         ALU.subtract))
                    if c == 1 and st.load:
                        columns(st.after())

            pipeline(eng, body, NE)

        @block.scalar
        def _(eng):
            def load(st):
                at = st.index()
                eng.dma_start(w1_in[:, :, :],
                              mlp1_w[bass.ds(at, 1), :, :].rearrange(
                                  "e (k p two) h -> two p (e k) h", two=2, p=128)[0]
                              ).then_inc(f_w.handle, 16)
                eng.dma_start(w2_in[:, :, :],
                              mlp2_w[bass.ds(at, 1), :, :].rearrange("e (k p) i -> p (e k) i", p=128)
                              ).then_inc(f_w.handle, 16)

            def high(st):
                for n, w in enumerate((w1_hi, w2_hi)):
                    f_wt.wait(eng, st, n + 1)
                    f_whi.done(eng.activation(w[:, st.par, :, :].rearrange("p k n -> p (k n)"),
                                              WB[n][:, :], ACT.Copy))

            load(Step(None, 0, 0))
            high(Step(None, 0, 0))

            def body(st):
                if st.load:
                    f_wt.wait(eng, st, 2)
                    load(st.after())
                for c in range(NC):
                    if not st.heads:
                        continue
                    for m in range(HT):
                        n = c * HT + m
                        f_u.wait(eng, st, n + 1)
                        f_sg.done(eng.activation(sg[:, c % 2, m, :], u[:, c % 2, m, :], ACT.Sigmoid,
                                                 scale=ALPHA))
                    for m in range(HT):
                        n = c * HT + m
                        f_s.wait(eng, st, n + 1)
                        f_y.wait(eng, st, CB * (c - 1))
                        f_shi.done(eng.activation(s_hi[:, c % 2, m, :], s_f[:, c % 2, m, :], ACT.Copy))
                    if c == 2 and st.load:
                        high(st.after())

            pipeline(eng, body, NE)

        @block.vector
        def _(eng):
            def low(st):
                for n, (w, hi) in enumerate(((w1_lo, w1_hi), (w2_lo, w2_hi))):
                    f_whi.wait(eng, st, n + 1)
                    f_wlo.done(eng.tensor_tensor(
                        w[:, st.par, :, :].rearrange("p k n -> p (k n)"), WB[n][:, :],
                        hi[:, st.par, :, :].bitcast(F32).rearrange("p k n -> p (k n)"), ALU.subtract))

            eng.wait_ge(f_bT, 1)
            for m in range(HT):
                last = eng.tensor_copy(b1T[:, :, m], Y[0][:, m * NE:(m + 1) * NE])
            last.then_inc(f_bT, 1)
            low(Step(None, 0, 0))

            def body(st):
                for c in range(NC):
                    if st.heads:
                        for m in range(HT):
                            n = c * HT + m
                            if n == 0:
                                f_col.wait(eng, st, 1)
                            f_h.wait(eng, st, n + 1)
                            f_sg.wait(eng, st, n + 1 - 2 * HT)
                            f_u.done(eng.tensor_scalar(u[:, c % 2, m, :], H[c % 2][m][:, 0:CT],
                                                       b1c[:, st.par, m:m + 1], LIMIT, ALU.add,
                                                       ALU.min))
                        for m in range(HT):
                            n = c * HT + m
                            f_sg.wait(eng, st, n + 1)
                            f_slo.wait(eng, st, n + 1 - 2 * HT)
                            f_s.done(eng.scalar_tensor_tensor(s_f[:, c % 2, m, :], u[:, c % 2, m, :],
                                                              LIMIT + 1.0, sg[:, c % 2, m, :],
                                                              ALU.mult, ALU.mult))
                    if c == 2 and st.load:
                        low(st.after())
                    add(st, c)

            def add(st, c):
                if c == 0:
                    if not st.tail:
                        return
                    own, cc = st.before(), NC - 1
                else:
                    if not st.heads:
                        return
                    own, cc = st, c - 1
                for b in range(CB):
                    batch = cc * CB + b
                    if b % 2 == 0:
                        f_y.wait(eng, own, batch + 2)
                    f_acc.wait(eng, own, batch + 1 - CB)
                    f_acc.done(eng.scalar_tensor_tensor(
                        acc[0:TQ, batch, :], Y[b // 2][0:TQ, (b % 2) * D:(b % 2 + 1) * D],
                        rc[:, own.par, batch:batch + 1], acc[0:TQ, batch, :], ALU.mult, ALU.add))

            pipeline(eng, body, NE)

        @block.tensor
        def _(eng):
            def weights(st):
                f_w.wait(eng, st, 1)
                f_wlo.wait(eng, st, 2, -1)
                for k in range(KT):
                    for m in range(HT):
                        last = eng.transpose(WB[0][:, k * HID + m * 128:k * HID + (m + 1) * 128],
                                             w1_in[:, m, k * 128:(k + 1) * 128], ident[:, :])
                f_wt.done(last)
                for m in range(HT):
                    for k in range(KT):
                        last = eng.transpose(WB[1][:, m * D + k * 128:m * D + (k + 1) * 128],
                                             w2_in[:, k, m * 128:(m + 1) * 128], ident[:, :])
                f_wt.done(last)

            eng.wait_ge(f_b, 16)
            for m in range(HT):
                last = eng.transpose(Y[0][:, m * NE:(m + 1) * NE],
                                     b1_in[:, m * D:(m + 1) * D].rearrange("e (i two) -> e two i",
                                                                          two=2)[:, 0, :],
                                     ident[0:NE, 0:NE])
            last.then_inc(f_bT, 1)
            weights(Step(None, 0, 0))
            eng.wait_ge(f_bT, 2)

            def output(st, c):
                if c == 0:
                    if not st.tail:
                        return
                    own, cc = st.before(), NC - 1
                else:
                    if not st.heads:
                        return
                    own, cc = st, c - 1
                f_slo.wait(eng, own, (cc + 1) * HT)
                for b in range(CB):
                    batch = cc * CB + b
                    if b % 2 == 0:
                        f_acc.wait(eng, own, batch - 2)
                    n = 0
                    for i, j in PASSES:
                        for m in range(HT):
                            n += 1
                            last = eng.matmul(Y[b // 2][0:TQ, (b % 2) * D:(b % 2 + 1) * D],
                                              ss[i][:, cc % 2, m, b * TQ:(b + 1) * TQ],
                                              w2[j][:, own.par, m, :], start=(n == 1),
                                              stop=(n == HT * len(PASSES)))
                    f_y.done(last)

            def body(st):
                for c in range(NC):
                    if st.heads:
                        for m in range(HT):
                            if c == 0 and m == 0:
                                f_wlo.wait(eng, st, 2)
                            f_u.wait(eng, st, c * HT + m + 1 - 2 * HT)
                            n = 0
                            for i, j in PASSES:
                                for k in range(KT):
                                    n += 1
                                    last = eng.matmul(H[c % 2][m][:, 0:CT],
                                                      w1[i][:, st.par, k, m * 128:(m + 1) * 128],
                                                      tt[j][:, k, c * CT:(c + 1) * CT],
                                                      start=(n == 1), stop=(n == KT * len(PASSES)))
                            f_h.done(last)
                    output(st, c)
                    if c == 1 and st.load:
                        weights(st.after())

            pipeline(eng, body, NE)


_INS = ["x", "ctx_1024", "g_xattn", "g_ffn", "L0_xattn_ln_gamma", "L0_xattn_ln_beta", "L0_xattn_w_q",
        "L0_xattn_w_kv", "L0_xattn_w_out", "L0_xattn_b_out", "L0_xattn_gate", "L0_ffn_w_freq_real",
        "L0_ffn_w_freq_imag", "L0_ffn_bias", "L1_xattn_Wq", "L1_xattn_bq", "L1_xattn_Wk",
        "L1_xattn_bk", "L1_xattn_Wv", "L1_xattn_bv", "L1_ffn_scale", "L1_ffn_gate_w",
        "L1_ffn_gate_b", "L1_ffn_mlp1_w", "L1_ffn_mlp1_b", "L1_ffn_mlp2_w", "L1_ffn_mlp2_b"]


def kernel(**inputs):
    import concourse.bacc as bacc
    from concourse.bass_utils import run_bass_kernel_spmd

    nc = bacc.Bacc("TRN2", target_bir_lowering=False, num_devices=1)
    arrays, args = {}, []

    def give(name, a):
        a = np.ascontiguousarray(a)
        arrays[name] = a
        args.append(nc.dram_tensor(name, a.shape, mybir.dt.from_np(a.dtype), kind="ExternalInput").ap())

    for name in _INS:
        give(f"in_{name}", inputs[name])
    jk = (np.arange(D)[:, None] * np.arange(D)[None, :]) % D
    angle = 2.0 * np.pi * jk / D
    give("dft", np.stack([np.cos(angle), np.sin(angle), -np.sin(angle)]).astype(np.float32))
    out = nc.dram_tensor("out_0", (B, TQ, D), F32, kind="ExternalOutput").ap()
    build(nc, *args, out)
    r = run_bass_kernel_spmd(nc, [arrays], core_ids=[0])
    return r.results[0]["out_0"]
```

```python
from contextlib import ExitStack

import numpy as np
import concourse.bass as bass
from concourse import mybir

F32 = mybir.dt.float32
F32R = mybir.dt.float32r
ALU = mybir.AluOpType
ACT = mybir.ActivationFunctionType
AX = mybir.AxisListType

B, TQ, D = 16, 112, 256
SK = 375
KT = D // 128
NH, DH = 16, 64
NP = NH // 2
INNER = NH * DH
KEYT, NKEY = 125, 3
SKE = SK + 1
NE, TOPK = 16, 4
HID = 256
CB = 4
NC = B // CB
HT = HID // 128
CT = CB * TQ
EPS = 1e-5
ALPHA, LIMIT = 1.702, 7.0


class Event:

    def __init__(self, handle, per, unit=1):
        self.handle, self.per, self.unit = handle, per, unit

    def wait(self, eng, step, k, shift=0):
        n = step.off + shift
        fixed = (self.per * n + k) * self.unit
        if step.reg is None:
            if fixed > 0:
                eng.wait_ge(self.handle, fixed)
        else:
            eng.wait_ge(self.handle, step.reg * (self.per * self.unit) + fixed)

    def done(self, ins):
        ins.then_inc(self.handle, self.unit)


class Step:

    def __init__(self, reg, off, par, heads=True, tail=True, load=True):
        self.reg, self.off, self.par = reg, off, par
        self.heads, self.tail, self.load = heads, tail, load

    def before(self):
        return Step(self.reg, self.off - 1, 1 - self.par)

    def after(self):
        return Step(self.reg, self.off + 1, 1 - self.par)

    def index(self):
        return self.off if self.reg is None else self.reg + self.off


def pipeline(eng, body, n):
    body(Step(None, 0, 0, tail=False))
    body(Step(None, 1, 1))
    with eng.Fori(2, n - 3, 2) as i:
        body(Step(i, 0, 0))
        body(Step(i, 1, 1))
    body(Step(None, n - 2, 0))
    body(Step(None, n - 1, 1, load=False))
    body(Step(None, n, 0, heads=False, load=False))


class Chain:

    def __init__(self, eng, event):
        self.eng, self.event, self.n = eng, event, 0

    def __call__(self, ins):
        self.event.done(ins)
        self.n += 1

    def wait(self, step):
        self.event.wait(self.eng, step, self.n)


def build(nc, x, ctx, g_xattn, g_ffn, ln_gamma, ln_beta, w_q, w_kv, w_out, b_out, gate, w_re, w_im,
          ffn_bias, Wq1, bq1, Wk1, bk1, Wv1, bv1, rms_scale, gate_w, gate_b, mlp1_w, mlp1_b, mlp2_w,
          mlp2_b, dft, out):
    top = ExitStack()
    with top:
        def sb(name, shape, dt=F32, scope=top):
            return scope.enter_context(nc.sbuf_tensor(name, shape, dt))

        def sem(name):
            return top.enter_context(nc.semaphore(name))

        def event(name, per, unit=1):
            return Event(sem(name), per, unit)

        ident = sb("ident", [128, 128])
        acc = sb("acc", [128, B, D])
        tT_hi = sb("tT_hi", [128, KT, B * TQ], F32R)
        tT_lo = sb("tT_lo", [128, KT, B * TQ], F32R)
        route = sb("route", [TQ, NE, B])

        b1T = sb("b1T", [128, NE, HT])
        w1_in = sb("w1_in", [128, HT, D])
        w2_in = sb("w2_in", [128, KT, HID])
        f_w = event("f_w", 1, 32)

        psum = [top.enter_context(nc.psum_tensor(f"bank{i}", [128, 512], F32)) for i in range(8)]

        def load_expert(eng, at):
            eng.dma_start(w1_in[:, :, :],
                          mlp1_w[bass.ds(at, 1), :, :].rearrange(
                              "e (k p two) h -> two p (e k) h", two=2, p=128)[0]
                          ).then_inc(f_w.handle, 16)
            eng.dma_start(w2_in[:, :, :],
                          mlp2_w[bass.ds(at, 1), :, :].rearrange("e (k p) i -> p (e k) i", p=128)
                          ).then_inc(f_w.handle, 16)

        phase1(nc, sb, event, sem, psum, ident, acc, tT_hi, tT_lo, route, x, ctx, g_xattn, g_ffn,
               ln_gamma, ln_beta, w_q, w_kv, w_out, b_out, gate, w_re, w_im, ffn_bias, Wq1, bq1, Wk1,
               bk1, Wv1, bv1, rms_scale, gate_w, gate_b, mlp2_b, dft, b1T, mlp1_b, load_expert)
        phase2(nc, sb, event, sem, psum, ident, acc, tT_hi, tT_lo, route, b1T, w1_in, w2_in, f_w,
               load_expert, out)


def phase1(nc, sb, event, sem, psum, ident, acc, tT_hi, tT_lo, route, x, ctx, g_xattn, g_ffn,
           ln_gamma, ln_beta, w_q, w_kv, w_out, b_out, gate, w_re, w_im, ffn_bias, Wq1, bq1, Wk1,
           bk1, Wv1, bv1, rms_scale, gate_w, gate_b, mlp2_b, dft, b1T, mlp1_b, load_expert):
    scope = ExitStack()
    with scope:
        def t(name, shape, dt=F32):
            return sb(name, shape, dt, scope)

        wq = t("wq", [128, KT, INNER])
        wkv_hi = t("wkv_hi", [128, KT, 2 * INNER], F32R)
        wkv_lo = t("wkv_lo", [128, KT, 2 * INNER], F32R)
        wo = t("wo", [128, NP, D])
        wqk = t("wqk", [128, KT, D])
        qbk = t("qbk", [128, KT])
        kbq = t("kbq", [128, KT])
        bqk = t("bqk", [128, 1])
        wv1 = t("wv1", [128, KT, D])
        fmix = t("fmix", [128, KT, D])
        gwT = t("gwT", [128, KT, NE])
        b2 = t("b2", [NE, D])
        cols = t("cols", [128, 5, KT])
        GAMMA, BETA, BQ, BK, RMS = range(5)
        rows = t("rows", [128, 3, D])
        gbrow = t("gbrow", [128, NE])
        gates = t("gates", [128, 5])
        gt = t("gt", [128, 6])
        minus_half = t("minus_half", [128, 1])
        carrier = t("carrier", [1, 1])
        earlier = t("earlier", [TQ, NE, NE])

        x_in = t("x_in", [TQ, 2, D])
        ctx_in = t("ctx_in", [128, 2, NKEY, D])
        ctxT_hi = t("ctxT_hi", [128, 2, KT, SKE], F32R)
        ctxT_lo = t("ctxT_lo", [128, 2, KT, SKE], F32R)
        n0 = t("n0", [TQ, D])
        xn = t("xn", [TQ, D])
        xnT = t("xnT", [128, KT, TQ])
        q_hi = t("q_hi", [128, NP, 2, TQ], F32R)
        q_lo = t("q_lo", [128, NP, 2, TQ], F32R)
        k_hi = t("k_hi", [128, NP, SKE], F32R)
        k_lo = t("k_lo", [128, NP, SKE], F32R)
        v = t("v", [128, NKEY, INNER])
        prob = t("prob", [128, 2, SK])
        probT = t("probT", [KEYT, 2, NKEY, TQ])
        negmax = t("negmax", [TQ, NH])
        rowsum = t("rowsum", [TQ, NH])
        rinv = t("rinv", [TQ, NH])
        oT = t("oT", [128, NP, TQ])
        ln_h = t("ln_h", [TQ, 24])
        ln_t = t("ln_t", [TQ, 24])
        xb0 = t("xb0", [TQ, 2, D])
        x1 = x2 = x3 = t("x123", [TQ, D])
        xb1 = xb2 = t("xb12", [TQ, D])
        n1 = n2 = tn = t("n12t", [TQ, D])
        n3 = t("n3", [TQ, D])
        xm = t("xm", [TQ, D])
        nT = t("nT", [128, KT, TQ])
        qk_hi = t("qk_hi", [128, KT, TQ], F32R)
        qk_lo = t("qk_lo", [128, KT, TQ], F32R)
        prob1 = t("prob1", [TQ, SK])
        prob1T = t("prob1T", [KEYT, NKEY, TQ])
        sm1 = t("sm1", [TQ, 8])
        cT = t("cT", [128, KT, TQ])
        tf = t("tf", [128, KT, TQ])
        gl = t("gl", [TQ, NE])
        cmp_a = t("cmp_a", [TQ, NE, NE])
        cmp_b = t("cmp_b", [TQ, NE, NE])
        rk = t("rk", [TQ, 4, NE])
        rs = t("rs", [TQ, 4])
        rT = t("rT", [NE, TQ])

        KV = [psum[0], psum[1]]
        S = [psum[2], psum[3]]
        PT = [psum[4], psum[5]]
        OT = psum[6]
        TL = psum[7]

        ld_wkv = [sem("ld_wk"), sem("ld_wv")]
        ld_wq, ld_w, ld_stage, ld_vec = sem("ld_wq"), sem("ld_w"), sem("ld_stage"), sem("ld_vec")
        s_ident = sem("s_ident")
        s_zero = sem("s_zero")
        s_zero_q = sem("s_zero_q")
        s_gates = sem("s_gates")
        s_rows = sem("s_rows")
        s_wkv = sem("s_wkv")
        s_wk_lo = sem("s_wk_lo")
        s_wv_lo = sem("s_wv_lo")
        s_su_pe = sem("s_su_pe")
        s_su = sem("s_su")

        e_x = event("e_x", 1, 16)
        e_ctx = event("e_ctx", 1, 16)
        e_kv_pe = event("e_kv_pe", 20)
        e_kv_act = event("e_kv_act", 17)
        e_kv_dve = event("e_kv_dve", 15)
        e_mv_h = event("e_mv_h", 2)
        e_rs_h = event("e_rs_h", 2)
        e_xn = event("e_xn", 1)
        e_s = event("e_s", NH)
        e_max = event("e_max", NH)
        e_exp = event("e_exp", NH)
        e_rinv = event("e_rinv", NH)
        e_prob = event("e_prob", NH)
        e_pt_pe = event("e_pt_pe", NH)
        e_pt = event("e_pt", NH)
        e_o = event("e_o", NH)
        e_oT = event("e_oT", NP)
        e_xb0 = event("e_xb0", 1)
        e_ch = event("e_ch", 11)
        e_tl = event("e_tl", 13)
        e_tl_act = event("e_tl_act", 6)
        e_tl_dve = event("e_tl_dve", 9)
        e_mv_t = event("e_mv_t", 4)
        e_rs_t = event("e_rs_t", 4)
        e_n = event("e_n", 3)
        e_n3 = event("e_n3", 1)
        e_xb = event("e_xb", 3)
        e_ct = event("e_ct", 31)
        e_bias1 = event("e_bias1", 1)
        e_r1 = event("e_r1", 1)
        e_gmax = event("e_gmax", 1)
        e_gexp = event("e_gexp", 1)
        e_tT = event("e_tT", 1)
        e_route = event("e_route", 1)
        e_route_c = event("e_route_c", 1)
        e_pt_ch = event("e_pt_ch", 2)

        scale_h = float(DH) ** -0.5
        scale_1 = float(D) ** -0.5
        PASSES = ((0, 0), (0, 1), (1, 0))
        ctxT = (ctxT_hi, ctxT_lo)
        wkv = (wkv_hi, wkv_lo)
        kk = (k_hi, k_lo)
        qq = (q_hi, q_lo)
        qk = (qk_hi, qk_lo)

        USES = ["x"] * KT + ["q"] + ["c"] * KT + ["k"] * 2 + ["q"] + ["v0", "v1"] * NKEY + ["k"] * (NP - 2)
        ACT_READS = [int(u != "v1") for u in USES]
        DVE_READS = [int(u not in ("v0", "x")) for u in USES]
        USE_X, USE_C, USE_V = USES.index("x"), USES.index("c"), USES.index("v0")
        USE_Q = [n for n, u in enumerate(USES) if u == "q"]
        USE_K = [n for n, u in enumerate(USES) if u == "k"]

        def wait_kv_free(eng, step, n):
            last, shift = (n - 2, 0) if n >= 2 else (n - 2 + len(USES), -1)
            if ACT_READS[last]:
                e_kv_act.wait(eng, step, sum(ACT_READS[:last + 1]), shift)
            if DVE_READS[last]:
                e_kv_dve.wait(eng, step, sum(DVE_READS[:last + 1]), shift)

        TL_READ = {0: (0, 1), 1: (1, 1), 2: (1, 2), 3: (2, 2), 4: (3, 3), 5: (4, 4), 6: (5, 4),
                   7: (5, 5), 8: (5, 6), 9: (6, 6), 10: (6, 7), 11: (6, 8), 12: (6, 9)}
        SLOT = {1: -1, 2: 0, 3: 3, 4: 4, 5: 6, 6: 8, 7: 9, 8: 10, 9: 13, 10: 14, 11: 17, 12: 18}
        STAGE = {s: n for n, s in SLOT.items()}
        SLOTS = NH + 3
        AT_STATS, AT_XN, AT_X, AT_CTX, AT_K, AT_Q = (7, 8), 9, 11, (13, 14), (15, 16), (12, 17)
        OWN_K = (1, 2, 4, 6, 8, 10)
        LAG_T, LAG_O = 2, 3

        w_kv_in = acc[:, :, :].rearrange("p b d -> p (b d)").rearrange("p (k n) -> p k n", k=KT)
        stage = acc
        b1_in = (n3[0:NE, :], xm[0:NE, :])
        gw_in = cmp_a[0:NE, :, :].rearrange("p a b -> p (a b)")
        ST_WK, ST_RE, ST_IM, ST_COS, ST_SIN, ST_NSIN, ST_A, ST_B = range(0, 8 * KT, KT)
        SETUP = (6, 7, 8, 9, 10, 12, 14)
        AT_GW = 3 * KT
        AT_B1 = AT_GW + KT * NE

        def w_kv_part(a, n):
            return a[:, :, n * INNER:(n + 1) * INNER]

        block = scope.enter_context(nc.Block())

        @block.sync
        def _(eng):
            def load(dst, src, s):
                eng.dma_start(dst, src).then_inc(s, 16)

            def wide(a):
                return a.rearrange("(k p) n -> p k n", p=128)

            for n, g in enumerate((g_xattn, g_ffn)):
                load(gates[:, 2 * n:2 * n + 2], g.partition_broadcast(128), ld_vec)
            load(gates[:, 4:5], gate.partition_broadcast(128), ld_vec)
            for n, c in enumerate((ln_gamma, ln_beta, bq1, bk1, rms_scale)):
                eng.dma_start(cols[:, n, :], c.rearrange("(k p) -> p k", p=128),
                              allow_slow_non_contiguous=True).then_inc(ld_vec, 16)
            for n, r in enumerate((b_out, ffn_bias, bv1)):
                load(rows[:, n, :], r.partition_broadcast(128), ld_vec)
            load(gbrow[:, :], gate_b.partition_broadcast(128), ld_vec)
            for n in range(2):
                load(w_kv_part(w_kv_in, n), w_kv_part(wide(w_kv), n), ld_wkv[n])
            load(gw_in, gate_w, ld_stage)
            for m in range(HT):
                load(b1_in[m], mlp1_b[:, m * 256:(m + 1) * 256], ld_stage)
            eng.wait_ge(s_wk_lo, 1)
            eng.wait_ge(s_wv_lo, 1)
            load(stage[:, ST_WK:ST_WK + KT, :], wide(Wk1), ld_stage)
            load(stage[:, ST_A:ST_A + KT, :], wide(Wq1), ld_stage)
            load(stage[:, ST_RE:ST_RE + KT, :], wide(w_re), ld_stage)
            load(stage[:, ST_IM:ST_IM + KT, :], wide(w_im), ld_stage)
            for n, at in enumerate((ST_COS, ST_SIN, ST_NSIN)):
                load(stage[:, at:at + KT, :], wide(dft[n]), ld_stage)
            load(wo[:, :, :], wide(w_out), ld_w)
            load(wv1[:, :, :], wide(Wv1), ld_w)
            load(b2[:, :], mlp2_b, ld_w)
            load_expert(eng, 0)

        N_STAGE, N_W, N_VEC = 8 + HT, 3, 12

        @block.gpsimd
        def _(eng):
            def load_x(b, par):
                eng.dma_start(x_in[:, par, :], x[bass.ds(b, 1), :, :].rearrange("b t d -> t (b d)")
                              ).then_inc(e_x.handle, 16)

            def load_ctx(b, par):
                eng.dma_start(ctx_in[0:KEYT, par, :, :],
                              ctx[bass.ds(b, 1), :, :].rearrange("b (k t) d -> t (b k) d", t=KEYT)
                              ).then_inc(e_ctx.handle, 16)

            load_x(0, 0)
            load_ctx(0, 0)
            eng.memset(minus_half[:, :], -0.5)
            eng.memset(ident[:, :], 0.0).then_inc(s_ident, 1)
            eng.memset(earlier[:, :, :], 1.0).then_inc(s_zero, 1)
            eng.wait_ge(s_ident, 1)
            eng.affine_select(out=ident[:, :], in_=ident[:, :], compare_op=ALU.not_equal, fill=1.0,
                              base=0, pattern=[[-1, 128]], channel_multiplier=1).then_inc(s_ident, 1)
            eng.wait_ge(s_zero, 1)
            eng.affine_select(out=earlier[:, :, :], in_=earlier[:, :, :], compare_op=ALU.is_gt, fill=0.0,
                              base=0, pattern=[[1, NE], [-1, NE]], channel_multiplier=0)
            for par in range(2):
                for k in range(KT):
                    for c in ctxT:
                        last = eng.memset(c[:, par, k, SK:SKE].bitcast(F32), 0.0)
            last.then_inc(s_zero, 1)

            def power(a, y, e_done):
                e_done.done(eng.tensor_tensor(y, a, minus_half[0:TQ, :], ALU.pow))

            lh = [ln_h[:, n:n + 1] for n in range(24)]
            lt = [ln_t[:, n:n + 1] for n in range(24)]

            def ahead(nx, s):
                if s in AT_STATS:
                    n = AT_STATS.index(s)
                    e_mv_h.wait(eng, nx, n + 1)
                    power(lh[12 * n + 8], lh[12 * n + 9], e_rs_h)
                if s == AT_XN:
                    e_tl_dve.wait(eng, nx, 1, -2)
                    e_xb0.done(eng.tensor_tensor(xb0[:, nx.par, :], x_in[:, nx.par, :], rows[0:TQ, 0, :],
                                                 ALU.add))

            def body(st):
                tb = st.before()
                pt = Chain(eng, e_pt_ch)
                if st.load:
                    e_xn.wait(eng, st, 1, -1)
                    e_xb0.wait(eng, st, 1, -1)
                    load_x(st.after().index(), 1 - st.par)
                if st.tail:
                    e_mv_t.wait(eng, tb, 1)
                    power(lt[8], lt[9], e_rs_t)
                    e_xb.done(eng.tensor_tensor(xb1[:, :], x1[:, :], rows[0:TQ, 1, :], ALU.add))
                for s in range(SLOTS):
                    if s == SLOT[7] + 1 and st.load:
                        if st.tail:
                            e_tl.wait(eng, tb, 8)
                        else:
                            e_s.wait(eng, st, s)
                        load_ctx(st.after().index(), 1 - st.par)
                    if st.tail:
                        if s == SLOT[2]:
                            e_mv_t.wait(eng, tb, 2)
                            power(lt[8], lt[9], e_rs_t)
                            e_xb.done(eng.tensor_tensor(xb2[:, :], x2[:, :], rows[0:TQ, 2, :], ALU.add))
                        if s == SLOT[8]:
                            e_mv_t.wait(eng, tb, 3)
                            power(lt[8], lt[9], e_rs_t)
                        if s == SLOT[8] + 1:
                            e_mv_t.wait(eng, tb, 4)
                            power(lt[20], lt[21], e_rs_t)
                            e_n3.wait(eng, tb, 1)
                            e_tl_dve.wait(eng, tb, TL_READ[12][1], -1)
                            pt(eng.tensor_tensor(xm[:, :], n3[:, :],
                                                 gt[0:TQ, 3:4].broadcast_to([TQ, D]), ALU.mult))
                            pt.wait(tb)
                            e_xb.done(eng.tensor_tensor(xm[:, :], xm[:, :], x3[:, :], ALU.add))
                        if s == SLOT[9]:
                            at = bass.ds(tb.index() * TQ, TQ)
                            e_tl_act.wait(eng, tb, TL_READ[9][0])
                            pt(eng.tensor_copy(tT_hi[:, :, at], tf[:, :, :]))
                            pt.wait(tb)
                            e_tT.done(eng.tensor_tensor(tT_lo[:, :, at], tf[:, :, :],
                                                        tT_hi[:, :, at].bitcast(F32), ALU.subtract))
                        if s == SLOT[11]:
                            e_route.wait(eng, tb, 1)
                            e_route_c.done(eng.tensor_copy(
                                route[:, :, bass.ds(tb.index(), 1)].rearrange("t e b -> t (e b)"),
                                rk[:, 2, :]))
                    if st.load:
                        ahead(st.after(), s)
                assert pt.n in (0, e_pt_ch.per), pt.n

            for s in range(SLOTS):
                if s == AT_XN:
                    eng.wait_ge(s_gates, 2)
                    for n, g in enumerate((5, 2, 1)):
                        eng.tensor_scalar(rows[:, n, :], rows[:, n, :], gt[:, g:g + 1], None, ALU.mult)
                    eng.tensor_scalar(cols[:, BQ, :], cols[:, BQ, :], scale_1, None, ALU.mult
                                      ).then_inc(s_rows, 1)
                    eng.wait_ge(s_rows, 1)
                ahead(Step(None, 0, 0), s)
            eng.wait_ge(s_wkv, 2)
            eng.tensor_tensor(w_kv_part(wkv_lo, 1), w_kv_part(w_kv_in, 1),
                              w_kv_part(wkv_hi, 1).bitcast(F32), ALU.subtract).then_inc(s_wv_lo, 1)
            pipeline(eng, body, B)

        @block.scalar
        def _(eng):
            eng.dma_start(wq[:, :, :], w_q.rearrange("(k p) n -> p k n", p=128)).then_inc(ld_wq, 16)
            eng.wait_ge(ld_vec, 16 * N_VEC)
            eng.activation(gt[:, 0:5], gates[:, :], ACT.Tanh).then_inc(s_gates, 1)

            def split(n):
                eng.wait_ge(ld_wkv[n], 16)
                eng.activation(w_kv_part(wkv_hi, n), w_kv_part(w_kv_in, n), ACT.Copy).then_inc(s_wkv, 1)

            def read_kv(step, n):
                assert ACT_READS[n]
                e_kv_pe.wait(eng, step, n + 1)
                return KV[n % 2]

            def key_hi(step, p):
                bank = read_kv(step, USE_K[p])
                e_kv_act.done(eng.activation(k_hi[:, p, :], bank[:, 0:SKE], ACT.Copy))

            def ahead(nx, s):
                if s in AT_CTX:
                    k = AT_CTX.index(s)
                    bank = read_kv(nx, USE_C + k)
                    e_kv_act.done(eng.activation(ctxT_hi[:, nx.par, k, 0:SK], bank[:, 0:SK],
                                                 ACT.Copy))
                if s == AT_X:
                    for k in range(KT):
                        bank = read_kv(nx, USE_X + k)
                        e_kv_act.done(eng.activation(xnT[:, k, :], bank[:, 0:TQ], ACT.Identity,
                                                     bias=cols[:, BETA, k:k + 1],
                                                     scale=cols[:, GAMMA, k:k + 1]))
                if s in AT_K:
                    key_hi(nx, AT_K.index(s))
                if s in AT_Q:
                    n = AT_Q.index(s)
                    bank = read_kv(nx, USE_Q[n])
                    pairs = slice(n * NP // 2, (n + 1) * NP // 2)
                    for half in range(2):
                        rows_ = slice(64 * half, 64 * half + 64)
                        last = eng.activation(
                            q_hi[rows_, pairs, half, :],
                            bank[rows_, 0:NP // 2 * TQ].rearrange("p (a t) -> p a t", t=TQ),
                            ACT.Copy, scale=scale_h)
                    e_kv_act.done(last)

            def body(st):
                tb = st.before()
                if st.heads:
                    for j in range(NKEY):
                        bank = read_kv(st, USE_V + 2 * j)
                        e_kv_act.done(eng.activation(v[0:KEYT, j, 0:512], bank[0:KEYT, :], ACT.Copy))
                if st.tail:
                    normed(tb, 1)
                for s in range(SLOTS + 1):
                    if st.heads and s > LAG_O + 1 and (s - LAG_O) % 2 == 0:
                        p = (s - LAG_O) // 2 - 1
                        e_o.wait(eng, st, 2 * p + 2)
                        e_oT.done(eng.activation(oT[:, p, :], OT[:, 0:TQ], ACT.Copy))
                    if s >= 1:
                        read(st, s - 1)
                    if st.heads and LAG_T <= s < NH + LAG_T:
                        h = s - LAG_T
                        e_pt_pe.wait(eng, st, h + 1)
                        e_o.wait(eng, st, h - 1)
                        e_pt.done(eng.activation(probT[:, h % 2, :, :].rearrange("p k t -> p (k t)"),
                                                 PT[h % 2][0:KEYT, 0:NKEY * TQ], ACT.Copy))
                    if st.heads and s < NH:
                        e_max.wait(eng, st, s + 1)
                        e_pt_pe.wait(eng, st, s - 1)
                        e_exp.done(eng.activation(prob[0:TQ, s % 2, :], S[s % 2][0:TQ, 0:SK], ACT.Exp,
                                                  bias=negmax[:, s:s + 1], accum_out=rowsum[:, s:s + 1]))
                    if st.tail:
                        if s == SLOT[5] + 1:
                            e_bias1.wait(eng, tb, 1)
                            e_tl_act.done(eng.activation(prob1[:, :], TL[0:TQ, 0:SK], ACT.Exp,
                                                         bias=sm1[:, 3:4], accum_out=sm1[:, 4:5]))
                        if s == SLOT[10] + 1:
                            e_gmax.wait(eng, tb, 1)
                            e_gexp.done(eng.activation(rk[:, 1, :], gl[:, :], ACT.Exp, bias=rs[:, 0:1]))

            def normed(tb, n):
                e_tl.wait(eng, tb, n + 1)
                e_tl_act.done(eng.activation(nT[:, :, :].rearrange("p k t -> p (k t)"),
                                             TL[:, 0:KT * TQ], ACT.Copy))

            def read(st, s):
                tb = st.before()
                if st.heads and s in OWN_K:
                    key_hi(st, 2 + OWN_K.index(s))
                if st.tail:
                    if s == SLOT[3]:
                        normed(tb, 3)
                    if s == SLOT[4]:
                        e_tl.wait(eng, tb, 5)
                        for k in range(KT):
                            last = eng.activation(qk_hi[:, k, :], TL[:, k * TQ:(k + 1) * TQ],
                                                  ACT.Identity, bias=kbq[:, k:k + 1])
                        e_tl_act.done(last)
                    if s == SLOT[6]:
                        e_tl.wait(eng, tb, 7)
                        e_tl_act.done(eng.activation(prob1T[:, :, :].rearrange("p k t -> p (k t)"),
                                                     TL[0:KEYT, 0:NKEY * TQ], ACT.Copy))
                    if s == SLOT[9]:
                        e_tl.wait(eng, tb, 10)
                        e_tT.wait(eng, tb, 1, -1)
                        for k in range(KT):
                            last = eng.activation(tf[:, k, :], TL[:, k * TQ:(k + 1) * TQ],
                                                  ACT.Copy, scale=cols[:, RMS, k:k + 1])
                        e_tl_act.done(last)
                if st.load:
                    ahead(st.after(), s)

            for s in range(SLOTS):
                if s == AT_K[0]:
                    split(0)
                ahead(Step(None, 0, 0), s)
                if s == AT_K[0]:
                    split(1)
            eng.wait_ge(s_rows, 1)
            pipeline(eng, body, B)

        @block.vector
        def _(eng):
            for q in qq:
                eng.memset(q[0:64, :, 1, :].bitcast(F32), 0.0)
                last = eng.memset(q[64:128, :, 0, :].bitcast(F32), 0.0)
            last.then_inc(s_zero_q, 1)

            def setup(n):
                eng.wait_ge(s_su_pe, n + 1)
                at = {0: ST_WK, 1: ST_A, 4: ST_A, 5: ST_B}.get(n)
                if n in (0, 1):
                    ins = eng.tensor_copy(stage[:, at:at + KT, :].rearrange("p k n -> p (k n)"), TL[:, :])
                if n == 2:
                    eng.tensor_copy(nT[:, :, :], cols[:, BQ, :].unsqueeze(2).broadcast_to([128, KT, TQ]))
                    ins = eng.tensor_scalar(wqk[:, :, :].rearrange("p k n -> p (k n)"), TL[:, :],
                                            scale_1, None, ALU.mult)
                if n == 3:
                    eng.tensor_scalar(qbk[:, :], TL[:, 0:KT], scale_1, None, ALU.mult)
                    eng.tensor_copy(kbq[:, :], TL[:, KT:2 * KT])
                    for m in range(HT):
                        eng.tensor_copy(b1T[:, :, m], TL[:, AT_B1 + m * NE:AT_B1 + (m + 1) * NE])
                    eng.tensor_copy(bqk[0:TQ, :], TL[0:TQ, 2 * KT:2 * KT + 1])
                    ins = eng.tensor_copy(gwT[:, :, :].rearrange("p k n -> p (k n)"),
                                          TL[:, AT_GW:AT_GW + KT * NE])
                if n in (4, 5):
                    ins = eng.tensor_scalar(stage[:, at:at + KT, :].rearrange("p k n -> p (k n)"),
                                            TL[:, :], 1.0 / D, None, ALU.mult)
                if n == 6:
                    ins = eng.tensor_copy(fmix[:, :, :].rearrange("p k n -> p (k n)"), TL[:, :])
                ins.then_inc(s_su, 1)

            def read_kv(step, n):
                assert DVE_READS[n]
                e_kv_pe.wait(eng, step, n + 1)
                if ACT_READS[n]:
                    e_kv_act.wait(eng, step, sum(ACT_READS[:n + 1]))
                return KV[n % 2]

            def key_lo(step, p):
                bank = read_kv(step, USE_K[p])
                e_kv_dve.done(eng.tensor_tensor(k_lo[:, p, :], bank[:, 0:SKE],
                                                k_hi[:, p, :].bitcast(F32), ALU.subtract))

            def value(step, j):
                bank = read_kv(step, USE_V + 2 * j + 1)
                e_kv_dve.done(eng.tensor_copy(v[0:KEYT, j, 512:1024], bank[0:KEYT, :]))

            def stats(chain, step, src, at, e_done, squares=False):
                chain(eng.bn_stats(at[:, 0:6], src))
                chain.wait(step)
                eng.memset(carrier[:, :], 0.0)
                chain(eng.bn_aggr(at[:, 6:8], at[:, 0:6]))
                chain.wait(step)
                var = at[:, 7:8]
                if squares:
                    var = at[:, 11:12]
                    chain(eng.scalar_tensor_tensor(var, at[:, 6:7], at[:, 6:7], at[:, 7:8], ALU.mult,
                                                   ALU.add))
                    chain.wait(step)
                e_done.done(eng.tensor_scalar(at[:, 8:9], var, EPS, None, ALU.add))

            def refine(chain, step, at):
                a, y, w = at[:, 8:9], at[:, 9:10], at[:, 10:11]
                chain(eng.scalar_tensor_tensor(w, y, y, a, ALU.mult, ALU.mult))
                chain.wait(step)
                chain(eng.tensor_scalar(w, w, -0.5, 1.5, ALU.mult, ALU.add))
                chain.wait(step)
                chain(eng.tensor_tensor(y, y, w, ALU.mult))
                chain.wait(step)

            def norm(dst, src, at):
                return eng.tensor_scalar(dst, src, at[:, 6:7], at[:, 9:10], ALU.subtract, ALU.mult)

            lh = [ln_h[:, 0:12], ln_h[:, 12:24]]
            lt = [ln_t[:, 0:12], ln_t[:, 12:24]]

            def ahead(nx, s, ch):
                if s == AT_STATS[0]:
                    e_x.wait(eng, nx, 1)
                    stats(ch, nx, x_in[:, nx.par, :], lh[0], e_mv_h)
                if s == AT_STATS[1]:
                    e_rs_h.wait(eng, nx, 1)
                    refine(ch, nx, lh[0])
                    ch(norm(n0[:, :], x_in[:, nx.par, :], lh[0]))
                    ch.wait(nx)
                    stats(ch, nx, n0[:, :], lh[1], e_mv_h)
                if s == AT_XN:
                    e_rs_h.wait(eng, nx, 2)
                    refine(ch, nx, lh[1])
                    e_xn.done(norm(xn[:, :], n0[:, :], lh[1]))
                if s in AT_CTX:
                    k = AT_CTX.index(s)
                    bank = read_kv(nx, USE_C + k)
                    e_kv_dve.done(eng.tensor_tensor(ctxT_lo[:, nx.par, k, 0:SK], bank[:, 0:SK],
                                                    ctxT_hi[:, nx.par, k, 0:SK].bitcast(F32),
                                                    ALU.subtract))
                if s in AT_K:
                    key_lo(nx, AT_K.index(s))
                if s in AT_Q:
                    n = AT_Q.index(s)
                    bank = read_kv(nx, USE_Q[n])
                    pairs = slice(n * NP // 2, (n + 1) * NP // 2)
                    for half in range(2):
                        rows_ = slice(64 * half, 64 * half + 64)
                        last = eng.scalar_tensor_tensor(
                            q_lo[rows_, pairs, half, :],
                            bank[rows_, 0:NP // 2 * TQ].rearrange("p (a t) -> p a t", t=TQ),
                            scale_h, q_hi[rows_, pairs, half, :].bitcast(F32),
                            ALU.mult, ALU.subtract)
                    e_kv_dve.done(last)

            def body(st):
                tb = st.before()
                ch, ct = Chain(eng, e_ch), Chain(eng, e_ct)
                if st.heads:
                    value(st, 0)
                if st.tail:
                    e_tl.wait(eng, tb, 1)
                    e_xb0.wait(eng, tb, 1)
                    e_xb.wait(eng, tb, 3, -1)
                    e_tl_dve.done(eng.scalar_tensor_tensor(x1[:, :], TL[0:TQ, 0:D], gt[0:TQ, 5:6],
                                                           xb0[:, tb.par, :], ALU.mult, ALU.add))
                    e_tl_dve.wait(eng, tb, 1)
                    stats(ct, tb, x1[:, :], lt[0], e_mv_t)
                if st.heads:
                    value(st, 1)
                if st.tail:
                    e_rs_t.wait(eng, tb, 1)
                    refine(ct, tb, lt[0])
                    e_n.done(norm(n1[:, :], x1[:, :], lt[0]))
                if st.heads:
                    value(st, 2)
                for s in range(SLOTS + 1):
                    if st.heads:
                        if 1 <= s <= NH:
                            e_exp.wait(eng, st, s)
                            e_rinv.done(eng.reciprocal(rinv[:, s - 1:s], rowsum[:, s - 1:s]))
                        if s < NH:
                            e_s.wait(eng, st, s + 1)
                            e_max.done(eng.tensor_reduce(negmax[:, s:s + 1], S[s % 2][0:TQ, 0:SK], AX.X,
                                                         ALU.max, negate=True))
                        if 1 <= s <= NH:
                            e_rinv.wait(eng, st, s)
                            e_prob.done(eng.tensor_scalar(prob[0:TQ, (s - 1) % 2, :],
                                                          prob[0:TQ, (s - 1) % 2, :],
                                                          rinv[:, s - 1:s], None, ALU.mult))
                    if s >= 1:
                        if st.heads and s - 1 in OWN_K:
                            key_lo(st, 2 + OWN_K.index(s - 1))
                        if st.tail:
                            tail(tb, s - 1, ct)
                        if st.load:
                            ahead(st.after(), s - 1, ch)
                        if st.tail:
                            router(tb, s - 1, ct)
                        elif s - 1 in SETUP:
                            setup(SETUP.index(s - 1))
                assert ch.n in (0, e_ch.per) and ct.n in (0, e_ct.per), (ch.n, ct.n)

            def router(tb, s, ct):
                if s == SLOT[10]:
                    e_tl.wait(eng, tb, 11)
                    e_tl_dve.done(eng.tensor_tensor(gl[:, :], TL[0:TQ, 0:NE], gbrow[0:TQ, :],
                                                    ALU.add))
                    e_tl_dve.wait(eng, tb, TL_READ[10][1])
                    e_gmax.done(eng.tensor_reduce(rs[:, 0:1], gl[:, :], AX.X, ALU.max, negate=True))
                    g_j = gl[:, :].unsqueeze(1).broadcast_to([TQ, NE, NE])
                    g_e = gl[:, :].unsqueeze(2).broadcast_to([TQ, NE, NE])
                    ct(eng.tensor_tensor(cmp_b[:, :, :], g_j, g_e, ALU.is_equal))
                    ct(eng.tensor_tensor(cmp_a[:, :, :], g_j, g_e, ALU.is_gt))
                if s == SLOT[10] + 1:
                    ct.wait(tb)
                    ct(eng.tensor_tensor(cmp_b[:, :, :], cmp_b[:, :, :], earlier[:, :, :], ALU.mult))
                    ct.wait(tb)
                    ct(eng.tensor_tensor(cmp_a[:, :, :], cmp_a[:, :, :], cmp_b[:, :, :], ALU.add))
                    ct.wait(tb)
                    ct(eng.tensor_reduce(rk[:, 0, :], cmp_a[:, :, :], AX.X, ALU.add))
                    ct.wait(tb)
                    e_gexp.wait(eng, tb, 1)
                    ct(eng.scalar_tensor_tensor(rk[:, 3, :], rk[:, 0, :], TOPK - 0.5, rk[:, 1, :],
                                                ALU.is_lt, ALU.mult, accum_out=rs[:, 1:2]))
                    ct.wait(tb)
                    ct(eng.reciprocal(rs[:, 2:3], rs[:, 1:2]))
                    ct.wait(tb)
                    e_route_c.wait(eng, tb, 1, -1)
                    e_route.done(eng.tensor_scalar(rk[:, 2, :], rk[:, 3, :], rs[:, 2:3],
                                                   gt[0:TQ, 3:4], ALU.mult, ALU.mult))

            def tail(tb, s, ct):
                if s == SLOT[2]:
                    e_tl.wait(eng, tb, 3)
                    e_xb.wait(eng, tb, 1)
                    e_tl_dve.done(eng.scalar_tensor_tensor(x2[:, :], TL[0:TQ, 0:D], gt[0:TQ, 2:3],
                                                           xb1[:, :], ALU.mult, ALU.add))
                    e_tl_dve.wait(eng, tb, TL_READ[2][1])
                    stats(ct, tb, x2[:, :], lt[0], e_mv_t)
                if s == SLOT[2] + 1:
                    e_rs_t.wait(eng, tb, 2)
                    refine(ct, tb, lt[0])
                    e_n.done(norm(n2[:, :], x2[:, :], lt[0]))
                if s == SLOT[4]:
                    e_tl.wait(eng, tb, 5)
                    e_tl_act.wait(eng, tb, TL_READ[4][0])
                    eng.tensor_tensor(sm1[:, 0:1], TL[0:TQ, 256:257], bqk[0:TQ, :], ALU.add)
                    for k in range(KT):
                        last = eng.scalar_tensor_tensor(qk_lo[:, k, :], TL[:, k * TQ:(k + 1) * TQ],
                                                        kbq[:, k:k + 1], qk_hi[:, k, :].bitcast(F32),
                                                        ALU.add, ALU.subtract)
                    e_tl_dve.done(last)
                if s == SLOT[5]:
                    e_tl.wait(eng, tb, 6)
                    e_tl_dve.done(eng.tensor_reduce(sm1[:, 1:2], TL[0:TQ, 0:SK], AX.X, ALU.max))
                    e_tl_dve.wait(eng, tb, TL_READ[5][1])
                    ct(eng.tensor_tensor(sm1[:, 2:3], sm1[:, 1:2], sm1[:, 0:1], ALU.add))
                    ct.wait(tb)
                    e_bias1.done(eng.tensor_tensor(sm1[:, 3:4], sm1[:, 0:1], sm1[:, 2:3],
                                                   ALU.subtract))
                if s == SLOT[5] + 1:
                    e_tl_act.wait(eng, tb, TL_READ[5][0])
                    ct(eng.reciprocal(sm1[:, 5:6], sm1[:, 4:5]))
                    ct.wait(tb)
                    ct(eng.tensor_tensor(sm1[:, 6:7], sm1[:, 5:6], gt[0:TQ, 1:2], ALU.mult))
                if s == SLOT[7]:
                    e_tl.wait(eng, tb, 8)
                    e_tl_dve.done(eng.tensor_copy(cT[:, :, :].rearrange("p k t -> p (k t)"),
                                                  TL[:, 0:KT * TQ]))
                if s == SLOT[8]:
                    e_tl.wait(eng, tb, 9)
                    e_xb.wait(eng, tb, 2)
                    ct.wait(tb)
                    e_tl_dve.done(eng.scalar_tensor_tensor(x3[:, :], TL[0:TQ, 0:D], sm1[:, 6:7],
                                                           xb2[:, :], ALU.mult, ALU.add))
                    e_tl_dve.wait(eng, tb, TL_READ[8][1])
                    stats(ct, tb, x3[:, :], lt[0], e_mv_t)
                if s == SLOT[8] + 1:
                    e_rs_t.wait(eng, tb, 3)
                    refine(ct, tb, lt[0])
                    e_n3.done(norm(n3[:, :], x3[:, :], lt[0]))
                    e_n3.wait(eng, tb, 1)
                    stats(ct, tb, n3[:, :], lt[1], e_mv_t, squares=True)
                if s == SLOT[8] + 2:
                    e_rs_t.wait(eng, tb, 4)
                    refine(ct, tb, lt[1])
                    e_n.done(eng.tensor_scalar(tn[:, :], n3[:, :], lt[1][:, 9:10], None, ALU.mult))
                if s == SLOT[11]:
                    e_tl.wait(eng, tb, 12)
                    e_tl_dve.done(eng.tensor_copy(rT[:, :], TL[0:NE, 0:TQ]))
                if s == SLOT[12]:
                    e_tl.wait(eng, tb, 13)
                    e_xb.wait(eng, tb, 3)
                    e_tl_dve.done(eng.tensor_tensor(
                        acc[0:TQ, bass.ds(tb.index(), 1), :].rearrange("t b d -> t (b d)"),
                        TL[0:TQ, 0:D], xm[:, :], ALU.add))

            ch = Chain(eng, e_ch)
            for s in range(SLOTS):
                if s == AT_XN + 1:
                    eng.wait_ge(s_gates, 1)
                    eng.tensor_tensor(gt[:, 5:6], gt[:, 0:1], gt[:, 4:5], ALU.mult).then_inc(s_gates, 1)
                if s == AT_K[0]:
                    eng.wait_ge(s_wkv, 1)
                    eng.tensor_tensor(w_kv_part(wkv_lo, 0), w_kv_part(w_kv_in, 0),
                                      w_kv_part(wkv_hi, 0).bitcast(F32), ALU.subtract
                                      ).then_inc(s_wk_lo, 1)
                ahead(Step(None, 0, 0), s, ch)
            eng.wait_ge(s_zero, 2)
            pipeline(eng, body, B)

        @block.tensor
        def _(eng):
            def square(terms):
                for m in range(KT):
                    n = 0
                    for a, b in terms:
                        for k in range(KT):
                            n += 1
                            last = eng.matmul(TL[:, m * D:(m + 1) * D],
                                              stage[:, a + k, m * 128:(m + 1) * 128], stage[:, b + k, :],
                                              start=(n == 1), stop=(n == KT * len(terms)))
                return last

            def setup(n):
                if n == 0:
                    eng.wait_ge(ld_stage, 16 * N_STAGE)
                else:
                    eng.wait_ge(s_su, n)
                if n in (0, 1):
                    src = (ST_WK, ST_A)[n]
                    for e in range(KT):
                        for d in range(KT):
                            last = eng.transpose(TL[:, e * D + d * 128:e * D + (d + 1) * 128],
                                                 stage[:, src + d, e * 128:(e + 1) * 128], ident[:, :])
                if n == 2:
                    last = square([(ST_A, ST_WK)])
                if n == 3:
                    def column(at, lhs, vector, m_size=128):
                        for k in range(KT):
                            eng.matmul(TL[0:m_size, at:at + 1], lhs(k), cols[:, vector, k:k + 1],
                                       start=(k == 0), stop=(k == KT - 1))

                    for m in range(KT):
                        piece = slice(m * 128, (m + 1) * 128)
                        column(m, lambda k: stage[:, ST_A + k, piece], BK)
                        column(KT + m, lambda k: stage[:, ST_WK + k, piece], BQ)
                    column(2 * KT, lambda k: nT[:, k, :], BK, TQ)
                    for m in range(HT):
                        eng.transpose(TL[:, AT_B1 + m * NE:AT_B1 + (m + 1) * NE],
                                      b1_in[m].rearrange("e (i two) -> e two i", two=2)[:, 0, :],
                                      ident[0:NE, 0:NE])
                    for k in range(KT):
                        last = eng.transpose(TL[:, AT_GW + k * NE:AT_GW + (k + 1) * NE],
                                             gw_in[:, k * 128:(k + 1) * 128], ident[0:NE, 0:NE])
                if n == 4:
                    last = square([(ST_RE, ST_COS), (ST_IM, ST_SIN)])
                if n == 5:
                    last = square([(ST_IM, ST_COS), (ST_RE, ST_NSIN)])
                if n == 6:
                    last = square([(ST_A, ST_COS), (ST_B, ST_NSIN)])
                last.then_inc(s_su_pe, 1)

            def split_product(out_, lhs, rhs):
                n = 0
                for i, j in PASSES:
                    for k in range(KT):
                        n += 1
                        last = eng.matmul(out_, lhs(i, k), rhs(j, k), start=(n == 1),
                                          stop=(n == KT * len(PASSES)))
                return last

            def key(step, p):
                n = USE_K[p]
                wait_kv_free(eng, step, n)
                e_kv_pe.done(split_product(
                    KV[n % 2][:, 0:SKE], lambda i, k: wkv[i][:, k, p * 128:(p + 1) * 128],
                    lambda j, k: ctxT[j][:, step.par, k, :]))

            def tail(tb, n):
                if n == 0:
                    e_oT.wait(eng, tb, NP)
                    e_tl_dve.wait(eng, tb, TL_READ[12][1], -1)
                else:
                    a, d = TL_READ[n - 1]
                    if n == 1 or TL_READ[n - 2][0] != a:
                        if a:
                            e_tl_act.wait(eng, tb, a)
                    if n == 1 or TL_READ[n - 2][1] != d:
                        e_tl_dve.wait(eng, tb, d)
                if n == 0:
                    for p in range(NP):
                        last = eng.matmul(TL[0:TQ, 0:D], oT[:, p, :], wo[:, p, :], start=(p == 0),
                                          stop=(p == NP - 1))
                if n in (1, 3, 9):
                    e_n.wait(eng, tb, {1: 1, 3: 2, 9: 3}[n])
                    src = {1: n1, 3: n2, 9: tn}[n]
                    for k in range(KT):
                        last = eng.transpose(TL[:, k * TQ:(k + 1) * TQ],
                                             src[:, k * 128:(k + 1) * 128], ident[0:TQ, 0:TQ])
                if n == 2:
                    for k in range(KT):
                        last = eng.matmul(TL[0:TQ, 0:D], nT[:, k, :], fmix[:, k, :], start=(k == 0),
                                          stop=(k == KT - 1))
                if n == 4:
                    for k in range(KT):
                        eng.matmul(TL[0:TQ, 256:257], nT[:, k, :], qbk[:, k:k + 1], start=(k == 0),
                                   stop=(k == KT - 1))
                    for m in range(KT):
                        for k in range(KT):
                            last = eng.matmul(TL[:, m * TQ:(m + 1) * TQ],
                                              wqk[:, k, m * 128:(m + 1) * 128], nT[:, k, :],
                                              start=(k == 0), stop=(k == KT - 1))
                if n == 5:
                    last = split_product(TL[0:TQ, 0:SKE], lambda i, k: qk[i][:, k, :],
                                         lambda j, k: ctxT[j][:, tb.par, k, :])
                if n == 6:
                    for k in range(NKEY):
                        last = eng.transpose(TL[0:KEYT, k * TQ:(k + 1) * TQ],
                                             prob1[:, k * KEYT:(k + 1) * KEYT], ident[0:TQ, 0:TQ])
                if n == 7:
                    for m in range(KT):
                        for k in range(NKEY):
                            last = eng.matmul(TL[:, m * TQ:(m + 1) * TQ],
                                              ctx_in[0:KEYT, tb.par, k, m * 128:(m + 1) * 128],
                                              prob1T[:, k, :], start=(k == 0), stop=(k == NKEY - 1))
                if n == 8:
                    for k in range(KT):
                        last = eng.matmul(TL[0:TQ, 0:D], cT[:, k, :], wv1[:, k, :], start=(k == 0),
                                          stop=(k == KT - 1))
                if n == 10:
                    for k in range(KT):
                        last = eng.matmul(TL[0:TQ, 0:NE], tf[:, k, :], gwT[:, k, :], start=(k == 0),
                                          stop=(k == KT - 1))
                if n == 11:
                    e_route.wait(eng, tb, 1)
                    last = eng.transpose(TL[0:NE, 0:TQ], rk[:, 2, :], ident[0:TQ, 0:TQ])
                if n == 12:
                    last = eng.matmul(TL[0:TQ, 0:D], rT[:, :], b2[:, :], start=True, stop=True)
                e_tl.done(last)

            def ahead(nx, s):
                if s in AT_CTX:
                    k = AT_CTX.index(s)
                    if k == 0:
                        e_ctx.wait(eng, nx, 1)
                    wait_kv_free(eng, nx, USE_C + k)
                    for j in range(NKEY):
                        last = eng.transpose(KV[(USE_C + k) % 2][:, j * KEYT:(j + 1) * KEYT],
                                             ctx_in[0:KEYT, nx.par, j, k * 128:(k + 1) * 128],
                                             ident[0:KEYT, 0:KEYT])
                    e_kv_pe.done(last)
                if s == AT_X:
                    e_xn.wait(eng, nx, 1)
                    for k in range(KT):
                        wait_kv_free(eng, nx, USE_X + k)
                        e_kv_pe.done(eng.transpose(KV[(USE_X + k) % 2][:, 0:TQ], xn[:, k * 128:(k + 1) * 128],
                                                   ident[0:TQ, 0:TQ]))
                if s in AT_K:
                    if s == AT_K[0]:
                        e_kv_dve.wait(eng, nx, sum(DVE_READS[:USE_C + KT]))
                    key(nx, AT_K.index(s))
                if s in AT_Q:
                    n = AT_Q.index(s)
                    if n == 0:
                        e_kv_act.wait(eng, nx, sum(ACT_READS[:USE_X + KT]))
                    wait_kv_free(eng, nx, USE_Q[n])
                    for a in range(NP // 2):
                        p = n * NP // 2 + a
                        for k in range(KT):
                            last = eng.matmul(KV[USE_Q[n] % 2][:, a * TQ:(a + 1) * TQ],
                                              wq[:, k, p * 128:(p + 1) * 128], xnT[:, k, :],
                                              start=(k == 0), stop=(k == KT - 1))
                    e_kv_pe.done(last)

            def body(st):
                tb = st.before()
                for n in range(2 * NKEY):
                    j, half = n // 2, n % 2
                    if n == 2 and st.tail:
                        tail(tb, 0)
                    if not st.heads:
                        continue
                    wait_kv_free(eng, st, USE_V + n)
                    e_kv_pe.done(split_product(
                        KV[(USE_V + n) % 2][0:KEYT, :],
                        lambda i, k: ctxT[i][:, st.par, k, j * KEYT:(j + 1) * KEYT],
                        lambda jj, k: wkv[jj][:, k, INNER + half * 512:INNER + (half + 1) * 512]))
                if st.tail:
                    tail(tb, 1)
                for s in range(SLOTS):
                    if st.heads and s < NH:
                        p, half = s // 2, s % 2
                        if half == 0:
                            n = max(USE_Q[1], USE_K[p])
                            e_kv_dve.wait(eng, st, sum(DVE_READS[:n + 1]))
                        e_exp.wait(eng, st, *((s - 1, 0) if s >= 2 else (NH + s - 1, -1)))
                        for n, (i, j) in enumerate(PASSES):
                            last = eng.matmul(S[s % 2][0:TQ, 0:SKE], qq[i][:, p, half, :], kk[j][:, p, :],
                                              start=(n == 0), stop=(n == len(PASSES) - 1))
                        e_s.done(last)
                    if st.heads and LAG_T <= s < NH + LAG_T:
                        h = s - LAG_T
                        e_prob.wait(eng, st, h + 1)
                        e_pt.wait(eng, st, *((h - 1, 0) if h >= 2 else (NH + h - 1, -1)))
                        for k in range(NKEY):
                            last = eng.transpose(PT[h % 2][0:KEYT, k * TQ:(k + 1) * TQ],
                                                 prob[0:TQ, h % 2, k * KEYT:(k + 1) * KEYT],
                                                 ident[0:TQ, 0:TQ])
                        e_pt_pe.done(last)
                    if st.heads and LAG_O <= s < NH + LAG_O:
                        h = s - LAG_O
                        p, half = h // 2, h % 2
                        e_pt.wait(eng, st, h + 1)
                        if half == 0:
                            e_oT.wait(eng, st, p)
                        for k in range(NKEY):
                            last = eng.matmul(
                                OT[64 * half:64 * half + 64, 0:TQ],
                                v[0:KEYT, k, h * DH:(h + 1) * DH], probT[:, h % 2, k, :],
                                start=(k == 0), stop=(k == NKEY - 1))
                        e_o.done(last)
                    if st.heads and s in OWN_K:
                        key(st, 2 + OWN_K.index(s))
                    if st.load:
                        ahead(st.after(), s)
                    if st.tail and s in STAGE:
                        tail(tb, STAGE[s])
                    if not st.tail and s in SETUP:
                        setup(SETUP.index(s))
                if not st.tail:
                    eng.wait_ge(s_su, len(SETUP))
                    eng.wait_ge(ld_w, 16 * N_W)

            eng.wait_ge(s_ident, 2)
            for s in range(SLOTS):
                if s == AT_Q[0]:
                    eng.wait_ge(ld_wq, 16)
                if s == AT_K[0]:
                    eng.wait_ge(s_wk_lo, 1)
                    eng.wait_ge(s_zero, 2)
                ahead(Step(None, 0, 0), s)
            eng.wait_ge(s_wv_lo, 1)
            eng.wait_ge(s_zero_q, 1)
            eng.wait_ge(s_rows, 1)
            pipeline(eng, body, B)


def phase2(nc, sb, event, sem, psum, ident, acc, tT_hi, tT_lo, route, b1T, w1_in, w2_in, f_w,
           load_expert, out):
    scope = ExitStack()
    with scope:
        def t(name, shape, dt=F32):
            return sb(name, shape, dt, scope)

        w1_hi = t("w1_hi", [128, 2, KT, HID], F32R)
        w1_lo = t("w1_lo", [128, 2, KT, HID], F32R)
        w2_hi = t("w2_hi", [128, 2, HT, D], F32R)
        w2_lo = t("w2_lo", [128, 2, HT, D], F32R)
        b1c = t("b1c", [128, 2, HT])
        rc = t("rc", [TQ, 2, B])
        u = t("u", [128, 2, HT, CT])
        sg = t("sg", [128, 2, HT, CT])
        s_f = t("s_f", [128, 2, HT, CT])
        s_hi = t("s_hi", [128, NC, HT, CT], F32R)
        s_lo = t("s_lo", [128, NC, HT, CT], F32R)
        w1, w2, tt, ss = (w1_hi, w1_lo), (w2_hi, w2_lo), (tT_hi, tT_lo), (s_hi, s_lo)
        H = [[psum[0], psum[1]], [psum[2], psum[3]]]
        Y = [psum[4], psum[5]]
        WB = [psum[6], psum[7]]
        PASSES = ((0, 0), (0, 1), (1, 0))

        NCH = NC * HT
        LAG = 2
        f_wt = event("f_wt", 2)
        f_whi = event("f_whi", 2)
        f_wlo = event("f_wlo", 2)
        f_col = event("f_col", 1)
        f_h = event("f_h", NCH)
        f_u = event("f_u", NCH)
        f_sg = event("f_sg", NCH)
        f_s = event("f_s", NCH)
        f_shi = event("f_shi", NCH)
        f_slo = event("f_slo", NCH)
        f_y = event("f_y", B)
        f_acc = event("f_acc", B)
        f_out = sem("f_out")

        block = scope.enter_context(nc.Block())

        @block.sync
        def _(eng):
            for c in range(NC):
                eng.wait_ge(f_acc.handle, B * (NE - 1) + CB * (c + 1))
                eng.dma_start(out[c * CB:(c + 1) * CB, :, :].rearrange("b t d -> t b d"),
                              acc[0:TQ, c * CB:(c + 1) * CB, :]).then_inc(f_out, 16)
            eng.wait_ge(f_out, 16 * NC)

        @block.gpsimd
        def _(eng):
            def columns(st):
                f_acc.wait(eng, st, B, -2)
                b1_e = b1T[:, bass.ds(st.index(), 1), :].rearrange("p e m -> p (e m)")
                rc_e = route[:, bass.ds(st.index(), 1), :].rearrange("t e b -> t (e b)")
                eng.tensor_copy(b1c[:, st.par, :], b1_e)
                f_col.done(eng.tensor_copy(rc[:, st.par, :], rc_e))

            columns(Step(None, 0, 0))

            def body(st):
                for c in range(NC):
                    if st.heads:
                        for m in range(HT):
                            n = c * HT + m
                            f_shi.wait(eng, st, n + 1)
                            f_y.wait(eng, st, CB * (c + 1), -1)
                            f_slo.done(eng.tensor_tensor(s_lo[:, c, m, :], s_f[:, c % 2, m, :],
                                                         s_hi[:, c, m, :].bitcast(F32),
                                                         ALU.subtract))
                    if c == LAG and st.load:
                        columns(st.after())

            pipeline(eng, body, NE)

        @block.scalar
        def _(eng):
            def high(st):
                for n, w in enumerate((w1_hi, w2_hi)):
                    f_wt.wait(eng, st, n + 1)
                    f_whi.done(eng.activation(w[:, st.par, :, :].rearrange("p k n -> p (k n)"),
                                              WB[n][:, :], ACT.Copy))

            high(Step(None, 0, 0))

            def body(st):
                if st.load:
                    f_wt.wait(eng, st, 2)
                    load_expert(eng, st.after().index())
                for c in range(NC):
                    if not st.heads:
                        continue
                    for m in range(HT):
                        n = c * HT + m
                        f_u.wait(eng, st, n + 1)
                        f_sg.done(eng.activation(sg[:, c % 2, m, :], u[:, c % 2, m, :], ACT.Sigmoid,
                                                 scale=ALPHA))
                    for m in range(HT):
                        n = c * HT + m
                        f_s.wait(eng, st, n + 1)
                        f_y.wait(eng, st, CB * (c + 1), -1)
                        f_shi.done(eng.activation(s_hi[:, c, m, :], s_f[:, c % 2, m, :], ACT.Copy))
                    if c == 2 and st.load:
                        high(st.after())

            pipeline(eng, body, NE)

        @block.vector
        def _(eng):
            def low(st):
                for n, (w, hi) in enumerate(((w1_lo, w1_hi), (w2_lo, w2_hi))):
                    f_whi.wait(eng, st, n + 1)
                    f_wlo.done(eng.tensor_tensor(
                        w[:, st.par, :, :].rearrange("p k n -> p (k n)"), WB[n][:, :],
                        hi[:, st.par, :, :].bitcast(F32).rearrange("p k n -> p (k n)"), ALU.subtract))

            low(Step(None, 0, 0))

            def body(st):
                for c in range(NC):
                    if st.heads:
                        for m in range(HT):
                            n = c * HT + m
                            if n == 0:
                                f_col.wait(eng, st, 1)
                            f_h.wait(eng, st, n + 1)
                            f_sg.wait(eng, st, n + 1 - 2 * HT)
                            f_u.done(eng.tensor_scalar(u[:, c % 2, m, :], H[c % 2][m][:, 0:CT],
                                                       b1c[:, st.par, m:m + 1], LIMIT, ALU.add,
                                                       ALU.min))
                        for m in range(HT):
                            n = c * HT + m
                            f_sg.wait(eng, st, n + 1)
                            f_slo.wait(eng, st, n + 1 - 2 * HT)
                            f_s.done(eng.scalar_tensor_tensor(s_f[:, c % 2, m, :], u[:, c % 2, m, :],
                                                              LIMIT + 1.0, sg[:, c % 2, m, :],
                                                              ALU.mult, ALU.mult))
                    if c == 2 and st.load:
                        low(st.after())
                    add(st, c)

            def add(st, c):
                if c < LAG:
                    if not st.tail:
                        return
                    own, cc = st.before(), c + NC - LAG
                else:
                    if not st.heads:
                        return
                    own, cc = st, c - LAG
                for b in range(CB):
                    batch = cc * CB + b
                    if b % 2 == 0:
                        f_y.wait(eng, own, batch + 2)
                    f_acc.wait(eng, own, batch + 1 - CB)
                    f_acc.done(eng.scalar_tensor_tensor(
                        acc[0:TQ, batch, :], Y[b // 2][0:TQ, (b % 2) * D:(b % 2 + 1) * D],
                        rc[:, own.par, batch:batch + 1], acc[0:TQ, batch, :], ALU.mult, ALU.add))

            pipeline(eng, body, NE)

        @block.tensor
        def _(eng):
            def weights(st):
                f_w.wait(eng, st, 1)
                f_wlo.wait(eng, st, 2, -1)
                for k in range(KT):
                    for m in range(HT):
                        last = eng.transpose(WB[0][:, k * HID + m * 128:k * HID + (m + 1) * 128],
                                             w1_in[:, m, k * 128:(k + 1) * 128], ident[:, :])
                f_wt.done(last)
                for m in range(HT):
                    for k in range(KT):
                        last = eng.transpose(WB[1][:, m * D + k * 128:m * D + (k + 1) * 128],
                                             w2_in[:, k, m * 128:(m + 1) * 128], ident[:, :])
                f_wt.done(last)

            weights(Step(None, 0, 0))

            def output(st, c):
                if c < LAG:
                    if not st.tail:
                        return
                    own, cc = st.before(), c + NC - LAG
                else:
                    if not st.heads:
                        return
                    own, cc = st, c - LAG
                f_slo.wait(eng, own, (cc + 1) * HT)
                for b in range(CB):
                    batch = cc * CB + b
                    if b % 2 == 0:
                        f_acc.wait(eng, own, batch - 2)
                    n = 0
                    for i, j in PASSES:
                        for m in range(HT):
                            n += 1
                            last = eng.matmul(Y[b // 2][0:TQ, (b % 2) * D:(b % 2 + 1) * D],
                                              ss[i][:, cc, m, b * TQ:(b + 1) * TQ],
                                              w2[j][:, own.par, m, :], start=(n == 1),
                                              stop=(n == HT * len(PASSES)))
                    f_y.done(last)

            def body(st):
                for c in range(NC):
                    if st.heads:
                        for m in range(HT):
                            if c == 0 and m == 0:
                                f_wlo.wait(eng, st, 2)
                            f_u.wait(eng, st, c * HT + m + 1 - 2 * HT)
                            n = 0
                            for i, j in PASSES:
                                for k in range(KT):
                                    n += 1
                                    last = eng.matmul(H[c % 2][m][:, 0:CT],
                                                      w1[i][:, st.par, k, m * 128:(m + 1) * 128],
                                                      tt[j][:, k, c * CT:(c + 1) * CT],
                                                      start=(n == 1), stop=(n == KT * len(PASSES)))
                            f_h.done(last)
                    output(st, c)
                    if c == 1 and st.load:
                        weights(st.after())

            pipeline(eng, body, NE)


_INS = ["x", "ctx_1024", "g_xattn", "g_ffn", "L0_xattn_ln_gamma", "L0_xattn_ln_beta", "L0_xattn_w_q",
        "L0_xattn_w_kv", "L0_xattn_w_out", "L0_xattn_b_out", "L0_xattn_gate", "L0_ffn_w_freq_real",
        "L0_ffn_w_freq_imag", "L0_ffn_bias", "L1_xattn_Wq", "L1_xattn_bq", "L1_xattn_Wk",
        "L1_xattn_bk", "L1_xattn_Wv", "L1_xattn_bv", "L1_ffn_scale", "L1_ffn_gate_w",
        "L1_ffn_gate_b", "L1_ffn_mlp1_w", "L1_ffn_mlp1_b", "L1_ffn_mlp2_w", "L1_ffn_mlp2_b"]


def kernel(**inputs):
    import concourse.bacc as bacc
    from concourse.bass_utils import run_bass_kernel_spmd

    nc = bacc.Bacc("TRN2", target_bir_lowering=False, num_devices=1)
    arrays, args = {}, []

    def give(name, a):
        a = np.ascontiguousarray(a)
        arrays[name] = a
        args.append(nc.dram_tensor(name, a.shape, mybir.dt.from_np(a.dtype), kind="ExternalInput").ap())

    for name in _INS:
        give(f"in_{name}", inputs[name])
    jk = (np.arange(D)[:, None] * np.arange(D)[None, :]) % D
    angle = 2.0 * np.pi * jk / D
    give("dft", np.stack([np.cos(angle), np.sin(angle), -np.sin(angle)]).astype(np.float32))
    out = nc.dram_tensor("out_0", (B, TQ, D), F32, kind="ExternalOutput").ap()
    build(nc, *args, out)
    r = run_bass_kernel_spmd(nc, [arrays], core_ids=[0])
    return r.results[0]["out_0"]
```
